# Optimizing a Trainium2 kernel written in Bass

```python
import numpy as np
import jax
import jax.numpy as jnp

def _softmax(x, axis=-1):
    return jax.nn.softmax(x, axis=axis)

def _gelu(x):
    return jax.nn.gelu(x, approximate=True)

def _silu(x):
    return jax.nn.silu(x)

def _sigmoid(x):
    return jax.nn.sigmoid(x)

def _layernorm(x, axis=-1, eps=1e-05):
    m = jnp.mean(x, axis=axis, keepdims=True)
    v = jnp.var(x, axis=axis, keepdims=True)
    return (x - m) / jnp.sqrt(v + eps)

def _scatter_add(tgt, idx, src, axis=0):
    return tgt.at[idx].add(src)

def _segment_sum(src, seg, n):
    return jax.ops.segment_sum(src, seg, n)
kernel_name = 'mk_gps_d1_gnn_r8_0c1124'

def setup_inputs(seed: int=0):
    np.random.seed(seed)
    _w = jnp.asarray

    def _rec_inputs():
        import jax
        import jax.numpy as jnp
        _gk = jax.random.key(seed)
        x = -6.415e-05 + 1 * jax.random.normal(jax.random.fold_in(_gk, 1), (2500, 512), jnp.float32)
        src = jax.random.randint(jax.random.fold_in(_gk, 2), (80000,), 0, 2500, jnp.int32)
        dst = jnp.minimum((2500 * jax.random.uniform(jax.random.fold_in(_gk, 3), (80000,)) ** 2.0).astype(jnp.int32), 19999)
        _o = jnp.argsort(dst, stable=True)
        src = src[_o]
        dst = dst[_o]
        return (x, src, dst)
    x, src, dst = _rec_inputs()

    def _L0_gnn_setup():
        import jax, jax.numpy as jnp
        import numpy as np
        N = 2500
        E = 40000
        F_IN = 512
        HEADS = 8
        D = 64
        ALPHA = 0.2
        EPS = 1e-16

        def _gat_forward(x, edge_index, W_e, W_r, a):
            src = edge_index[0]
            dst = edge_index[1]
            h_e = jnp.einsum('nf,hfd->hnd', x, W_e)
            h_r = jnp.einsum('nf,hfd->hnd', x, W_r)
            a_src, a_dst, a_dif, a_abs, a_prd = jnp.split(a, 5, axis=1)
            s_src = jnp.einsum('hnd,hd->hn', h_e, a_src)[:, src]
            s_dst = jnp.einsum('hnd,hd->hn', h_e, a_dst)[:, dst]
            hr_src = h_r[:, src]
            hr_dst = h_r[:, dst]
            diff = hr_dst - hr_src
            score = s_src + s_dst + jnp.einsum('hed,hd->he', diff, a_dif) + jnp.einsum('hed,hd->he', jnp.abs(diff), a_abs) + jnp.einsum('hed,hd->he', hr_src * hr_dst, a_prd)
            alpha = jax.nn.leaky_relu(score, negative_slope=ALPHA)
            alpha_t = alpha.T
            m = jax.ops.segment_max(alpha_t, src, num_segments=N)
            ex = jnp.exp(alpha_t - m[src])
            denom = jax.ops.segment_sum(ex, src, num_segments=N)[src]
            att = ex / (denom + EPS)
            msg = att[:, :, None] * jnp.transpose(h_e[:, dst], (1, 0, 2))
            out = jax.ops.segment_sum(msg, src, num_segments=N)
            return out.reshape(N, HEADS * D)
        key = jax.random.key(seed)
        k1, k2, k3, k4, k5 = jax.random.split(key, 5)
        x = jax.random.normal(k1, (N, F_IN), dtype=jnp.float32)
        edge_index = jax.random.randint(k2, (2, E), 0, N, dtype=jnp.int64)
        s_w = np.sqrt(2.0 / (F_IN + D))
        W_e = jax.random.normal(k3, (HEADS, F_IN, D), dtype=jnp.float32) * s_w
        W_r = jax.random.normal(k4, (HEADS, F_IN, D), dtype=jnp.float32) * s_w
        s_a = np.sqrt(2.0 / (1 + 5 * D))
        a = jax.random.normal(k5, (HEADS, 5 * D), dtype=jnp.float32) * s_a
        return {'x': x, 'edge_index': edge_index, 'W_e': W_e, 'W_r': W_r, 'a': a}
    _L0_gnn_all = _L0_gnn_setup()
    _L0_gnn_in = {k: v for k, v in _L0_gnn_all.items() if k in ('W_e', 'W_r', 'a')}
    del _L0_gnn_all

    def _L0_mix_setup():
        import jax, jax.numpy as jnp
        import numpy as np
        DIM = 512
        HEADS = 8
        DIM_HEAD = 64
        SLICE = 32
        INNER = HEADS * DIM_HEAD
        key = jax.random.key(seed)
        ks = jax.random.split(key, 8)
        B, N = (8, 1024)
        s = 0.02
        return {'x': jax.random.normal(ks[0], (B, N, DIM), dtype=jnp.float32), 'W_in': jax.random.normal(ks[1], (DIM, INNER), dtype=jnp.float32) * s, 'b_in': jnp.zeros((INNER,), dtype=jnp.float32), 'Wq': jax.random.normal(ks[2], (DIM_HEAD, SLICE), dtype=jnp.float32) * s, 'Wk': jax.random.normal(ks[3], (DIM_HEAD, SLICE), dtype=jnp.float32) * s, 'Wv': jax.random.normal(ks[4], (DIM_HEAD, DIM_HEAD), dtype=jnp.float32) * s, 'W_out': jax.random.normal(ks[5], (INNER, DIM), dtype=jnp.float32) * s, 'b_out': jnp.zeros((DIM,), dtype=jnp.float32)}
    _L0_mix_all = _L0_mix_setup()
    _L0_mix_in = {k: v for k, v in _L0_mix_all.items() if k in ('W_in', 'b_in', 'Wq', 'Wk', 'Wv', 'W_out', 'b_out')}
    del _L0_mix_all

    def _L0_ffn_setup():
        import jax, jax.numpy as jnp
        import numpy as np
        E = 8
        K = 1
        D = 512
        I = 256
        B, T = (2, 256)
        key = jax.random.key(seed)
        ks = jax.random.split(key, 7)
        s = 0.02
        x = jax.random.normal(ks[0], (B, T, D), jnp.float32)
        gate_w = jax.random.normal(ks[1], (E, D), jnp.float32) * s
        w1 = jax.random.normal(ks[2], (E, I, D), jnp.float32) * s
        w2 = jax.random.normal(ks[3], (E, D, I), jnp.float32) * s
        w3 = jax.random.normal(ks[4], (E, I, D), jnp.float32) * s
        sw1 = jax.random.normal(ks[5], (I, D), jnp.float32) * s
        sw2 = jax.random.normal(ks[6], (D, I), jnp.float32) * s
        return {'x': x, 'gate_w': gate_w, 'w1': w1, 'w2': w2, 'w3': w3, 'sw1': sw1, 'sw2': sw2}
    _L0_ffn_all = _L0_ffn_setup()
    _L0_ffn_in = {k: v for k, v in _L0_ffn_all.items() if k in ('gate_w', 'w1', 'w2', 'w3', 'sw1', 'sw2')}
    del _L0_ffn_all
    return {'x': x, 'src': src, 'dst': dst, 'L0_gnn_W_e': _L0_gnn_in['W_e'], 'L0_gnn_W_r': _L0_gnn_in['W_r'], 'L0_gnn_a': _L0_gnn_in['a'], 'L0_mix_W_in': _L0_mix_in['W_in'], 'L0_mix_b_in': _L0_mix_in['b_in'], 'L0_mix_Wq': _L0_mix_in['Wq'], 'L0_mix_Wk': _L0_mix_in['Wk'], 'L0_mix_Wv': _L0_mix_in['Wv'], 'L0_mix_W_out': _L0_mix_in['W_out'], 'L0_mix_b_out': _L0_mix_in['b_out'], 'L0_ffn_gate_w': _L0_ffn_in['gate_w'], 'L0_ffn_w1': _L0_ffn_in['w1'], 'L0_ffn_w2': _L0_ffn_in['w2'], 'L0_ffn_w3': _L0_ffn_in['w3'], 'L0_ffn_sw1': _L0_ffn_in['sw1'], 'L0_ffn_sw2': _L0_ffn_in['sw2']}

def reference(x, src, dst, L0_gnn_W_e, L0_gnn_W_r, L0_gnn_a, L0_mix_W_in, L0_mix_b_in, L0_mix_Wq, L0_mix_Wk, L0_mix_Wv, L0_mix_W_out, L0_mix_b_out, L0_ffn_gate_w, L0_ffn_w1, L0_ffn_w2, L0_ffn_w3, L0_ffn_sw1, L0_ffn_sw2):
    import jax
    import jax.numpy as jnp

    def _L0_gnn_ref(x, edge_index, W_e, W_r, a):
        import jax, jax.numpy as jnp
        import numpy as np
        N = 2500
        E = 40000
        F_IN = 512
        HEADS = 8
        D = 64
        ALPHA = 0.2
        EPS = 1e-16

        def _gat_forward(x, edge_index, W_e, W_r, a):
            src = edge_index[0]
            dst = edge_index[1]
            h_e = jnp.einsum('nf,hfd->hnd', x, W_e)
            h_r = jnp.einsum('nf,hfd->hnd', x, W_r)
            a_src, a_dst, a_dif, a_abs, a_prd = jnp.split(a, 5, axis=1)
            s_src = jnp.einsum('hnd,hd->hn', h_e, a_src)[:, src]
            s_dst = jnp.einsum('hnd,hd->hn', h_e, a_dst)[:, dst]
            hr_src = h_r[:, src]
            hr_dst = h_r[:, dst]
            diff = hr_dst - hr_src
            score = s_src + s_dst + jnp.einsum('hed,hd->he', diff, a_dif) + jnp.einsum('hed,hd->he', jnp.abs(diff), a_abs) + jnp.einsum('hed,hd->he', hr_src * hr_dst, a_prd)
            alpha = jax.nn.leaky_relu(score, negative_slope=ALPHA)
            alpha_t = alpha.T
            m = jax.ops.segment_max(alpha_t, src, num_segments=N)
            ex = jnp.exp(alpha_t - m[src])
            denom = jax.ops.segment_sum(ex, src, num_segments=N)[src]
            att = ex / (denom + EPS)
            msg = att[:, :, None] * jnp.transpose(h_e[:, dst], (1, 0, 2))
            out = jax.ops.segment_sum(msg, src, num_segments=N)
            return out.reshape(N, HEADS * D)
        return _gat_forward(x, edge_index, W_e, W_r, a)

    def _L0_mix_ref(x, W_in, b_in, Wq, Wk, Wv, W_out, b_out):
        import jax, jax.numpy as jnp
        import numpy as np
        DIM = 512
        HEADS = 8
        DIM_HEAD = 64
        SLICE = 32
        INNER = HEADS * DIM_HEAD
        B, N, C = x.shape
        x_mid = (x @ W_in + b_in).reshape(B, N, HEADS, DIM_HEAD).transpose(0, 2, 1, 3)
        q = x_mid @ Wq
        k = x_mid @ Wk
        v = x_mid @ Wv
        q = jax.nn.softmax(q, axis=-1)
        k = jax.nn.softmax(k, axis=-2)
        kv = jnp.einsum('bhns,bhnc->bhsc', k, v)
        qkv = jnp.einsum('bhns,bhsc->bhnc', q, kv)
        qkv = qkv.transpose(0, 2, 1, 3).reshape(B, N, INNER)
        return qkv @ W_out + b_out

    def _L0_ffn_ref(x, gate_w, w1, w2, w3, sw1, sw2):
        import jax, jax.numpy as jnp
        import numpy as np
        E = 8
        K = 1
        D = 512
        I = 256
        B, T = (2, 256)
        xf = x.reshape(-1, D)
        logits = xf @ gate_w.T
        wts, idx = jax.lax.top_k(logits, K)
        wts = jax.nn.softmax(wts, axis=-1)
        comb = jnp.einsum('nke,nk->ne', jax.nn.one_hot(idx, E, dtype=xf.dtype), wts)
        h = jax.nn.silu(jnp.einsum('nd,eid->nei', xf, w1)) * jnp.einsum('nd,eid->nei', xf, w3)
        y = jnp.einsum('nei,edi->nd', h * comb[:, :, None], w2)
        y = y + jax.nn.gelu(xf @ sw1.T, approximate=False) @ sw2.T
        return y.reshape(x.shape)
    edge_index = jnp.stack([src, dst])
    xn = _layernorm(x, axis=-1)
    x = x + _L0_gnn_ref(xn, edge_index, L0_gnn_W_e, L0_gnn_W_r, L0_gnn_a) + _L0_mix_ref(xn[None], L0_mix_W_in, L0_mix_b_in, L0_mix_Wq, L0_mix_Wk, L0_mix_Wv, L0_mix_W_out, L0_mix_b_out)[0]
    x = x + _L0_ffn_ref(_layernorm(x, axis=-1)[None], L0_ffn_gate_w, L0_ffn_w1, L0_ffn_w2, L0_ffn_w3, L0_ffn_sw1, L0_ffn_sw2)[0]
    return x

_drawn_inputs = setup_inputs


def setup_inputs(seed=0):
    import zlib

    import numpy as np

    out = dict(_drawn_inputs(seed))
    spreads = {'L0_mix_b_in': (0.0, 0.8), 'L0_mix_b_out': (0.0, 0.688)}
    factors = {'L0_mix_W_in': 8.0,
     'L0_mix_Wq': 8.0,
     'L0_mix_Wk': 8.0,
     'L0_mix_Wv': 7.548,
     'L0_mix_W_out': 8.0,
     'L0_ffn_gate_w': 8.0,
     'L0_ffn_w1': 8.0,
     'L0_ffn_w2': 8.0,
     'L0_ffn_w3': 8.0,
     'L0_ffn_sw1': 4.723,
     'L0_ffn_sw2': 3.683}
    for name, (base, spread) in spreads.items():
        noise = np.random.default_rng([zlib.crc32(name.encode()), seed]).standard_normal(out[name].shape)
        drawn = base * np.exp(spread * noise) if base else spread * noise
        out[name] = jnp.asarray(drawn.astype(out[name].dtype))
    for name, factor in factors.items():
        out[name] = (out[name] * factor).astype(out[name].dtype)
    return out
```

```python
import concourse.bass as bass
from concourse import mybir
from contextlib import ExitStack

F32 = mybir.dt.float32
BF16 = mybir.dt.bfloat16
I32 = mybir.dt.int32
ALU = mybir.AluOpType
ACT = mybir.ActivationFunctionType
AX = mybir.AxisListType
DS = bass.ds

N, E, F, HEADS, D = 2500, 80000, 512, 8, 64
SLICE, EXPERTS, INNER = 32, 8, 256
P = 128
L = 125
NB = N // L
KF = F // P
ET = E // L
CH = 4
GROUP = 2
GE = GROUP * P
CHUNKS = P // HEADS
MAX_GROUPS = (E + NB * (GE - 1)) // GE
PIECE_GROUPS = -(-MAX_GROUPS // CHUNKS)
GROUPS = PIECE_GROUPS * CHUNKS
ST = GROUPS * GROUP
EP = ST * P
PIECE = EP // CHUNKS
PT = PIECE // P
REC_COLS = -(-(EP + 2) // P)
REC_ROWS = REC_COLS * P
KEY = 4096
PAD_RECORD = (KEY - 1) * KEY
ROUND = 12582912.0
TOKEN_TILES = (N + EXPERTS * (P - 1)) // P
TOK_ROWS = TOKEN_TILES * P
EW = F + HEADS
MIDDLE = float(EP // 2 // 256 * 256)
RECS = 4
BIG = 1e38


def linker(eng, sem, base=0):
    count = [0]

    def link(ins):
        count[0] += 1
        ins.then_inc(sem, 1)
        eng.wait_ge(sem, base + count[0])
    link.count = count
    return link


def make_constants(nc, sb):
    c = {
        "row": sb("iota_row", [P, P], F32), "col": sb("iota_col", [P, 1], F32),
        "rowb": sb("iota_row_bf", [P, P], BF16),
        "ident": sb("ident", [P, P], F32), "identb": sb("ident_bf", [P, P], BF16),
        "tri": sb("tri", [P, P], F32), "ones": sb("ones", [P, P], F32),
        "eps": sb("eps", [P, 1], F32),
    }
    return c


def clear_semaphores(nc, sems):
    with nc.Block() as block:
        @block.gpsimd
        def _(pool):
            first, last = sems[0].num, sems[-1].num
            assert [one.num for one in sems] == list(range(first, last + 1))
            pool.sem_clear(range(first, last + 1))


def sort_edges(nc, src, dst, recs, const, keep):
    ident, identb, tri, ones, row, rowb, col = (const[k] for k in ("ident", "identb", "tri", "ones", "row", "rowb", "col"))
    with ExitStack() as ctx:
        def sb(name, shape, dt):
            return ctx.enter_context(nc.sbuf_tensor(name, shape, dt))

        def ps(name, shape, dt=F32):
            return ctx.enter_context(nc.psum_tensor(name, shape, dt))

        sems = []

        def sem(name):
            sems.append(ctx.enter_context(nc.semaphore(name)))
            return sems[-1]

        src_i, dst_i = sb("src_i", [L, ET], I32), sb("dst_i", [L, ET], I32)
        fill = sb("fill", [P, REC_COLS], I32)
        blockf, localf = sb("blockf", [L, ET], F32), sb("localf", [L, ET], F32)
        scaled = sb("scaled", [L, ET], F32)
        onehot_block = sb("onehot_block", [L, ET, 2 * NB], BF16)
        before = sb("before", [L, NB, ET + 1], F32)
        firstp = sb("firstp", [L, ET, 2 * NB], BF16)
        zeros = sb("zeros", [L, ET], F32)
        high = sb("high", [L, ET], F32)
        onehot = [sb(f"onehot{h}", [L, CH, L], BF16) for h in range(2)]
        onehot_t = [sb(f"onehot_t{h}", [L, CH, L], BF16) for h in range(2)]
        ahead = [sb(f"ahead{h}", [L, CH, L], BF16) for h in range(2)]
        weighted = [sb(f"weighted{h}", [L, CH, 2 * NB], F32) for h in range(2)]
        slotf = sb("slotf", [L, ET], F32)
        totals = sb("totals", [L, NB], F32)
        groups_f, groups_i = sb("groups_f", [P, NB], F32), sb("groups_i", [P, NB], I32)
        group_end, group_start = sb("group_end", [P, NB], F32), sb("group_start", [P, NB], F32)
        base = sb("base", [L, NB], F32)
        giota = sb("giota", [1, GROUPS], F32)
        gcmp = sb("gcmp", [1, GROUPS, NB], BF16)
        gblk = sb("gblk", [1, GROUPS], F32)
        ps_hist = [ps(f"ps_hist{h}", [L, CH, NB]) for h in range(2)]
        ps_t = [ps(f"ps_t{h}", [L, CH, L + 1], BF16) for h in range(2)]
        ps_same = [ps(f"ps_same{h}", [L, 512]) for h in range(2)]
        ps_slot = [ps(f"ps_slot{h}", [L, CH, 2 * NB]) for h in range(2)]

        iotas_ready, consts_ready = sem("iotas_ready"), sem("consts_ready")
        edges_in, fill_set, fill_done = sem("edges_in"), sem("fill_set"), sem("fill_done")
        v_link = sem("sort_v_link")
        onehot_set = [sem(f"onehot_set{h}") for h in range(2)]
        hist_done = [sem(f"hist_done{h}") for h in range(2)]
        hist_kept = [sem(f"hist_kept{h}") for h in range(2)]
        totals_set, totals_done = sem("totals_set"), sem("totals_done")
        onehot2_set = [sem(f"onehot2_set{h}") for h in range(2)]
        t_done = [sem(f"t_done{h}") for h in range(2)]
        t_kept = [sem(f"t_kept{h}") for h in range(2)]
        same_done = [sem(f"same_done{h}") for h in range(2)]
        ahead_set = [sem(f"ahead_set{h}") for h in range(2)]
        slot_done = [sem(f"slot_done{h}") for h in range(2)]
        weighted_set = [sem(f"weighted_set{h}") for h in range(2)]
        weighted_used = [sem(f"weighted_used{h}") for h in range(2)]
        firstp_set = sem("firstp_set")
        ITER = ET // CH // 2
        block_ctx = ExitStack()
        block = block_ctx.enter_context(nc.Block())

        @block.sync
        def _(sp):
            sp.dma_start(src_i[:, :], src.rearrange("(p t) -> p t", t=ET)).then_inc(edges_in, 16)
            sp.dma_start(dst_i[:, :], dst.rearrange("(p t) -> p t", t=ET)).then_inc(edges_in, 16)
            sp.wait_ge(fill_set, 1)
            for rec in recs:
                sp.dma_start(rec.rearrange("(p c) o -> p (c o)", c=REC_COLS), fill[:, :]).then_inc(fill_done, 16)
            sp.wait_ge(fill_done, 16 * RECS)

        @block.gpsimd
        def _(pool):
            nc.gpsimd.iota(row[:, :], pattern=[[1, P]], base=0, channel_multiplier=0, allow_small_or_imprecise_dtypes=True).then_inc(iotas_ready, 1)
            nc.gpsimd.iota(col[:, :], pattern=[[1, 1]], base=0, channel_multiplier=1, allow_small_or_imprecise_dtypes=True).then_inc(iotas_ready, 1)
            nc.gpsimd.iota(giota[:, :], pattern=[[1, GROUPS]], base=0, channel_multiplier=0, allow_small_or_imprecise_dtypes=True).then_inc(iotas_ready, 1)
            nc.gpsimd.memset(fill[:, :], PAD_RECORD).then_inc(fill_set, 1)
            nc.gpsimd.memset(const["eps"][:, :], 1e-5)
            nc.gpsimd.memset(ones[:, :], 1.0).then_inc(consts_ready, 1)

        @block.vector
        def _(dve):
            link = linker(dve, v_link)
            v = nc.vector
            for h in range(2):
                dve.sem_inc(hist_done[h], 1)
                dve.sem_inc(slot_done[h], 1)
                dve.sem_inc(weighted_used[h], 1)
            dve.wait_ge(iotas_ready, 3)
            v.tensor_copy(rowb[:, :], row[:, :])
            v.tensor_scalar(ident[:, :], row[:, :], col[:, 0:1], None, ALU.is_equal)
            v.tensor_scalar(identb[:, :], row[:, :], col[:, 0:1], None, ALU.is_equal)
            link(v.tensor_scalar(tri[:, :], row[:, :], col[:, 0:1], None, ALU.is_gt))
            dve.sem_inc(consts_ready, 1)
            dve.wait_ge(edges_in, 32)
            v.scalar_tensor_tensor(keep["key"][:, :], src_i[:, :], float(KEY), dst_i[:, :], ALU.mult, ALU.add)
            link(v.tensor_scalar(scaled[:, :], src_i[:, :], 1.0 / L, 0.5 / L - 0.5, ALU.mult, ALU.add))
            link(v.tensor_scalar(blockf[:, :], scaled[:, :], ROUND, -ROUND, ALU.add, ALU.add))
            link(v.scalar_tensor_tensor(localf[:, :], blockf[:, :], -float(L), src_i[:, :], ALU.mult, ALU.add))
            link(v.tensor_tensor(onehot_block[:, :, NB:2 * NB], blockf[:, :].unsqueeze(2).broadcast_to([L, ET, NB]),
                                 row[0:L, 0:NB].unsqueeze(1).broadcast_to([L, ET, NB]), ALU.is_equal))
            v.memset(before[:, :, 0:1], 0.0)
            v.memset(zeros[:, :], 0.0)
            link(v.tensor_scalar(onehot_block[:, :, 0:NB], onehot_block[:, :, NB:2 * NB], 256.0, None, ALU.mult))
            with v.Fori(0, ITER) as t:
                for h in range(2):
                    dve.wait_ge(hist_done[h], t + 1)
                    for j in range(CH):
                        ins = v.tensor_scalar(onehot[h][:, j, :], rowb[0:L, 0:L],
                                              localf[:, DS((2 * t + h) * CH + j, 1)], None, ALU.is_equal)
                    ins.then_inc(onehot_set[h], 1)
            for h in range(2):
                dve.wait_ge(hist_kept[h], ITER + 1)
            for b in range(NB):
                ins = v.tensor_tensor_scan(before[:, b, 1:ET + 1], before[:, b, 1:ET + 1], zeros[:, :], 0.0, ALU.add, ALU.add)
            link(ins)
            v.tensor_copy(totals[:, :], before[:, :, ET]).then_inc(totals_set, 1)
            dve.wait_ge(totals_done, 1)
            link(v.tensor_scalar(groups_i[0:L, :], ps_hist[0][:, 1, :], float(GE - 1), None, ALU.add))
            link(v.tensor_scalar(groups_i[0:L, :], groups_i[0:L, :], GE.bit_length() - 1, None, ALU.logical_shift_right))
            link(v.tensor_copy(groups_f[0:L, :], groups_i[0:L, :]))
            link(v.tensor_tensor_scan(group_end[0:L, :], groups_f[0:L, :], zeros[:, 0:NB], 0.0, ALU.add, ALU.add))
            link(v.tensor_sub(group_start[0:L, :], group_end[0:L, :], groups_f[0:L, :]))
            link(v.tensor_scalar(base[:, :], group_start[0:L, :], float(GE), 1.0 - MIDDLE, ALU.mult, ALU.add))
            link(v.tensor_add(base[:, :], base[:, :], ps_hist[0][:, 0, :]))
            link(v.tensor_tensor(gcmp[:, :, :], giota[:, :].unsqueeze(2).broadcast_to([1, GROUPS, NB]),
                                 group_start[0:1, :].unsqueeze(1).broadcast_to([1, GROUPS, NB]), ALU.is_ge))
            link(v.tensor_reduce(gblk[:, :], gcmp[:, :, 1:NB], AX.X, ALU.add))
            v.tensor_copy(keep["group_block"][:, :], gblk[:, :])
            for b in range(NB):
                link(v.tensor_scalar(before[:, b, 0:ET], before[:, b, 0:ET], base[:, b:b + 1], None, ALU.add))
                link(v.tensor_scalar(high[:, :], before[:, b, 0:ET], 1.0 / 256, 0.5 / 256 - 0.5, ALU.mult, ALU.add))
                link(v.tensor_scalar(high[:, :], high[:, :], ROUND, -ROUND, ALU.add, ALU.add))
                v.tensor_copy(firstp[:, :, b], high[:, :])
                link(v.scalar_tensor_tensor(firstp[:, :, NB + b], high[:, :], -256.0, before[:, b, 0:ET], ALU.mult, ALU.add))
            dve.sem_inc(firstp_set, 1)

            def onehots(t, h):
                dve.wait_ge(t_done[h], t + 1)
                for j in range(CH):
                    ins = v.tensor_scalar(onehot[h][:, j, :], rowb[0:L, 0:L],
                                          localf[:, DS((2 * t + h) * CH + j, 1)], None, ALU.is_equal)
                ins.then_inc(onehot2_set[h], 1)

            for h in range(2):
                dve.sem_inc(t_done[h], 1)
            with v.Fori(0, ITER) as t:
                for h in range(2):
                    onehots(t, h)
                for h in range(2):
                    dve.wait_ge(same_done[h], t + 1)
                    dve.wait_ge(slot_done[h], t + 1)
                    v.tensor_tensor(ahead[h][:, :, :], ps_same[h][:, 0:CH * L].rearrange("p (c e) -> p c e", c=CH),
                                    tri[0:L, 0:L].unsqueeze(1).broadcast_to([L, CH, L]), ALU.mult).then_inc(ahead_set[h], 1)
                for h in range(2):
                    dve.wait_ge(slot_done[h], t + 2)
                    dve.wait_ge(weighted_used[h], t + 1)
                    v.tensor_tensor(weighted[h][:, :, :], ps_slot[h][:, :, :],
                                    onehot_block[:, DS((2 * t + h) * CH, CH), :], ALU.mult).then_inc(weighted_set[h], 1)
                for h in range(2):
                    dve.wait_ge(weighted_set[h], t + 2)
                    v.tensor_reduce(slotf[:, DS((2 * t + h) * CH, CH)], weighted[h][:, :, :], AX.X, ALU.add).then_inc(weighted_used[h], 1)
            for h in range(2):
                dve.wait_ge(weighted_used[h], ITER + 1)
            v.tensor_scalar(keep["slot"][:, :], slotf[:, :], MIDDLE, None, ALU.add)

        @block.tensor
        def _(pe):
            pe.wait_ge(consts_ready, 2)
            with nc.tensor.Fori(0, ITER) as t:
                for h in range(2):
                    pe.wait_ge(onehot_set[h], t + 1)
                    pe.wait_ge(hist_kept[h], t + 1)
                    for j in range(CH):
                        ins = nc.tensor.matmul(ps_hist[h][:, j, :], onehot[h][:, j, :],
                                               onehot_block[:, DS((2 * t + h) * CH + j, 1), NB:2 * NB].rearrange("p o b -> p (o b)"), start=True, stop=True)
                    ins.then_inc(hist_done[h], 1)
            pe.wait_ge(totals_set, 1)
            nc.tensor.matmul(ps_hist[0][:, 0, :], tri[0:L, 0:L], totals[:, :], start=True, stop=True)
            nc.tensor.matmul(ps_hist[0][:, 1, :], ones[0:L, 0:L], totals[:, :], start=True, stop=True).then_inc(totals_done, 1)
            pe.wait_ge(firstp_set, 1)
            with nc.tensor.Fori(0, ITER) as t:
                for h in range(2):
                    pe.wait_ge(onehot2_set[h], t + 1)
                    pe.wait_ge(t_kept[h], t + 1)
                    for j in range(CH):
                        ins = nc.tensor.transpose(ps_t[h][:, j, 0:L], onehot[h][:, j, :], identb[0:L, 0:L])
                    ins.then_inc(t_done[h], 1)
                for h in range(2):
                    pe.wait_ge(t_kept[h], t + 2)
                    pe.wait_ge(ahead_set[h], t + 1)
                    for j in range(CH):
                        ins = nc.tensor.matmul(ps_same[h][:, j * L:(j + 1) * L], onehot_t[h][:, j, :], onehot_t[h][:, j, :], start=True, stop=True)
                    ins.then_inc(same_done[h], 1)
                for h in range(2):
                    pe.wait_ge(ahead_set[h], t + 2)
                    pe.wait_ge(weighted_set[h], t + 1)
                    for j in range(CH):
                        tile = DS((2 * t + h) * CH + j, 1)
                        nc.tensor.matmul(ps_slot[h][:, j, :], onehot_t[h][:, j, :],
                                         firstp[:, tile, :].rearrange("p o b -> p (o b)"), start=True, stop=False)
                        ins = nc.tensor.matmul(ps_slot[h][:, j, NB:2 * NB], ahead[h][:, j, :],
                                               onehot_block[:, tile, NB:2 * NB].rearrange("p o b -> p (o b)"), start=False, stop=True)
                    ins.then_inc(slot_done[h], 1)

        @block.scalar
        def _(act):
            for h in range(2):
                act.sem_inc(hist_kept[h], 1)
                act.sem_inc(t_kept[h], 1)
                act.sem_inc(ahead_set[h], 1)
                act.sem_inc(weighted_set[h], 1)
            with nc.scalar.Fori(0, ITER) as t:
                for h in range(2):
                    act.wait_ge(hist_done[h], t + 2)
                    nc.scalar.activation(before[:, :, DS((2 * t + h) * CH + 1, CH)], ps_hist[h][:, :, :].rearrange("p c b -> p b c"), ACT.Copy).then_inc(hist_kept[h], 1)
            with nc.scalar.Fori(0, ITER) as t:
                for h in range(2):
                    act.wait_ge(t_done[h], t + 2)
                    act.wait_ge(slot_done[h], t + 1)
                    nc.scalar.activation(onehot_t[h][:, :, :], ps_t[h][:, :, 0:L], ACT.Copy).then_inc(t_kept[h], 1)

        block_ctx.close()
        clear_semaphores(nc, sems)


def scatter_records(nc, pool, keep, recs, sb, sem):
    slot_set = [sb(f"scatter_slot{s}", [L, RECS], I32) for s in range(2)]
    key_set = [sb(f"scatter_key{s}", [L, RECS], I32) for s in range(2)]
    staged = [sem(f"scatter_staged{s}") for s in range(2)]
    written = [sem(f"records_written{j}") for j in range(RECS)]
    turns = ET // RECS // 2

    def turn(t, s, first=False):
        at = DS((t * 2 + s) * RECS, RECS)
        nc.gpsimd.tensor_copy(slot_set[s][:, :], keep["slot"][:, at])
        nc.gpsimd.tensor_copy(key_set[s][:, :], keep["key"][:, at]).then_inc(staged[s], 1)
        pool.wait_ge(staged[s], t + 1)
        pool.nop(nofuse=True)
        for j in range(RECS):
            if not first:
                pool.wait_ge(written[j], t * 32 + s * 16)
                pool.nop(nofuse=True)
            nc.gpsimd.indirect_dma_start(recs[j], bass.IndirectOffsetOnAxis(ap=slot_set[s][:, j:j + 1], axis=0),
                                         key_set[s][:, j:j + 1], None).then_inc(written[j], 16)

    turn(0, 0, first=True)
    turn(0, 1)
    with nc.gpsimd.Fori(1, turns) as t:
        turn(t, 0)
        turn(t, 1)
    for j in range(RECS):
        pool.wait_ge(written[j], ET // RECS * 16)


def project_and_mix(nc, a, const, keep, x_sb, recs, tab_v, tab_u, tab_e):
    ident, ones, eps = const["ident"], const["ones"], const["eps"]
    with ExitStack() as ctx:
        def sb(name, shape, dt=F32):
            return ctx.enter_context(nc.sbuf_tensor(name, shape, dt))

        def ps(name, shape, dt=F32):
            return ctx.enter_context(nc.psum_tensor(name, shape, dt))

        def sem(name):
            return ctx.enter_context(nc.semaphore(name))

        w_e, w_r = sb("w_e", [P, KF, HEADS, D]), sb("w_r", [P, KF, HEADS, D])
        w_in, w_out = sb("w_in", [P, KF, F]), sb("w_out", [P, KF, F])
        a_row = sb("a_row", [P, HEADS, 5, D])
        b_in_col, b_out_row = sb("b_in_col", [P, KF]), sb("b_out_row", [1, F])
        wq2, wk2 = sb("wq2", [P, 2 * SLICE]), sb("wk2", [P, 2 * SLICE])
        wv2 = sb("wv2", [P, 2 * D])
        w_node = sb("w_node", [P, KF, 2 * HEADS])
        half_prd = sb("half_prd", [P, HEADS, D])
        prod_e = sb("prod_e", [P, KF, HEADS, D])
        term = sb("term", [P, 4, KF, HEADS])
        stats, moments = sb("stats", [L, NB, 6]), sb("moments", [L, NB, 2])
        deviation, rstd = sb("deviation", [L, NB]), sb("rstd", [L, NB])
        xn = sb("xn", [L, F])
        xn_t = sb("xn_t", [P, KF, L])
        xm_t = sb("xm_t", [P, KF, L])
        row_v, row_e, row_u = sb("row_v", [L, EW]), sb("row_e", [L, F]), sb("row_u", [L, HEADS])
        squares, squares_w, square_sum = sb("squares", [L, HEADS, D]), sb("squares_w", [L, HEADS, D]), sb("square_sum", [L, HEADS])
        q_max, q_sum, q_inv = sb("q_max", [L, HEADS]), sb("q_sum", [L, HEADS]), sb("q_inv", [L, HEADS])
        q_exp, q_soft = sb("q_exp", [L, HEADS, SLICE]), sb("q_soft", [L, HEADS * SLICE])
        qt_all, kt_all = sb("qt_all", [P, 2, N]), sb("kt_all", [P, 2, N])
        v_all = sb("v_all", [L, NB, F])
        k_max, k_sum, k_inv = sb("k_max", [P, 2]), sb("k_sum", [P, 2]), sb("k_inv", [P, 2])
        staged_t = sb("staged_t", [P, 2, L])
        k_rows = sb("k_rows", [L, 2 * P])
        head_of_row, head_of_row_i = sb("head_of_row", [P, 1]), sb("head_of_row_i", [P, 1], I32)
        head_of_col, same_head = sb("head_of_col", [P, 2 * P]), sb("same_head", [P, 2 * P])
        late = prod_e[:, :, :, :].rearrange("p k h d -> p (k h d)")
        kv = late[:, 0:F].rearrange("p (g c) -> p g c", g=2)
        kv_t = late[:, F:2 * F].rearrange("p (g c n) -> p g c n", g=2, c=2)
        kvw = late[:, 2 * F:4 * F].rearrange("p (g f) -> p g f", g=2)
        zero_rows = sb("zero_rows", [L, 2 * P])
        ps_xt, ps_hr, ps_he = ps("ps_xt", [P, F]), ps("ps_hr", [P, F]), ps("ps_he", [P, F])
        ps_s, ps_xm, ps_q = ps("ps_s", [L, 2 * HEADS]), ps("ps_xm", [P, F]), ps("ps_q", [L, F])
        ps_v, ps_k = ps("ps_v", [P, F]), ps("ps_k", [P, F])

        loaded = [sem(f"loaded{i}") for i in range(2)]
        zeroed, masks_set = sem("zeroed"), sem("masks_set")
        dve_link = sem("mix_dve_link")
        var_set, dev_set = sem("var_set"), sem("dev_set")
        weights_set = sem("weights_set")
        names = ("xn_set xt_done xt_kept proj_done rows_kept rows_set rows_free xm_done xm_kept qvk_done kv_kept "
                 "q_shifted q_exped q_set qt_done qt_kept loop_link kmax_set kexp_set k_staged k_done k_kept kv_done "
                 "kv_set kvt_done kvt_kept kvw_done kvw_kept q_staged mix_done mix_added").split()
        s = {n: sem(n) for n in names}
        rows_out, weights_in = sem("rows_out"), sem("weights_in")
        WEIGHT_LOADS = 2 * KF + 5
        block = ctx.enter_context(nc.Block())

        @block.sync
        def _(sp):
            sp.dma_start(x_sb[:, :, :], a["x"].rearrange("(t p) f -> p t f", p=L)).then_inc(loaded[0], 16)
            sp.wait_ge(zeroed, 1)
            for h in range(2):
                sp.dma_start(wq2[h * D:(h + 1) * D, h * SLICE:(h + 1) * SLICE], a["L0_mix_Wq"]).then_inc(loaded[1], 16)
                sp.dma_start(wk2[h * D:(h + 1) * D, h * SLICE:(h + 1) * SLICE], a["L0_mix_Wk"]).then_inc(loaded[1], 16)
                sp.dma_start(wv2[h * D:(h + 1) * D, h * D:(h + 1) * D], a["L0_mix_Wv"]).then_inc(loaded[1], 16)
            with nc.sync.Fori(0, NB) as t:
                sp.wait_ge(s["rows_set"], t + 2)
                at = DS(t * L, L)
                sp.dma_start(tab_v[at, :], row_v[:, :]).then_inc(rows_out, 16)
                sp.dma_start(tab_u[at, 0:F], row_v[:, 0:F]).then_inc(rows_out, 16)
                sp.dma_start(tab_u[at, F:EW], row_u[:, :]).then_inc(rows_out, 16)
                sp.dma_start(tab_e[at, :], row_e[:, :]).then_inc(rows_out, 16)
                sp.wait_ge(rows_out, t * 64 + 64)
                sp.sem_inc(s["rows_free"], 1)

        @block.gpsimd
        def _(pool):
            nc.gpsimd.memset(wq2[:, :], 0.0)
            nc.gpsimd.memset(wk2[:, :], 0.0)
            nc.gpsimd.memset(zero_rows[:, :], 0.0)
            nc.gpsimd.memset(wv2[:, :], 0.0).then_inc(zeroed, 1)
            nc.gpsimd.iota(head_of_row_i[:, :], pattern=[[1, 1]], base=0, channel_multiplier=1)
            nc.gpsimd.iota(head_of_col[:, :], pattern=[[1, 2 * P // D], [0, D]], base=0, channel_multiplier=0,
                           allow_small_or_imprecise_dtypes=True).then_inc(masks_set, 1)
            scatter_records(nc, pool, keep, recs, sb, sem)

        @block.vector
        def _(dve):
            v = nc.vector
            link = linker(dve, dve_link)
            for n in ("xt_done", "qt_done", "mix_done", "k_done"):
                dve.sem_inc(s[n], 1)
            dve.wait_ge(loaded[0], 16)
            with v.Fori(0, NB) as t:
                ins = v.bn_stats(stats[:, DS(t, 1), :].rearrange("p o s -> p (o s)"),
                                 x_sb[:, DS(t, 1), :].rearrange("p o f -> p (o f)"))
            link(v.memset(q_max[:, :], 0.0))
            for t in range(NB):
                ins = v.bn_aggr(moments[:, t, :], stats[:, t, :])
            ins.then_inc(var_set, 1)
            dve.wait_ge(weights_in, 16 * WEIGHT_LOADS)

            def a_part(i):
                return a_row[:, :, i, :].unsqueeze(1).broadcast_to([P, KF, HEADS, D])

            for i, (w, part) in enumerate(((w_e, 0), (w_e, 1), (w_r, 2))):
                link(v.tensor_tensor(prod_e[:, :, :, :], w[:, :, :, :], a_part(part), ALU.mult))
                link(v.tensor_reduce(term[:, i, :, :], prod_e[:, :, :, :], AX.X, ALU.add))
            v.tensor_sub(w_node[:, :, 0:HEADS], term[:, 0, :, :], term[:, 2, :, :])
            v.tensor_add(w_node[:, :, HEADS:2 * HEADS], term[:, 1, :, :], term[:, 2, :, :])
            v.tensor_scalar(half_prd[:, :, :], a_row[:, :, 4, :], 0.5, None, ALU.mult).then_inc(weights_set, 1)
            dve.wait_ge(weights_set, 1)
            dve.wait_ge(masks_set, 1)
            link(v.tensor_scalar(head_of_row_i[:, :], head_of_row_i[:, :], SLICE.bit_length() - 1, None, ALU.logical_shift_right))
            link(v.tensor_copy(head_of_row[:, :], head_of_row_i[:, :]))
            link(v.tensor_scalar(same_head[:, :], head_of_col[:, :], head_of_row[:, 0:1], None, ALU.is_equal))
            dve.wait_ge(dev_set, 1)
            link(v.reciprocal(rstd[:, :], deviation[:, :]))
            STEPS = 7
            with v.Fori(0, NB) as t:
                step = linker(dve, s["loop_link"], t * STEPS)
                dve.wait_ge(s["xt_done"], t + 1)
                v.tensor_scalar(xn[:, :], x_sb[:, DS(t, 1), :].rearrange("p o f -> p (o f)"), moments[:, DS(t, 1), 0:1].rearrange("p a b -> p (a b)"),
                                rstd[:, DS(t, 1)], ALU.subtract, ALU.mult).then_inc(s["xn_set"], 1)
                dve.wait_ge(s["rows_kept"], t + 2)
                h_r = row_v[:, 0:F].rearrange("p (h d) -> p h d", h=HEADS)
                step(v.tensor_tensor(squares[:, :, :], h_r, h_r, ALU.mult))
                step(v.tensor_tensor(squares_w[:, :, :], squares[:, :, :], half_prd[0:L, :, :], ALU.mult))
                step(v.tensor_reduce(square_sum[:, :], squares_w[:, :, :], AX.X, ALU.add))
                v.tensor_tensor(row_v[:, F:EW], ps_s[:, HEADS:2 * HEADS], square_sum[:, :], ALU.add)
                v.scalar_tensor_tensor(row_u[:, :], ps_s[:, 0:HEADS], -1.0, square_sum[:, :], ALU.mult, ALU.subtract).then_inc(s["rows_set"], 1)
                dve.wait_ge(s["qvk_done"], t + 2)
                q = ps_q[:, 0:HEADS * SLICE].rearrange("p (h s) -> p h s", h=HEADS)
                step(v.tensor_reduce(q_max[:, :], q, AX.X, ALU.max))
                v.tensor_tensor(q_exp[:, :, :], q, q_max[:, :].unsqueeze(2).broadcast_to([L, HEADS, SLICE]), ALU.subtract).then_inc(s["q_shifted"], 1)
                dve.wait_ge(s["q_exped"], t + 1)
                step(v.tensor_reduce(q_sum[:, :], q_exp[:, :, :], AX.X, ALU.add))
                step(v.reciprocal(q_inv[:, :], q_sum[:, :]))
                dve.wait_ge(s["qt_done"], t + 1)
                step(v.tensor_tensor(q_soft[:, :].rearrange("p (h s) -> p h s", h=HEADS), q_exp[:, :, :],
                                     q_inv[:, :].unsqueeze(2).broadcast_to([L, HEADS, SLICE]), ALU.mult))
                dve.sem_inc(s["q_set"], 1)
            assert step.count[0] == STEPS
            dve.wait_ge(s["kv_kept"], NB + 1)
            link(v.tensor_reduce(k_max[:, :], kt_all[:, :, :], AX.X, ALU.max))
            v.tensor_scalar(k_max[:, :], k_max[:, :], -1.0, None, ALU.mult).then_inc(s["kmax_set"], 1)
            dve.wait_ge(s["kexp_set"], 1)
            link(v.tensor_reduce(k_sum[:, :], kt_all[:, :, :], AX.X, ALU.add))
            link(v.reciprocal(k_inv[:, :], k_sum[:, :]))
            with v.Fori(0, NB) as t:
                dve.wait_ge(s["k_done"], t + 1)
                v.tensor_copy(staged_t[:, :, :], kt_all[:, :, DS(t * L, L)]).then_inc(s["k_staged"], 1)
            dve.wait_ge(s["kv_done"], 1)
            for g, acc in enumerate((ps_hr, ps_he)):
                ins = v.scalar_tensor_tensor(kv[:, g, :], acc[:, 0:2 * P], k_inv[:, g:g + 1], same_head[:, :], ALU.mult, ALU.mult)
            ins.then_inc(s["kv_set"], 1)
            dve.wait_ge(s["qt_kept"], NB + 1)
            with v.Fori(0, NB) as t:
                dve.wait_ge(s["mix_done"], t + 1)
                v.tensor_copy(staged_t[:, :, :], qt_all[:, :, DS(t * L, L)]).then_inc(s["q_staged"], 1)
                dve.wait_ge(s["mix_done"], t + 2)
                tile = x_sb[:, DS(t, 1), :].rearrange("p o f -> p (o f)")
                v.tensor_tensor(tile, ps_xm[0:L, :], tile, ALU.add).then_inc(s["mix_added"], 1)

        @block.tensor
        def _(pe):
            t_ = nc.tensor
            pe.wait_ge(weights_set, 1)
            pe.wait_ge(loaded[1], 16 * 6)
            pe.wait_ge(weights_in, 16 * WEIGHT_LOADS)
            with t_.Fori(0, NB) as t:
                pe.wait_ge(s["xn_set"], t + 1)
                pe.wait_ge(s["xt_kept"], t + 1)
                for k in range(KF):
                    ins = t_.transpose(ps_xt[:, k * L:(k + 1) * L], xn[:, k * P:(k + 1) * P], ident[0:L, 0:L])
                ins.then_inc(s["xt_done"], 1)
                pe.wait_ge(s["xt_kept"], t + 2)
                pe.wait_ge(s["rows_kept"], t + 1)
                pe.wait_ge(s["rows_set"], t + 1)
                for k in range(KF):
                    t_.matmul(ps_hr[0:L, :], xn_t[:, k, :], w_r[:, k, :, :].rearrange("p h d -> p (h d)"), start=k == 0, stop=k == KF - 1)
                for k in range(KF):
                    t_.matmul(ps_he[0:L, :], xn_t[:, k, :], w_e[:, k, :, :].rearrange("p h d -> p (h d)"), start=k == 0, stop=k == KF - 1)
                for k in range(KF):
                    ins = t_.matmul(ps_s[:, :], xn_t[:, k, :], w_node[:, k, :], start=k == 0, stop=k == KF - 1)
                ins.then_inc(s["proj_done"], 1)
                pe.wait_ge(s["xm_kept"], t + 1)
                for c in range(KF):
                    for k in range(KF):
                        ins = t_.matmul(ps_xm[:, c * L:(c + 1) * L], w_in[:, k, c * P:(c + 1) * P], xn_t[:, k, :], start=k == 0, stop=k == KF - 1)
                ins.then_inc(s["xm_done"], 1)
                pe.wait_ge(s["xm_kept"], t + 2)
                pe.wait_ge(s["kv_kept"], t + 1)
                pe.wait_ge(s["qt_kept"], t + 1)
                for c in range(KF):
                    t_.matmul(ps_q[:, c * 2 * SLICE:(c + 1) * 2 * SLICE], xm_t[:, c, :], wq2[:, :], start=True, stop=True)
                    t_.matmul(ps_v[0:L, c * P:(c + 1) * P], xm_t[:, c, :], wv2[:, :], start=True, stop=True)
                    half = c % 2 * D
                    ins = t_.matmul(ps_k[half:half + D, c // 2 * L:(c // 2 + 1) * L], wk2[:, :], xm_t[:, c, :], start=True, stop=True)
                ins.then_inc(s["qvk_done"], 1)
                pe.wait_ge(s["q_set"], t + 1)
                pe.wait_ge(s["kv_kept"], t + 2)
                for g in range(2):
                    ins = t_.transpose(ps_k[:, g * L:(g + 1) * L], q_soft[:, g * P:(g + 1) * P], ident[0:L, 0:L])
                ins.then_inc(s["qt_done"], 1)
            pe.wait_ge(s["rows_kept"], NB + 1)
            pe.wait_ge(zeroed, 1)
            for acc in (ps_hr, ps_he):
                t_.matmul(acc[:, 0:2 * P], zero_rows[:, 0:P], zero_rows[:, :], start=True, stop=False)
            with t_.Fori(0, NB) as t:
                pe.wait_ge(s["k_staged"], t + 1)
                pe.wait_ge(s["k_kept"], t + 1)
                for g in range(2):
                    ins = t_.transpose(ps_q[:, g * P:(g + 1) * P], staged_t[:, g, :], ident[:, :])
                ins.then_inc(s["k_done"], 1)
                pe.wait_ge(s["k_kept"], t + 2)
                for g, acc in enumerate((ps_hr, ps_he)):
                    ins = t_.matmul(acc[:, 0:2 * P], k_rows[:, g * P:(g + 1) * P],
                                    v_all[:, DS(t, 1), g * 2 * P:(g + 1) * 2 * P].rearrange("p o c -> p (o c)"), start=False, stop=False)
            for acc in (ps_hr, ps_he):
                ins = t_.matmul(acc[:, 0:2 * P], zero_rows[:, 0:P], zero_rows[:, :], start=False, stop=True)
            ins.then_inc(s["kv_done"], 1)
            pe.wait_ge(s["kv_set"], 1)
            for g in range(2):
                for c in range(2):
                    ins = t_.transpose(ps_xt[:, (2 * g + c) * P:(2 * g + c + 1) * P], kv[:, g, c * P:(c + 1) * P], ident[:, :])
            ins.then_inc(s["kvt_done"], 1)
            pe.wait_ge(s["kvt_kept"], 1)
            pe.wait_ge(s["qt_kept"], NB + 1)
            for g, acc in enumerate((ps_v, ps_k)):
                for c in range(2):
                    ins = t_.matmul(acc[:, :], kv_t[:, g, c, :], w_out[:, 2 * g + c, :], start=c == 0, stop=c == 1)
            ins.then_inc(s["kvw_done"], 1)
            pe.wait_ge(s["kvw_kept"], 1)
            with t_.Fori(0, NB) as t:
                pe.wait_ge(s["q_staged"], t + 1)
                pe.wait_ge(s["mix_added"], t + 1)
                for g in range(2):
                    t_.matmul(ps_xm[0:L, :], staged_t[:, g, :], kvw[:, g, :], start=g == 0, stop=False)
                t_.matmul(ps_xm[0:L, :], ones[0:1, 0:L], b_out_row[:, :], start=False, stop=True).then_inc(s["mix_done"], 1)

        @block.scalar
        def _(act):
            sc = nc.scalar
            for w, name in ((w_r, "L0_gnn_W_r"), (w_e, "L0_gnn_W_e")):
                for k in range(KF):
                    act.dma_start(w[:, k, :, :], a[name][:, k * P:(k + 1) * P, :].rearrange("h p d -> p h d")).then_inc(weights_in, 16)
            act.dma_start(w_in[:, :, :], a["L0_mix_W_in"].rearrange("(k p) f -> p k f", p=P)).then_inc(weights_in, 16)
            act.dma_start(w_out[:, :, :], a["L0_mix_W_out"].rearrange("(k p) f -> p k f", p=P)).then_inc(weights_in, 16)
            act.dma_start(a_row[:, :, :, :], a["L0_gnn_a"].rearrange("h (c d) -> h c d", d=D).partition_broadcast(P)).then_inc(weights_in, 16)
            act.dma_start(b_in_col[:, :], a["L0_mix_b_in"].rearrange("(k p) -> p k", p=P), allow_slow_non_contiguous=True).then_inc(weights_in, 16)
            act.dma_start(b_out_row[:, :], a["L0_mix_b_out"].rearrange("(o f) -> o f", o=1)).then_inc(weights_in, 16)
            for n in ("xt_kept", "rows_kept", "rows_free", "xm_kept", "kv_kept", "qt_kept", "k_kept", "mix_added", "xm_done", "qvk_done", "rows_set"):
                act.sem_inc(s[n], 1)
            act.wait_ge(weights_in, 16 * WEIGHT_LOADS)
            act.wait_ge(var_set, 1)
            sc.activation(deviation[:, :], moments[:, :, 1], ACT.Sqrt, bias=eps[0:L, 0:1]).then_inc(dev_set, 1)
            with sc.Fori(0, NB) as t:
                act.wait_ge(s["xt_done"], t + 2)
                act.wait_ge(s["xm_done"], t + 1)
                sc.copy(xn_t[:, :, :], ps_xt[:, 0:KF * L].rearrange("p (k n) -> p k n", k=KF)).then_inc(s["xt_kept"], 1)
                act.wait_ge(s["proj_done"], t + 1)
                act.wait_ge(s["rows_free"], t + 1)
                sc.copy(row_e[:, :], ps_he[0:L, :])
                sc.copy(row_v[:, 0:F], ps_hr[0:L, :]).then_inc(s["rows_kept"], 1)
                act.wait_ge(s["xm_done"], t + 2)
                act.wait_ge(s["qvk_done"], t + 1)
                for c in range(KF):
                    ins = sc.activation(xm_t[:, c, :], ps_xm[:, c * L:(c + 1) * L], ACT.Identity, bias=b_in_col[:, c:c + 1])
                ins.then_inc(s["xm_kept"], 1)
                act.wait_ge(s["qvk_done"], t + 2)
                sc.copy(v_all[:, DS(t, 1), :].rearrange("p o f -> p (o f)"), ps_v[0:L, :])
                sc.copy(kt_all[:, :, DS(t * L, L)], ps_k[:, 0:2 * L].rearrange("p (g n) -> p g n", g=2)).then_inc(s["kv_kept"], 1)
                act.wait_ge(s["q_shifted"], t + 1)
                sc.activation(q_exp[:, :, :], q_exp[:, :, :], ACT.Exp).then_inc(s["q_exped"], 1)
                act.wait_ge(s["qt_done"], t + 2)
                sc.copy(qt_all[:, :, DS(t * L, L)], ps_k[:, 0:2 * L].rearrange("p (g n) -> p g n", g=2)).then_inc(s["qt_kept"], 1)
            act.wait_ge(s["kmax_set"], 1)
            for g in range(2):
                ins = sc.activation(kt_all[:, g, :], kt_all[:, g, :], ACT.Exp, bias=k_max[:, g:g + 1])
            ins.then_inc(s["kexp_set"], 1)
            with sc.Fori(0, NB) as t:
                act.wait_ge(s["k_done"], t + 2)
                sc.copy(k_rows[:, :], ps_q[:, 0:2 * P]).then_inc(s["k_kept"], 1)
            act.wait_ge(s["kvt_done"], 1)
            sc.copy(kv_t[:, :, :, :].rearrange("p g c n -> p (g c n)"), ps_xt[:, :]).then_inc(s["kvt_kept"], 1)
            act.wait_ge(s["kvw_done"], 1)
            sc.copy(kvw[:, 0, :], ps_v[:, :])
            sc.copy(kvw[:, 1, :], ps_k[:, :]).then_inc(s["kvw_kept"], 1)


def read_sorted_edges(nc, const, recs, merged, edge):
    ROWS, PER = ST // 6, 6
    with ExitStack() as ctx:
        def sb(name, shape, dt=F32):
            return ctx.enter_context(nc.sbuf_tensor(name, shape, dt))

        def sem(name):
            return ctx.enter_context(nc.semaphore(name))

        lists = sb("lists", [ROWS, RECS, PER * P], I32)
        best = sb("best", [ROWS, PER * P])
        best_i = sb("best_i", [ROWS, PER * P], I32)
        key_t = sb("key_t", [P, ST], I32)
        source_i = sb("source_i", [P, ST], I32)
        source, scaled, blk, pad = sb("source", [P, ST]), sb("scaled_t", [P, ST]), sb("blk_t", [P, ST]), sb("pad_t", [P, ST])
        ps_key = ctx.enter_context(nc.psum_tensor("ps_key", [P, 2, 512], F32))
        lists_in, merged_set, merged_out = sem("lists_in"), sem("merged_set"), sem("merged_out")
        turned, link_s = sem("turned"), sem("read_link")
        block = ctx.enter_context(nc.Block())

        @block.sync
        def _(sp):
            for j in range(RECS):
                sp.dma_start(lists[:, j, :], recs[j][1:1 + EP, :].rearrange("(r x) o -> r (x o)", r=ROWS)).then_inc(lists_in, 16)
            sp.dma_start(merged[0:1, :], recs[0][0:1, :]).then_inc(merged_out, 16)
            sp.dma_start(merged[EP + 1:EP + 2, :], recs[0][EP + 1:EP + 2, :]).then_inc(merged_out, 16)
            sp.wait_ge(merged_set, 1)
            sp.dma_start(merged[1:1 + EP, :].rearrange("(r x) o -> r (x o)", r=ROWS), best_i[:, :]).then_inc(merged_out, 16)
            sp.wait_ge(merged_out, 48)

        @block.vector
        def _(dve):
            v = nc.vector
            link = linker(dve, link_s)
            dve.wait_ge(lists_in, 16 * RECS)
            link(v.tensor_tensor(best[:, :], lists[:, 0, :], lists[:, 1, :], ALU.min))
            for j in range(2, RECS):
                link(v.tensor_tensor(best[:, :], best[:, :], lists[:, j, :], ALU.min))
            v.tensor_copy(best_i[:, :], best[:, :]).then_inc(merged_set, 1)
            dve.wait_ge(turned, 1)
            link(v.tensor_copy(key_t[:, :].rearrange("p (r i j) -> p i j r", i=2, j=PER // 2),
                               ps_key[:, :, 0:PER // 2 * ROWS].rearrange("p i (j r) -> p i j r", j=PER // 2)))
            link(v.tensor_scalar(source_i[:, :], key_t[:, :], KEY.bit_length() - 1, None, ALU.logical_shift_right))
            v.tensor_scalar(edge["dst"][:, :], key_t[:, :], KEY - 1, None, ALU.bitwise_and)
            link(v.tensor_copy(source[:, :], source_i[:, :]))
            v.tensor_scalar(edge["src"][:, :], source[:, :], float(N - 1), None, ALU.min)
            link(v.tensor_scalar(scaled[:, :], source[:, :], 1.0 / L, 0.5 / L - 0.5, ALU.mult, ALU.add))
            v.tensor_scalar(pad[:, :], source[:, :], float(N), 1000.0, ALU.is_ge, ALU.mult)
            link(v.tensor_scalar(blk[:, :], scaled[:, :], ROUND, -ROUND, ALU.add, ALU.add))
            link(v.scalar_tensor_tensor(source[:, :], blk[:, :], -float(L), source[:, :], ALU.mult, ALU.add))
            link(v.tensor_add(edge["local"][:, :], source[:, :], pad[:, :]))

        @block.tensor
        def _(pe):
            pe.wait_ge(merged_set, 1)
            for j in range(PER):
                half, at = j // (PER // 2), j % (PER // 2) * ROWS
                ins = nc.tensor.transpose(ps_key[:, half, at:at + ROWS], best[:, j * P:(j + 1) * P], const["ident"][0:ROWS, 0:ROWS])
            ins.then_inc(turned, 1)


def score_edges(nc, a, const, edge, tab_v, tab_u, scores):
    ident, row = const["ident"], const["row"]
    ITER = GROUPS // 2
    with ExitStack() as ctx:
        def sb(name, shape, dt=F32):
            return ctx.enter_context(nc.sbuf_tensor(name, shape, dt))

        def ps(name, shape, dt=F32):
            return ctx.enter_context(nc.psum_tensor(name, shape, dt))

        def sem(name):
            return ctx.enter_context(nc.semaphore(name))

        def sems(name):
            return [sem(f"{name}{h}") for h in range(2)]

        def sbs(name, shape, dt=F32):
            return [sb(f"{name}{h}", shape, dt) for h in range(2)]

        index_v, index_u = sbs("index_v", [P, GROUP], I32), sbs("index_u", [P, GROUP], I32)
        rows_v, rows_u = sbs("rows_v", [P, GROUP, EW]), sbs("rows_u", [P, GROUP, EW])
        w, w_abs = sbs("w", [P, GROUP, EW]), sbs("w_abs", [P, KF, GE])
        slope, z = sbs("slope", [P, KF, GE]), sbs("z", [P, KF, GE])
        score = sbs("score", [HEADS, GE])
        a_abs, minus_prd = sb("a_abs", [P, KF]), sb("minus_prd", [P, KF])
        head_i, head_f = sb("head_i", [P, KF], I32), sb("head_f", [P, KF])
        head_sum = sb("head_sum", [P, KF, HEADS])
        ps_w = [ps(f"ps_w{h}", [P, KF, GE]) for h in range(2)]
        ps_score = [ps(f"ps_score{h}", [P, 512]) for h in range(2)]

        index_set, gathered, w_set, turned = sems("index_set"), sems("gathered"), sems("w_set"), sems("w_turned")
        abs_set, slope_set, z_set, summed = sems("abs_set"), sems("slope_set"), sems("z_set"), sems("summed")
        score_kept, score_free, score_out = sems("score_kept"), sems("score_free"), sems("score_out")
        vectors_in, iota_set, vectors_set, link_s = sem("vectors_in"), sem("head_iota_set"), sem("vectors_set"), sem("score_link")
        block = ctx.enter_context(nc.Block())

        @block.sync
        def _(sp):
            for tile, part in ((a_abs, 3), (minus_prd, 4)):
                for c in range(KF):
                    for half in range(2):
                        sp.dma_start(tile[half * D:(half + 1) * D, c:c + 1],
                                     a["L0_gnn_a"][2 * c + half, part * D:(part + 1) * D].rearrange("(d o) -> d o", o=1),
                                     allow_slow_non_contiguous=True).then_inc(vectors_in, 16)
            with nc.sync.Fori(0, ITER) as t:
                for h in range(2):
                    sp.wait_ge(score_kept[h], t + 2)
                    sp.dma_start(scores[:, DS((2 * t + h) * GE, GE)], score[h][:, :]).then_inc(score_out[h], 16)
                for h in range(2):
                    sp.wait_ge(score_out[h], t * 16 + 16)
                    sp.sem_inc(score_free[h], 1)

        @block.gpsimd
        def _(pool):
            nc.gpsimd.iota(head_i[:, :], pattern=[[2 * D, KF]], base=0, channel_multiplier=1).then_inc(iota_set, 1)
            with nc.gpsimd.Fori(0, ITER) as t:
                for h in range(2):
                    pool.wait_ge(w_set[h], t + 1)
                    pool.nop(nofuse=True)
                    at = DS((2 * t + h) * GROUP, GROUP)
                    nc.gpsimd.tensor_copy(index_v[h][:, :], edge["dst"][:, at])
                    nc.gpsimd.tensor_copy(index_u[h][:, :], edge["src"][:, at]).then_inc(index_set[h], 1)
                    pool.wait_ge(index_set[h], t + 1)
                    pool.nop(nofuse=True)
                    for j in range(GROUP):
                        for rows, index, table in ((rows_v, index_v, tab_v), (rows_u, index_u, tab_u)):
                            nc.gpsimd.indirect_dma_start(rows[h][:, j, :], None, table,
                                                         bass.IndirectOffsetOnAxis(ap=index[h][:, j:j + 1], axis=0)).then_inc(gathered[h], 16)

        @block.vector
        def _(dve):
            v = nc.vector
            link = linker(dve, link_s)
            for h in range(2):
                for free in (w_set, turned, z_set, summed):
                    dve.sem_inc(free[h], 1)
            dve.wait_ge(iota_set, 1)
            link(v.tensor_scalar(head_i[:, :], head_i[:, :], D.bit_length() - 1, None, ALU.logical_shift_right))
            link(v.tensor_copy(head_f[:, :], head_i[:, :]))
            for c in range(KF):
                v.tensor_scalar(head_sum[:, c, :], row[:, 0:HEADS], head_f[:, c:c + 1], None, ALU.is_equal)
            dve.wait_ge(vectors_in, 16 * 4 * KF)
            link(v.tensor_scalar(minus_prd[:, :], minus_prd[:, :], -0.5, None, ALU.mult))
            dve.sem_inc(vectors_set, 1)
            with v.Fori(0, ITER) as t:
                for h in range(2):
                    dve.wait_ge(gathered[h], t * (32 * GROUP) + 32 * GROUP)
                    dve.wait_ge(summed[h], t + 1)
                    v.tensor_tensor(w[h][:, :, :], rows_v[h][:, :, :], rows_u[h][:, :, :], ALU.subtract).then_inc(w_set[h], 1)
                for h in range(2):
                    dve.wait_ge(abs_set[h], t + 2)
                    for c in range(KF):
                        ins = v.tensor_scalar(slope[h][:, c, :], w_abs[h][:, c, :], minus_prd[:, c:c + 1], a_abs[:, c:c + 1], ALU.mult, ALU.add)
                    ins.then_inc(slope_set[h], 1)
                    dve.wait_ge(slope_set[h], t + 1)
                    v.tensor_tensor(z[h][:, :, :], w_abs[h][:, :, :], slope[h][:, :, :], ALU.mult).then_inc(z_set[h], 1)

        @block.tensor
        def _(pe):
            pe.wait_ge(vectors_set, 1)
            with nc.tensor.Fori(0, ITER) as t:
                for h in range(2):
                    pe.wait_ge(w_set[h], t + 2)
                    pe.wait_ge(abs_set[h], t + 1)
                    for c in range(KF):
                        for j in range(GROUP):
                            ins = nc.tensor.transpose(ps_w[h][:, c, j * P:(j + 1) * P], w[h][:, j, c * P:(c + 1) * P], ident[:, :])
                    ins.then_inc(turned[h], 1)
                for h in range(2):
                    pe.wait_ge(z_set[h], t + 2)
                    pe.wait_ge(score_kept[h], t + 1)
                    for c in range(KF):
                        nc.tensor.matmul(ps_score[h][0:HEADS, 0:GE], head_sum[:, c, :], z[h][:, c, :], start=c == 0, stop=False)
                    for j in range(GROUP):
                        ins = nc.tensor.matmul(ps_score[h][0:HEADS, j * P:(j + 1) * P], w[h][:, j, F:EW], ident[:, :], start=False, stop=j == GROUP - 1)
                    ins.then_inc(summed[h], 1)

        @block.scalar
        def _(act):
            for h in range(2):
                for free in (abs_set, score_free, score_kept):
                    act.sem_inc(free[h], 1)
            with nc.scalar.Fori(0, ITER) as t:
                for h in range(2):
                    act.wait_ge(turned[h], t + 2)
                    act.wait_ge(z_set[h], t + 1)
                    nc.scalar.activation(w_abs[h][:, :, :], ps_w[h][:, :, :], ACT.Abs).then_inc(abs_set[h], 1)
                for h in range(2):
                    act.wait_ge(summed[h], t + 2)
                    act.wait_ge(score_free[h], t + 1)
                    nc.scalar.copy(score[h][:, :], ps_score[h][0:HEADS, 0:GE]).then_inc(score_kept[h], 1)


def softmax_weights(nc, const, scores, merged, carry, weights, from_left):
    with ExitStack() as ctx:
        def sb(name, shape, dt=F32):
            return ctx.enter_context(nc.sbuf_tensor(name, shape, dt))

        def sem(name):
            return ctx.enter_context(nc.semaphore(name))

        keys = sb("keys", [P, PIECE + 2], I32)
        reset = sb("reset", [P, PIECE + 1])
        alpha, from_right = sb("alpha", [P, PIECE]), sb("from_right", [P, PIECE])
        ends = sb("ends", [P, 4])
        pieces = sb("pieces", [HEADS, CHUNKS, 4])
        state = sb("state", [HEADS, CHUNKS, 2])
        carries, carry_p = sb("carries", [HEADS, CHUNKS, 2]), sb("carry_p", [P, 2])
        ps_t = [ctx.enter_context(nc.psum_tensor(f"ps_weight_t{h}", [P, 512], F32)) for h in range(2)]
        keys_in, scores_in = sem("keys_in"), sem("scores_in")
        link_s, ends_set, ends_out, pieces_in = sem("softmax_link"), sem("ends_set"), sem("ends_out"), sem("pieces_in")
        carries_set, carries_out, carry_in = sem("carries_set"), sem("carries_out"), sem("carry_in")
        shifted, exped = sem("shifted"), sem("exped")
        turned, kept = [sem(f"weights_turned{h}") for h in range(2)], [sem(f"weights_kept{h}") for h in range(2)]
        block = ctx.enter_context(nc.Block())

        @block.sync
        def _(sp):
            sp.dma_start(alpha[:, :], scores.rearrange("h (c x) -> (h c) x", c=CHUNKS)).then_inc(scores_in, 16)
            for h in range(HEADS):
                rows = slice(h * CHUNKS, (h + 1) * CHUNKS)
                sp.dma_start(keys[rows, 1:PIECE + 1], merged[1:1 + EP, :].rearrange("(c x) o -> c (x o)", c=CHUNKS)).then_inc(keys_in, 16)
                sp.dma_start(keys[rows, 0:1], merged[0:EP, :].rearrange("(c x) o -> c (x o)", c=CHUNKS)[:, 0:1], allow_slow_non_contiguous=True).then_inc(keys_in, 16)
                sp.dma_start(keys[rows, PIECE + 1:PIECE + 2],
                             merged[2:2 + EP, :].rearrange("(c x) o -> c (x o)", c=CHUNKS)[:, PIECE - 1:PIECE], allow_slow_non_contiguous=True).then_inc(keys_in, 16)
            sp.wait_ge(ends_set, 1)
            sp.dma_start(carry[0:P, :], ends[:, :]).then_inc(ends_out, 16)
            sp.wait_ge(ends_out, 16)
            sp.dma_start(pieces[:, :, :], carry[0:P, :].rearrange("(h c) k -> h c k", c=CHUNKS)).then_inc(pieces_in, 16)
            sp.wait_ge(carries_set, 1)
            sp.dma_start(carry[P:2 * P, 0:2].rearrange("(h c) k -> h c k", c=CHUNKS), carries[:, :, :]).then_inc(carries_out, 16)
            sp.wait_ge(carries_out, 16)
            sp.dma_start(carry_p[:, :], carry[P:2 * P, 0:2]).then_inc(carry_in, 16)

        @block.vector
        def _(dve):
            v = nc.vector
            link = linker(dve, link_s)
            dve.wait_ge(keys_in, 16 * 3 * HEADS)
            link(v.tensor_scalar(keys[:, :], keys[:, :], KEY.bit_length() - 1, None, ALU.logical_shift_right))
            link(v.tensor_tensor(reset[:, :], keys[:, 1:PIECE + 2], keys[:, 0:PIECE + 1], ALU.not_equal))
            link(v.tensor_scalar(reset[:, :], reset[:, :], -BIG, None, ALU.mult))
            dve.wait_ge(scores_in, 16)
            link(v.scalar_tensor_tensor(alpha[:, :], alpha[:, :], 0.2, alpha[:, :], ALU.mult, ALU.max))

            def scans(left, right):
                v.tensor_tensor_scan(from_left[:, :], reset[:, 0:PIECE], alpha[:, :], left, ALU.add, ALU.max)
                link(v.tensor_tensor_scan(from_right[:, ::-1], reset[:, 1:PIECE + 1][:, ::-1], alpha[:, ::-1], right, ALU.add, ALU.max))

            scans(-BIG, -BIG)
            v.tensor_copy(ends[:, 0:1], from_left[:, PIECE - 1:PIECE])
            v.tensor_copy(ends[:, 1:2], from_right[:, 0:1])
            v.tensor_reduce(ends[:, 2:3], reset[:, 0:PIECE], AX.X, ALU.min)
            v.tensor_reduce(ends[:, 3:4], reset[:, 1:PIECE + 1], AX.X, ALU.min).then_inc(ends_set, 1)
            dve.wait_ge(pieces_in, 16)
            v.tensor_tensor_scan(state[:, :, 0], pieces[:, :, 2], pieces[:, :, 0], -BIG, ALU.add, ALU.max)
            v.tensor_tensor_scan(state[:, ::-1, 1], pieces[:, ::-1, 3], pieces[:, ::-1, 1], -BIG, ALU.add, ALU.max)
            link(v.memset(carries[:, :, :], -BIG))
            v.tensor_copy(carries[:, 1:CHUNKS, 0], state[:, 0:CHUNKS - 1, 0])
            v.tensor_copy(carries[:, 0:CHUNKS - 1, 1], state[:, 1:CHUNKS, 1]).then_inc(carries_set, 1)
            dve.wait_ge(carry_in, 16)
            scans(carry_p[:, 0:1], carry_p[:, 1:2])
            link(v.tensor_tensor(from_left[:, :], from_left[:, :], from_right[:, :], ALU.max))
            v.tensor_tensor(alpha[:, :], alpha[:, :], from_left[:, :], ALU.subtract).then_inc(shifted, 1)

        @block.scalar
        def _(act):
            act.wait_ge(shifted, 1)
            nc.scalar.activation(alpha[:, :], alpha[:, :], ACT.Exp).then_inc(exped, 1)
            for i in range(PT):
                act.wait_ge(turned[i % 2], i // 2 + 1)
                nc.scalar.copy(weights[:, :, i, :], ps_t[i % 2][:, 0:P].rearrange("p (h c) -> p c h", h=HEADS)).then_inc(kept[i % 2], 1)

        @block.tensor
        def _(pe):
            pe.wait_ge(exped, 1)
            for i in range(PT):
                if i >= 2:
                    pe.wait_ge(kept[i % 2], i // 2)
                nc.tensor.transpose(ps_t[i % 2][:, 0:P], alpha[:, i * P:(i + 1) * P], const["ident"][:, :]).then_inc(turned[i % 2], 1)


def gather_messages(nc, const, edge, group_block, weights, tab_e, sums, denominators):
    row = const["row"]
    ITER = GROUPS // 2
    with ExitStack() as ctx:
        def sb(name, shape, dt=F32):
            return ctx.enter_context(nc.sbuf_tensor(name, shape, dt))

        def sem(name):
            return ctx.enter_context(nc.semaphore(name))

        def sems(name):
            return [sem(f"{name}{h}") for h in range(2)]

        def sbs(name, shape, dt=F32):
            return [sb(f"{name}{h}", shape, dt) for h in range(2)]

        index = sbs("index_e", [P, GROUP], I32)
        rows, messages = sbs("rows_e", [P, GROUP, F]), sbs("messages", [P, GROUP, F])
        onehot = sbs("node_onehot", [P, GROUP, L])
        ps_sum = [ctx.enter_context(nc.psum_tensor(f"ps_sum{h}", [L, F], F32)) for h in range(2)]
        ps_den = [ctx.enter_context(nc.psum_tensor(f"ps_den{h}", [L, 512], F32)) for h in range(2)]
        index_set, gathered, messages_set, summed, added = (sems(n) for n in ("e_index_set", "e_gathered", "messages_set", "e_summed", "e_added"))
        link_s = sem("gather_link")
        tile_weights = weights[:, :, :, :].rearrange("p c i h -> p (c i) h")
        block = ctx.enter_context(nc.Block())

        @block.gpsimd
        def _(pool):
            with nc.gpsimd.Fori(0, ITER) as t:
                for h in range(2):
                    pool.wait_ge(messages_set[h], t + 1)
                    pool.nop(nofuse=True)
                    nc.gpsimd.tensor_copy(index[h][:, :], edge["dst"][:, DS((2 * t + h) * GROUP, GROUP)]).then_inc(index_set[h], 1)
                    pool.wait_ge(index_set[h], t + 1)
                    pool.nop(nofuse=True)
                    for j in range(GROUP):
                        nc.gpsimd.indirect_dma_start(rows[h][:, j, :], None, tab_e,
                                                     bass.IndirectOffsetOnAxis(ap=index[h][:, j:j + 1], axis=0)).then_inc(gathered[h], 16)

        @block.vector
        def _(dve):
            v = nc.vector
            link = linker(dve, link_s)
            v.memset(denominators[:, :, :], 0.0)
            link(v.memset(sums[:, :, :], 0.0))
            for h in range(2):
                for free in (messages_set, summed, added):
                    dve.sem_inc(free[h], 1)
            with v.Fori(0, ITER) as t:
                for h in range(2):
                    dve.wait_ge(summed[h], t + 1)
                    for j in range(GROUP):
                        v.tensor_scalar(onehot[h][:, j, :], row[:, 0:L], edge["local"][:, DS((2 * t + h) * GROUP + j, 1)], None, ALU.is_equal)
                    dve.wait_ge(gathered[h], t * (16 * GROUP) + 16 * GROUP)
                    w = tile_weights[:, DS((2 * t + h) * GROUP, GROUP), :].rearrange("p j h -> p (j h)")
                    v.tensor_tensor(messages[h][:, :, :].rearrange("p j (h d) -> p (j h) d", d=D),
                                    rows[h][:, :, :].rearrange("p j (h d) -> p (j h) d", d=D),
                                    w.unsqueeze(2).broadcast_to([P, GROUP * HEADS, D]), ALU.mult).then_inc(messages_set[h], 1)
                for h in range(2):
                    b = dve.value_load(group_block[0:1, DS(2 * t + h, 1)], min_val=0, max_val=NB - 1)
                    dve.wait_ge(summed[h], t + 2)
                    dve.wait_ge(added[1 - h], t + 1 + h)
                    total = sums[:, DS(b, 1), :].rearrange("p o f -> p (o f)")
                    v.tensor_tensor(total, ps_sum[h][:, :], total, ALU.add)
                    den = denominators[:, DS(b, 1), :].rearrange("p o h -> p (o h)")
                    v.tensor_tensor(den, ps_den[h][:, 0:HEADS], den, ALU.add).then_inc(added[h], 1)

        @block.tensor
        def _(pe):
            with nc.tensor.Fori(0, ITER) as t:
                for h in range(2):
                    pe.wait_ge(messages_set[h], t + 2)
                    pe.wait_ge(added[h], t + 1)
                    for j in range(GROUP):
                        nc.tensor.matmul(ps_sum[h][:, :], onehot[h][:, j, :], messages[h][:, j, :], start=j == 0, stop=j == GROUP - 1)
                        ins = nc.tensor.matmul(ps_den[h][:, 0:HEADS], onehot[h][:, j, :],
                                               tile_weights[:, DS((2 * t + h) * GROUP + j, 1), :].rearrange("p o h -> p (o h)"),
                                               start=j == 0, stop=j == GROUP - 1)
                    ins.then_inc(summed[h], 1)


def transpose_ffn_weights(nc, a, const, ffn):
    ident = const["ident"]
    IH = INNER // P
    with ExitStack() as ctx:
        def sem(name):
            return ctx.enter_context(nc.semaphore(name))

        up = [ctx.enter_context(nc.sbuf_tensor(f"up_rows{i}", [P, IH, F], F32)) for i in range(2)]
        down = ctx.enter_context(nc.sbuf_tensor("down_rows", [P, KF, INNER], F32))
        ps_w = [ctx.enter_context(nc.psum_tensor(f"ps_weight{i}", [P, 512], F32)) for i in range(6)]
        loaded, turned, kept, freed = sem("ffn_loaded"), sem("ffn_turned"), sem("ffn_kept"), sem("ffn_freed")
        ROUNDS = EXPERTS + 1
        block = ctx.enter_context(nc.Block())

        @block.sync
        def _(sp):
            with nc.sync.Fori(0, EXPERTS) as e:
                sp.wait_ge(freed, e + 1)
                for rows, name in ((up[0], "L0_ffn_w1"), (up[1], "L0_ffn_w3")):
                    sp.dma_start(rows[:, :, :], a[name][DS(e, 1), :, :].rearrange("o (i p) f -> p (o i) f", p=P)).then_inc(loaded, 16)
                sp.dma_start(down[:, :, :], a["L0_ffn_w2"][DS(e, 1), :, :].rearrange("o (k p) i -> p (o k) i", p=P)).then_inc(loaded, 16)
            sp.wait_ge(freed, EXPERTS + 1)
            sp.dma_start(up[0][:, :, :], a["L0_ffn_sw1"].rearrange("(i p) f -> p i f", p=P)).then_inc(loaded, 16)
            sp.dma_start(up[1][0:EXPERTS, 0, :], a["L0_ffn_gate_w"]).then_inc(loaded, 16)
            sp.dma_start(down[:, :, :], a["L0_ffn_sw2"].rearrange("(k p) i -> p k i", p=P)).then_inc(loaded, 16)

        def turn(pe, both):
            banks = iter(ps_w)
            for i in range(2 if both else 1):
                for half in range(IH):
                    bank = next(banks)
                    for k in range(KF):
                        nc.tensor.transpose(bank[:, k * P:(k + 1) * P], up[i][:, half, k * P:(k + 1) * P], ident[:, :])
            for half in range(IH):
                bank = next(banks)
                for k in range(KF):
                    ins = nc.tensor.transpose(bank[:, k * P:(k + 1) * P], down[:, k, half * P:(half + 1) * P], ident[:, :])
            return ins

        @block.tensor
        def _(pe):
            pe.sem_inc(freed, 1)
            pe.sem_inc(turned, 1)
            with nc.tensor.Fori(0, EXPERTS) as e:
                pe.wait_ge(loaded, e * 48 + 48)
                pe.wait_ge(kept, e + 1)
                turn(pe, True).then_inc(turned, 1)
                pe.wait_ge(turned, e + 2)
                pe.sem_inc(freed, 1)
            pe.wait_ge(loaded, ROUNDS * 48)
            pe.wait_ge(kept, EXPERTS + 1)
            for k in range(KF):
                nc.tensor.transpose(ps_w[5][:, k * EXPERTS:(k + 1) * EXPERTS], up[1][0:EXPERTS, 0, k * P:(k + 1) * P], ident[0:EXPERTS, 0:EXPERTS])
            turn(pe, False).then_inc(turned, 1)

        @block.scalar
        def _(act):
            act.sem_inc(kept, 1)
            sc = nc.scalar
            with sc.Fori(0, EXPERTS) as e:
                act.wait_ge(turned, e + 2)
                for i in range(2):
                    for half in range(IH):
                        at = i * INNER + half * P
                        sc.copy(ffn["up"][:, :, DS(e, 1), at:at + P].rearrange("p k o n -> p k (o n)"),
                                ps_w[i * IH + half][:, :].rearrange("p (k n) -> p k n", k=KF))
                for half in range(IH):
                    ins = sc.activation(ffn["down"][:, DS(e, 1), half, :].rearrange("p o f -> p (o f)"), ps_w[2 * IH + half][:, :], ACT.Copy, scale=0.5)
                ins.then_inc(kept, 1)
            act.wait_ge(turned, ROUNDS + 1)
            for half in range(IH):
                sc.copy(ffn["shared_up"][:, :, half * P:(half + 1) * P], ps_w[half][:, :].rearrange("p (k n) -> p k n", k=KF))
                sc.copy(ffn["shared_down"][:, half, :], ps_w[IH + half][:, :])
            sc.copy(ffn["gate"][:, :, :], ps_w[5][:, 0:KF * EXPERTS].rearrange("p (k e) -> p k e", k=KF))


def route_tokens(nc, const, ffn, x_sb, sums, denominators, tokens, tab_x, lists):
    ident, tri, ones, row, eps = (const[k] for k in ("ident", "tri", "ones", "row", "eps"))
    xn2 = sums
    with ExitStack() as ctx:
        def sb(name, shape, dt=F32):
            return ctx.enter_context(nc.sbuf_tensor(name, shape, dt))

        def ps(name, shape):
            return ctx.enter_context(nc.psum_tensor(name, shape, F32))

        def sem(name):
            return ctx.enter_context(nc.semaphore(name))

        inverse = sb("inverse", [L, NB * HEADS])
        stats, moments = sb("stats2", [L, NB, 6]), sb("moments2", [L, NB, 2])
        deviation, rstd = sb("deviation2", [L, NB]), sb("rstd2", [L, NB])
        staged = sb("xn2_tile", [L, F])
        xn2_t = sb("xn2_t", [P, KF, L])
        logits = sb("logits", [L, NB, EXPERTS])
        best, chosen = sb("best_logit", [L, NB]), sb("chosen", [L, NB])
        is_best, candidate = sb("is_best", [L, NB, EXPERTS]), sb("candidate", [L, NB, EXPERTS])
        far = sb("far_iota", [L, EXPERTS])
        routed, running, ahead = sb("routed", [L, NB, EXPERTS]), sb("running", [L, NB, EXPERTS]), sb("ahead_tiles", [L, NB, EXPERTS])
        zeros = sb("zeros_nb", [L, NB])
        tiles_i, tiles_f = sb("tiles_i", [L, EXPERTS], I32), sb("tiles_f", [L, EXPERTS])
        tile_end, tile_start = sb("tile_end", [L, EXPERTS]), sb("tile_start", [L, EXPERTS])
        slot_f = sb("token_slot_f", [L, NB])
        tile_cmp, tile_sum = sb("tile_cmp", [1, TOKEN_TILES, EXPERTS]), sb("tile_sum", [1, TOKEN_TILES])
        tile_iota = sb("tile_iota", [1, TOKEN_TILES])
        fill = sb("token_fill", [P, TOKEN_TILES], I32)
        ids = sb("token_ids", [L, NB], I32)
        listed = sb("listed", [TOKEN_TILES, RECS, P], I32)
        listed_f = sb("listed_f", [TOKEN_TILES, P])
        ps_t, ps_logit, ps_slot, ps_total, ps_ids = ps("ps_t2", [P, 512]), ps("ps_logit", [L, 512]), ps("ps_tslot", [L, 512]), ps("ps_ttotal", [L, 512]), ps("ps_ids", [P, 512])
        names = ("link var dev xn2_set xn2_out staged_set turned kept logit_done logit_kept prefix_set counted slots_set "
                 "filled fill_out listed_in listed_set ids_turned iotas").split()
        s = {n: sem(f"route_{n}") for n in names}
        written = [sem(f"ids_written{j}") for j in range(RECS)]
        scattered = sem("ids_scattered")
        block = ctx.enter_context(nc.Block())

        @block.sync
        def _(sp):
            sp.wait_ge(s["filled"], 1)
            for one in lists:
                sp.dma_start(one.rearrange("(p c) o -> p (c o)", c=TOKEN_TILES), fill[:, :]).then_inc(s["fill_out"], 16)
            sp.wait_ge(s["xn2_set"], 1)
            sp.dma_start(tab_x.rearrange("(t p) f -> p t f", p=L), xn2[:, :, :]).then_inc(s["xn2_out"], 16)
            sp.wait_ge(scattered, 1)
            for j, one in enumerate(lists):
                sp.dma_start(listed[:, j, :], one.rearrange("(c p) o -> c (p o)", p=P)).then_inc(s["listed_in"], 16)
            sp.wait_ge(s["xn2_out"], 16)

        @block.gpsimd
        def _(pool):
            nc.gpsimd.memset(fill[:, :], PAD_RECORD).then_inc(s["filled"], 1)
            nc.gpsimd.iota(ids[:, :], pattern=[[L, NB]], base=0, channel_multiplier=1)
            nc.gpsimd.iota(tile_iota[:, :], pattern=[[1, TOKEN_TILES]], base=0, channel_multiplier=0, allow_small_or_imprecise_dtypes=True).then_inc(s["iotas"], 1)
            pool.wait_ge(s["iotas"], 1)
            pool.wait_ge(s["fill_out"], 16 * RECS)
            pool.wait_ge(s["slots_set"], 1)
            for t in range(NB):
                j = t % RECS
                if t >= RECS:
                    pool.wait_ge(written[j], 16 * (t // RECS))
                nc.gpsimd.indirect_dma_start(lists[j], bass.IndirectOffsetOnAxis(ap=tokens["slot"][:, t:t + 1], axis=0),
                                             ids[:, t:t + 1], None).then_inc(written[j], 16)
            for j in range(RECS):
                pool.wait_ge(written[j], 16 * (NB // RECS))
            pool.sem_inc(scattered, 1)

        @block.vector
        def _(dve):
            v = nc.vector
            link = linker(dve, s["link"])
            for n in ("turned", "logit_kept"):
                dve.sem_inc(s[n], 1)
            den = denominators[:, :, :].rearrange("p b h -> p (b h)")
            link(v.tensor_scalar(inverse[:, :], den, 1e-16, None, ALU.add))
            link(v.reciprocal(inverse[:, :], inverse[:, :]))
            by_head = sums[:, :, :].rearrange("p b (h d) -> p (b h) d", d=D)
            link(v.tensor_tensor(by_head, by_head, inverse[:, :].unsqueeze(2).broadcast_to([L, NB * HEADS, D]), ALU.mult))
            link(v.tensor_tensor(x_sb[:, :, :], x_sb[:, :, :], sums[:, :, :], ALU.add))
            for t in range(NB):
                ins = v.bn_stats(stats[:, t, :], x_sb[:, t, :])
            link(ins)
            for t in range(NB):
                ins = v.bn_aggr(moments[:, t, :], stats[:, t, :])
            ins.then_inc(s["var"], 1)
            dve.wait_ge(s["dev"], 1)
            link(v.reciprocal(rstd[:, :], deviation[:, :]))
            for t in range(NB):
                ins = v.tensor_scalar(xn2[:, t, :], x_sb[:, t, :], moments[:, t, 0:1], rstd[:, t:t + 1], ALU.subtract, ALU.mult)
            link(ins)
            dve.sem_inc(s["xn2_set"], 1)
            with v.Fori(0, NB) as t:
                dve.wait_ge(s["turned"], t + 1)
                v.tensor_copy(staged[:, :], xn2[:, DS(t, 1), :].rearrange("p o f -> p (o f)")).then_inc(s["staged_set"], 1)
                dve.wait_ge(s["logit_done"], t + 1)
                v.tensor_copy(logits[:, DS(t, 1), :].rearrange("p o e -> p (o e)"), ps_logit[:, 0:EXPERTS]).then_inc(s["logit_kept"], 1)
            dve.wait_ge(s["logit_kept"], NB + 1)
            shape = [L, NB, EXPERTS]
            iota = row[0:L, 0:EXPERTS].unsqueeze(1).broadcast_to(shape)
            link(v.tensor_reduce(best[:, :], logits[:, :, :], AX.X, ALU.max))
            link(v.tensor_tensor(is_best[:, :, :], logits[:, :, :], best[:, :].unsqueeze(2).broadcast_to(shape), ALU.is_equal))
            link(v.tensor_scalar(far[:, :], row[0:L, 0:EXPERTS], float(EXPERTS), None, ALU.add))
            link(v.tensor_scalar(is_best[:, :, :], is_best[:, :, :], -float(EXPERTS), None, ALU.mult))
            link(v.tensor_tensor(candidate[:, :, :], is_best[:, :, :], far[:, :].unsqueeze(1).broadcast_to(shape), ALU.add))
            link(v.tensor_reduce(chosen[:, :], candidate[:, :, :], AX.X, ALU.min))
            link(v.tensor_tensor(routed[:, :, :], iota, chosen[:, :].unsqueeze(2).broadcast_to(shape), ALU.is_equal))
            link(v.memset(zeros[:, :], 0.0))
            for e in range(EXPERTS):
                ins = v.tensor_tensor_scan(running[:, :, e], routed[:, :, e], zeros[:, :], 0.0, ALU.add, ALU.add)
            link(ins)
            v.tensor_tensor(ahead[:, :, :], running[:, :, :], routed[:, :, :], ALU.subtract).then_inc(s["prefix_set"], 1)
            dve.wait_ge(s["counted"], 1)
            link(v.tensor_scalar(tiles_i[:, :], ps_total[:, 0:EXPERTS], float(P - 1), None, ALU.add))
            link(v.tensor_scalar(tiles_i[:, :], tiles_i[:, :], P.bit_length() - 1, None, ALU.logical_shift_right))
            link(v.tensor_copy(tiles_f[:, :], tiles_i[:, :]))
            link(v.tensor_tensor_scan(tile_end[:, :], tiles_f[:, :], zeros[:, 0:EXPERTS], 0.0, ALU.add, ALU.add))
            link(v.tensor_tensor(tile_start[:, :], tile_end[:, :], tiles_f[:, :], ALU.subtract))
            dve.wait_ge(s["iotas"], 1)
            link(v.tensor_tensor(tile_cmp[:, :, :], tile_iota[:, :].unsqueeze(2).broadcast_to([1, TOKEN_TILES, EXPERTS]),
                                 tile_start[0:1, :].unsqueeze(1).broadcast_to([1, TOKEN_TILES, EXPERTS]), ALU.is_ge))
            link(v.tensor_reduce(tile_sum[:, :], tile_cmp[:, :, 1:EXPERTS], AX.X, ALU.add))
            v.tensor_copy(tokens["expert"][:, :], tile_sum[:, :])
            link(v.tensor_scalar(tile_start[:, :], tile_start[:, :], float(P), None, ALU.mult))
            link(v.tensor_tensor(candidate[:, :, :], ps_slot[:, 0:NB * EXPERTS].rearrange("p (t e) -> p t e", e=EXPERTS),
                                 tile_start[:, :].unsqueeze(1).broadcast_to(shape), ALU.add))
            link(v.tensor_tensor(candidate[:, :, :], candidate[:, :, :], routed[:, :, :], ALU.mult))
            link(v.tensor_reduce(slot_f[:, :], candidate[:, :, :], AX.X, ALU.add))
            v.tensor_copy(tokens["slot"][:, :], slot_f[:, :]).then_inc(s["slots_set"], 1)
            dve.wait_ge(s["listed_in"], 16 * RECS)
            link(v.tensor_tensor(listed_f[:, :], listed[:, 0, :], listed[:, 1, :], ALU.min))
            for j in range(2, RECS):
                link(v.tensor_tensor(listed_f[:, :], listed_f[:, :], listed[:, j, :], ALU.min))
            v.tensor_scalar(listed_f[:, :], listed_f[:, :], float(N - 1), None, ALU.min).then_inc(s["listed_set"], 1)
            dve.wait_ge(s["ids_turned"], 1)
            v.tensor_copy(tokens["id"][:, :], ps_ids[:, 0:TOKEN_TILES])

        @block.tensor
        def _(pe):
            with nc.tensor.Fori(0, NB) as t:
                pe.wait_ge(s["staged_set"], t + 1)
                pe.wait_ge(s["kept"], t + 1)
                for k in range(KF):
                    ins = nc.tensor.transpose(ps_t[:, k * L:(k + 1) * L], staged[:, k * P:(k + 1) * P], ident[0:L, 0:L])
                ins.then_inc(s["turned"], 1)
                pe.wait_ge(s["kept"], t + 2)
                pe.wait_ge(s["logit_kept"], t + 1)
                for k in range(KF):
                    ins = nc.tensor.matmul(ps_logit[:, 0:EXPERTS], xn2_t[:, k, :], ffn["gate"][:, k, :], start=k == 0, stop=k == KF - 1)
                ins.then_inc(s["logit_done"], 1)
            pe.wait_ge(s["prefix_set"], 1)
            cols = NB * EXPERTS
            nc.tensor.matmul(ps_slot[:, 0:cols], tri[0:L, 0:L], routed[:, :, :].rearrange("p t e -> p (t e)"), start=True, stop=False)
            nc.tensor.matmul(ps_slot[:, 0:cols], ones[0:L, 0:L], ahead[:, :, :].rearrange("p t e -> p (t e)"), start=False, stop=True)
            nc.tensor.matmul(ps_total[:, 0:EXPERTS], ones[0:L, 0:L], running[:, NB - 1, :], start=True, stop=True).then_inc(s["counted"], 1)
            pe.wait_ge(s["listed_set"], 1)
            nc.tensor.transpose(ps_ids[:, 0:TOKEN_TILES], listed_f[:, :], ident[0:TOKEN_TILES, 0:TOKEN_TILES]).then_inc(s["ids_turned"], 1)

        @block.scalar
        def _(act):
            act.sem_inc(s["kept"], 1)
            act.wait_ge(s["var"], 1)
            nc.scalar.activation(deviation[:, :], moments[:, :, 1], ACT.Sqrt, bias=eps[0:L, 0:1]).then_inc(s["dev"], 1)
            with nc.scalar.Fori(0, NB) as t:
                act.wait_ge(s["turned"], t + 2)
                nc.scalar.copy(xn2_t[:, :, :], ps_t[:, 0:KF * L].rearrange("p (k n) -> p k n", k=KF)).then_inc(s["kept"], 1)


def run_experts(nc, const, ffn, tokens, tab_x, tab_y):
    ident = const["ident"]
    with ExitStack() as ctx:
        def sb(name, shape, dt=F32):
            return ctx.enter_context(nc.sbuf_tensor(name, shape, dt))

        def ps(name):
            return ctx.enter_context(nc.psum_tensor(name, [P, F], F32))

        def sem(name):
            return ctx.enter_context(nc.semaphore(name))

        index, rows = sb("token_index", [P, 1], I32), sb("token_rows", [P, F])
        x_t, hidden_t = sb("token_x_t", [P, KF, P]), sb("hidden_t", [P, KF, P])
        gate = sb("swiglu_gate", [P, INNER])
        hidden, y = sb("hidden", [P, F]), sb("token_y", [P, F])
        ps_t, ps_up, ps_shared, ps_h, ps_y = ps("ps_tx"), ps("ps_up"), ps("ps_shared"), ps("ps_hidden"), ps("ps_y")
        names = "index_set gathered turned kept up_done act_set gated gelu_set hidden_set h_turned h_kept y_done y_kept y_free y_out".split()
        s = {n: sem(f"expert_{n}") for n in names}
        block = ctx.enter_context(nc.Block())

        @block.sync
        def _(sp):
            with nc.sync.Fori(0, TOKEN_TILES) as t:
                sp.wait_ge(s["y_kept"], t + 2)
                sp.dma_start(tab_y[DS(t * P, P), :], y[:, :]).then_inc(s["y_out"], 16)
                sp.wait_ge(s["y_out"], t * 16 + 16)
                sp.sem_inc(s["y_free"], 1)

        @block.gpsimd
        def _(pool):
            with nc.gpsimd.Fori(0, TOKEN_TILES) as t:
                pool.wait_ge(s["turned"], t + 1)
                pool.nop(nofuse=True)
                nc.gpsimd.tensor_copy(index[:, :], tokens["id"][:, DS(t, 1)]).then_inc(s["index_set"], 1)
                pool.wait_ge(s["index_set"], t + 1)
                pool.nop(nofuse=True)
                nc.gpsimd.indirect_dma_start(rows[:, :], None, tab_x, bass.IndirectOffsetOnAxis(ap=index[:, 0:1], axis=0)).then_inc(s["gathered"], 16)

        @block.vector
        def _(dve):
            v = nc.vector
            for n in ("turned", "h_turned", "hidden_set"):
                dve.sem_inc(s[n], 1)
            with v.Fori(0, TOKEN_TILES) as t:
                dve.wait_ge(s["act_set"], t + 1)
                v.scalar_tensor_tensor(gate[:, :], gate[:, :], 1.0, ps_up[:, 0:INNER], ALU.add, ALU.mult).then_inc(s["gated"], 1)
                dve.wait_ge(s["gated"], t + 1)
                dve.wait_ge(s["h_turned"], t + 1)
                v.tensor_tensor(hidden[:, 0:INNER], ps_up[:, INNER:2 * INNER], gate[:, :], ALU.mult).then_inc(s["hidden_set"], 1)

        @block.tensor
        def _(pe):
            with nc.tensor.Fori(0, TOKEN_TILES) as t:
                e = pe.value_load(tokens["expert"][0:1, DS(t, 1)], min_val=0, max_val=EXPERTS - 1)
                pe.wait_ge(s["gathered"], t * 16 + 16)
                pe.wait_ge(s["kept"], t + 1)
                for k in range(KF):
                    ins = nc.tensor.transpose(ps_t[:, k * P:(k + 1) * P], rows[:, k * P:(k + 1) * P], ident[:, :])
                ins.then_inc(s["turned"], 1)
                pe.wait_ge(s["kept"], t + 2)
                pe.wait_ge(s["hidden_set"], t + 1)
                for k in range(KF):
                    nc.tensor.matmul(ps_up[:, :], x_t[:, k, :], ffn["up"][:, k, DS(e, 1), :].rearrange("p o n -> p (o n)"), start=k == 0, stop=k == KF - 1)
                for k in range(KF):
                    ins = nc.tensor.matmul(ps_shared[:, 0:INNER], x_t[:, k, :], ffn["shared_up"][:, k, :], start=k == 0, stop=k == KF - 1)
                ins.then_inc(s["up_done"], 1)
                pe.wait_ge(s["hidden_set"], t + 2)
                pe.wait_ge(s["gelu_set"], t + 1)
                pe.wait_ge(s["h_kept"], t + 1)
                for k in range(KF):
                    ins = nc.tensor.transpose(ps_h[:, k * P:(k + 1) * P], hidden[:, k * P:(k + 1) * P], ident[:, :])
                ins.then_inc(s["h_turned"], 1)
                pe.wait_ge(s["h_kept"], t + 2)
                pe.wait_ge(s["y_kept"], t + 1)
                for half in range(INNER // P):
                    nc.tensor.matmul(ps_y[:, :], hidden_t[:, half, :], ffn["down"][:, DS(e, 1), half, :].rearrange("p o f -> p (o f)"), start=half == 0, stop=False)
                for half in range(INNER // P):
                    ins = nc.tensor.matmul(ps_y[:, :], hidden_t[:, INNER // P + half, :], ffn["shared_down"][:, half, :], start=False, stop=half == INNER // P - 1)
                ins.then_inc(s["y_done"], 1)

        @block.scalar
        def _(act):
            sc = nc.scalar
            for n in ("kept", "h_kept", "y_kept", "y_free"):
                act.sem_inc(s[n], 1)
            with sc.Fori(0, TOKEN_TILES) as t:
                act.wait_ge(s["turned"], t + 2)
                sc.copy(x_t[:, :, :].rearrange("p k n -> p (k n)"), ps_t[:, :]).then_inc(s["kept"], 1)
                act.wait_ge(s["up_done"], t + 1)
                act.wait_ge(s["hidden_set"], t + 1)
                sc.activation(gate[:, :], ps_up[:, 0:INNER], ACT.Tanh, scale=0.5).then_inc(s["act_set"], 1)
                act.wait_ge(s["h_turned"], t + 1)
                sc.activation(hidden[:, INNER:2 * INNER], ps_shared[:, 0:INNER], ACT.Gelu).then_inc(s["gelu_set"], 1)
                act.wait_ge(s["h_turned"], t + 2)
                sc.copy(hidden_t[:, :, :].rearrange("p k n -> p (k n)"), ps_h[:, :]).then_inc(s["h_kept"], 1)
                act.wait_ge(s["y_done"], t + 1)
                act.wait_ge(s["y_free"], t + 1)
                sc.copy(y[:, :], ps_y[:, :]).then_inc(s["y_kept"], 1)


def write_result(nc, tokens, x_sb, tab_y, out):
    BUFFERS = 4
    with ExitStack() as ctx:
        back = [ctx.enter_context(nc.sbuf_tensor(f"back{i}", [L, F], F32)) for i in range(BUFFERS)]
        gathered = [ctx.enter_context(nc.semaphore(f"y_gathered{i}")) for i in range(BUFFERS)]
        added, stored = ctx.enter_context(nc.semaphore("y_added")), ctx.enter_context(nc.semaphore("stored"))
        block = ctx.enter_context(nc.Block())

        @block.gpsimd
        def _(pool):
            for t in range(NB):
                if t >= BUFFERS:
                    pool.wait_ge(added, t - BUFFERS + 1)
                nc.gpsimd.indirect_dma_start(back[t % BUFFERS][:, :], None, tab_y,
                                             bass.IndirectOffsetOnAxis(ap=tokens["slot"][:, t:t + 1], axis=0)).then_inc(gathered[t % BUFFERS], 16)

        @block.vector
        def _(dve):
            for t in range(NB):
                dve.wait_ge(gathered[t % BUFFERS], 16 * (t // BUFFERS + 1))
                nc.vector.tensor_add(x_sb[:, t, :], x_sb[:, t, :], back[t % BUFFERS][:, :]).then_inc(added, 1)

        @block.sync
        def _(sp):
            PER = 4
            for t in range(0, NB, PER):
                sp.wait_ge(added, t + PER)
                sp.dma_start(out[t * L:(t + PER) * L, :].rearrange("(t p) f -> p t f", p=L), x_sb[:, t:t + PER, :]).then_inc(stored, 16)
            sp.wait_ge(stored, 16 * (NB // PER))

def program(nc, a, out):
    def dram(name, shape, dt=F32):
        return nc.dram_tensor(name, shape, dt, kind="Internal").ap()

    recs = [dram(f"records{j}", [REC_ROWS, 1], I32) for j in range(RECS)]
    merged = dram("sorted_records", [EP + 2, 1], I32)
    tab_v, tab_u, tab_e = dram("target_rows", [N, EW]), dram("source_rows", [N, EW]), dram("message_rows", [N, F])
    tab_x, tab_y = dram("token_rows_in", [N, F]), dram("token_rows_out", [TOK_ROWS, F])
    token_lists = [dram(f"token_list{j}", [TOK_ROWS, 1], I32) for j in range(RECS)]
    scores, carry = dram("scores", [HEADS, EP]), dram("carry", [2 * P, 4])
    with ExitStack() as ctx:
        def sb(name, shape, dt=F32):
            return ctx.enter_context(nc.sbuf_tensor(name, shape, dt))

        def sem(name):
            return ctx.enter_context(nc.semaphore(name))

        const = make_constants(nc, sb)
        keep = {"key": sb("key", [L, ET], I32), "slot": sb("slot", [L, ET], I32), "group_block": sb("group_block", [1, GROUPS], I32)}
        sort_edges(nc, a["src"], a["dst"], recs, const, keep)
        x_sb = sb("x_sb", [L, NB, F])
        project_and_mix(nc, a, const, keep, x_sb, recs, tab_v, tab_u, tab_e)
        sums_space, denominators = sb("sums", [P, NB * F]), sb("denominators", [L, NB, HEADS])
        sums = sums_space[0:L, :].rearrange("p (b f) -> p b f", b=NB)
        edge_ctx = ExitStack()

        def sb_edge(name, shape, dt=F32):
            return edge_ctx.enter_context(nc.sbuf_tensor(name, shape, dt))

        edge = {"dst": sb_edge("edge_dst", [P, ST], I32), "src": sb_edge("edge_src", [P, ST], I32), "local": sb_edge("edge_local", [P, ST])}
        read_sorted_edges(nc, const, recs, merged, edge)
        score_edges(nc, a, const, edge, tab_v, tab_u, scores)
        weights = sb_edge("weights", [P, CHUNKS, PT, HEADS])
        softmax_weights(nc, const, scores, merged, carry, weights, sums_space[:, 0:PIECE])
        gather_messages(nc, const, edge, keep["group_block"], weights, tab_e, sums, denominators)
        edge_ctx.close()
        ffn = {"up": sb("up_t", [P, KF, EXPERTS, 2 * INNER]), "down": sb("down_t", [P, EXPERTS, INNER // P, F]),
               "shared_up": sb("shared_up_t", [P, KF, INNER]), "shared_down": sb("shared_down_t", [P, INNER // P, F]),
               "gate": sb("gate_t", [P, KF, EXPERTS])}
        tokens = {"slot": sb("token_slot", [L, NB], I32), "expert": sb("token_expert", [1, TOKEN_TILES], I32), "id": sb("token_id", [P, TOKEN_TILES], I32)}
        transpose_ffn_weights(nc, a, const, ffn)
        route_tokens(nc, const, ffn, x_sb, sums, denominators, tokens, tab_x, token_lists)
        run_experts(nc, const, ffn, tokens, tab_x, tab_y)
        write_result(nc, tokens, x_sb, tab_y, out)

_INS = ['x', 'src', 'dst', 'L0_gnn_W_e', 'L0_gnn_W_r', 'L0_gnn_a', 'L0_mix_W_in', 'L0_mix_b_in', 'L0_mix_Wq',
        'L0_mix_Wk', 'L0_mix_Wv', 'L0_mix_W_out', 'L0_mix_b_out', 'L0_ffn_gate_w', 'L0_ffn_w1', 'L0_ffn_w2',
        'L0_ffn_w3', 'L0_ffn_sw1', 'L0_ffn_sw2']


def kernel(**inputs):
    import numpy as _np
    import concourse.bacc as _bacc
    from concourse import mybir as _mybir
    from concourse.bass_utils import run_bass_kernel_spmd as _run

    nc = _bacc.Bacc("TRN2", target_bir_lowering=False, num_devices=1)
    arrays, args = {}, {}
    for name in _INS:
        a = _np.ascontiguousarray(inputs[name])
        arrays[f"in_{name}_dram"] = a
        args[name] = nc.dram_tensor(f"in_{name}_dram", a.shape, _mybir.dt.from_np(a.dtype), kind="ExternalInput").ap()
    out = nc.dram_tensor("out_0_dram", (2500, 512), _mybir.dt.float32, kind="ExternalOutput").ap()
    program(nc, args, out)
    r = _run(nc, [arrays], core_ids=[0])
    return r.results[0]["out_0_dram"]
```

```python
import concourse.bass as bass
from concourse import mybir
from contextlib import ExitStack

F32 = mybir.dt.float32
BF16 = mybir.dt.bfloat16
I32 = mybir.dt.int32
ALU = mybir.AluOpType
ACT = mybir.ActivationFunctionType
AX = mybir.AxisListType
DS = bass.ds

N, E, F, HEADS, D = 2500, 80000, 512, 8, 64
SLICE, EXPERTS, INNER = 32, 8, 256
P = 128
L = 125
NB = N // L
KF = F // P
ET = E // L
BUFS = 4
CH = 4
GROUP = 2
GE = GROUP * P
CHUNKS = P // HEADS
MAX_GROUPS = (E + NB * (GE - 1)) // GE
PIECE_GROUPS = -(-MAX_GROUPS // CHUNKS)
GROUPS = PIECE_GROUPS * CHUNKS
ST = GROUPS * GROUP
EP = ST * P
PIECE = EP // CHUNKS
PT = PIECE // P
REC_COLS = -(-(EP + 2) // P)
REC_ROWS = REC_COLS * P
KEY = 4096
PAD_RECORD = (KEY - 1) * KEY
ROUND = 12582912.0
TOKEN_TILES = (N + EXPERTS * (P - 1)) // P
TOK_ROWS = TOKEN_TILES * P
R = D // KF
EW = F + HEADS
MIDDLE = float(EP // 2 // 256 * 256)
RECS = 4
SCATTERS = ET // RECS // 2
SORT_SCATTERS = SCATTERS * 2 // 5
BIG = 1e38


def linker(eng, sem, base=0):
    count = [0]

    def link(ins):
        count[0] += 1
        ins.then_inc(sem, 1)
        eng.wait_ge(sem, base + count[0])
    link.count = count
    return link


def in_turns(eng, turns, steps):
    for q in range(BUFS):
        for behind, step in steps:
            if q >= behind:
                step(q - behind, (q - behind) % BUFS)
    with eng.Fori(1, turns) as t:
        for q in range(BUFS):
            for behind, step in steps:
                step(t * BUFS + (q - behind), (q - behind) % BUFS)
    last = max(behind for behind, _ in steps)
    for q in range(last):
        for behind, step in steps:
            if q < behind:
                step(turns * BUFS + q - behind, (q - behind) % BUFS)


def make_constants(nc, sb):
    c = {
        "row": sb("iota_row", [P, P], F32), "col": sb("iota_col", [P, 1], F32),
        "rowb": sb("iota_row_bf", [P, P], BF16),
        "ident": sb("ident", [P, P], F32), "identb": sb("ident_bf", [P, P], BF16),
        "tri": sb("tri", [P, P], F32), "ones": sb("ones", [P, P], F32),
        "eps": sb("eps", [P, 1], F32),
    }
    return c


def clear_semaphores(nc, sems):
    with nc.Block() as block:
        @block.gpsimd
        def _(pool):
            first, last = sems[0].num, sems[-1].num
            assert [one.num for one in sems] == list(range(first, last + 1))
            pool.sem_clear(range(first, last + 1))


def sort_edges(nc, src, dst, recs, written, const, keep):
    ident, identb, tri, ones, row, rowb, col = (const[k] for k in ("ident", "identb", "tri", "ones", "row", "rowb", "col"))
    with ExitStack() as ctx:
        def sb(name, shape, dt):
            return ctx.enter_context(nc.sbuf_tensor(name, shape, dt))

        def ps(name, shape, dt=F32):
            return ctx.enter_context(nc.psum_tensor(name, shape, dt))

        sems = []

        def sem(name):
            sems.append(ctx.enter_context(nc.semaphore(name)))
            return sems[-1]

        src_i, dst_i = sb("src_i", [L, ET], I32), sb("dst_i", [L, ET], I32)
        fill = sb("fill", [P, REC_COLS], I32)
        blockf, localf = sb("blockf", [L, ET], F32), sb("localf", [L, ET], F32)
        scaled = sb("scaled", [L, ET], F32)
        onehot_block = sb("onehot_block", [L, ET, 2 * NB], BF16)
        before = sb("before", [L, NB, ET + 1], F32)
        firstp = sb("firstp", [L, ET, 2 * NB], BF16)
        zeros = sb("zeros", [L, ET], F32)
        quotient = [sb(f"quotient{h}", [L, ET], F32) for h in range(2)]
        onehot = [sb(f"onehot{h}", [L, CH, L], BF16) for h in range(BUFS)]
        onehot_t = [sb(f"onehot_t{h}", [L, CH, L], BF16) for h in range(BUFS)]
        ahead = [sb(f"ahead{h}", [L, CH, L], BF16) for h in range(2)]
        weighted = [sb(f"weighted{h}", [L, CH, 2 * NB], F32) for h in range(2)]
        slotf = [sb(f"slotf{h}", [L, CH], F32) for h in range(2)]
        totals = sb("totals", [L, NB], F32)
        groups_f, groups_i = sb("groups_f", [P, NB], F32), sb("groups_i", [P, NB], I32)
        group_end, group_start = sb("group_end", [P, NB], F32), sb("group_start", [P, NB], F32)
        base = sb("base", [L, NB], F32)
        giota = sb("giota", [1, GROUPS], F32)
        gcmp = before[0:1, :, :].rearrange("p b t -> p (b t)")[:, 0:GROUPS * NB].rearrange("p (g b) -> p g b", b=NB)
        gblk = sb("gblk", [1, GROUPS], F32)
        ps_hist = [ps(f"ps_hist{h}", [L, CH, NB]) for h in range(2)]
        ps_t = [ps(f"ps_t{h}", [L, CH, L + 1], BF16) for h in range(2)]
        ps_same = [ps(f"ps_same{h}", [L, 512]) for h in range(2)]
        ps_slot = [ps(f"ps_slot{h}", [L, CH, 2 * NB]) for h in range(2)]

        iotas_ready, consts_ready = sem("iotas_ready"), sem("consts_ready")
        edges_in, fill_set, fill_done = sem("edges_in"), sem("fill_set"), sem("fill_done")
        v_link = sem("sort_v_link")
        counted_set, hist_done, hist_kept = sem("counted_set"), sem("hist_done"), sem("hist_kept")
        onehot_set, t_done, t_kept, same_done = sem("onehot_set"), sem("t_done"), sem("t_kept"), sem("same_done")
        ahead_set, slot_done, weighted_set, slotf_set, slot_set = sem("ahead_set"), sem("slot_done"), sem("weighted_set"), sem("slotf_set"), sem("slot_set")
        totals_set, totals_done = sem("totals_set"), sem("totals_done")
        base_set, based, quotient_set, digit_set, digits_set = sem("base_set"), sem("based"), sem("quotient_set"), sem("digit_set"), sem("digits_set")
        scatter_staged = [sem(f"sort_scatter_staged{h}") for h in range(2)]
        UNITS = ET // CH
        TURNS = UNITS // BUFS

        def at_least(eng, one, value):
            if not isinstance(value, int) or value > 0:
                eng.wait_ge(one, value)

        block_ctx = ExitStack()
        block = block_ctx.enter_context(nc.Block())

        @block.sync
        def _(sp):
            sp.dma_start(src_i[:, :], src.rearrange("(p t) -> p t", t=ET)).then_inc(edges_in, 16)
            sp.dma_start(dst_i[:, :], dst.rearrange("(p t) -> p t", t=ET)).then_inc(edges_in, 16)
            sp.wait_ge(fill_set, 1)
            for rec in recs:
                sp.dma_start(rec.rearrange("(p c) o -> p (c o)", c=REC_COLS), fill[:, :]).then_inc(fill_done, 16)
            sp.wait_ge(fill_done, 16 * RECS)

        @block.gpsimd
        def _(pool):
            nc.gpsimd.iota(row[:, :], pattern=[[1, P]], base=0, channel_multiplier=0, allow_small_or_imprecise_dtypes=True).then_inc(iotas_ready, 1)
            nc.gpsimd.iota(col[:, :], pattern=[[1, 1]], base=0, channel_multiplier=1, allow_small_or_imprecise_dtypes=True).then_inc(iotas_ready, 1)
            nc.gpsimd.iota(giota[:, :], pattern=[[1, GROUPS]], base=0, channel_multiplier=0, allow_small_or_imprecise_dtypes=True).then_inc(iotas_ready, 1)
            nc.gpsimd.memset(fill[:, :], PAD_RECORD).then_inc(fill_set, 1)
            nc.gpsimd.memset(const["eps"][:, :], 1e-5)
            nc.gpsimd.memset(ones[:, :], 1.0).then_inc(consts_ready, 1)
            pool.wait_ge(fill_done, 16 * RECS)
            scatter_records(nc, pool, keep, recs, written, scatter_staged, 0, SORT_SCATTERS, slot_set)

        @block.vector
        def _(dve):
            link = linker(dve, v_link)
            v = nc.vector
            dve.wait_ge(iotas_ready, 3)
            v.tensor_copy(rowb[:, :], row[:, :])
            v.tensor_scalar(ident[:, :], row[:, :], col[:, 0:1], None, ALU.is_equal)
            v.tensor_scalar(identb[:, :], row[:, :], col[:, 0:1], None, ALU.is_equal)
            link(v.tensor_scalar(tri[:, :], row[:, :], col[:, 0:1], None, ALU.is_gt))
            dve.sem_inc(consts_ready, 1)
            dve.wait_ge(edges_in, 32)
            v.scalar_tensor_tensor(keep["key"][:, :], src_i[:, :], float(KEY), dst_i[:, :], ALU.mult, ALU.add)
            link(v.tensor_scalar(scaled[:, :], src_i[:, :], 1.0 / L, 0.5 / L - 0.5, ALU.mult, ALU.add))
            link(v.tensor_scalar(blockf[:, :], scaled[:, :], ROUND, -ROUND, ALU.add, ALU.add))
            link(v.scalar_tensor_tensor(localf[:, :], blockf[:, :], -float(L), src_i[:, :], ALU.mult, ALU.add))
            link(v.tensor_tensor(onehot_block[:, :, NB:2 * NB], blockf[:, :].unsqueeze(2).broadcast_to([L, ET, NB]),
                                 row[0:L, 0:NB].unsqueeze(1).broadcast_to([L, ET, NB]), ALU.is_equal))
            v.memset(before[:, :, 0:1], 0.0)
            v.memset(zeros[:, :], 0.0)
            link(v.tensor_scalar(onehot_block[:, :, 0:NB], onehot_block[:, :, NB:2 * NB], 256.0, None, ALU.mult))
            def onehots(n, q, one):
                v.tensor_tensor(onehot[q][:, :, :], row[0:L, 0:L].unsqueeze(1).broadcast_to([L, CH, L]),
                                localf[:, DS(n * CH, CH)].unsqueeze(2).broadcast_to([L, CH, L]), ALU.is_equal).then_inc(one, 1)

            for q in range(BUFS):
                onehots(q, q, counted_set)
            with v.Fori(1, TURNS) as t:
                for q in range(BUFS):
                    dve.wait_ge(hist_done, t * BUFS + (q - BUFS + 1))
                    onehots(t * BUFS + q, q, counted_set)
            dve.wait_ge(hist_kept, UNITS)
            for b in range(NB):
                ins = v.tensor_tensor_scan(before[:, b, 1:ET + 1], before[:, b, 1:ET + 1], zeros[:, :], 0.0, ALU.add, ALU.add)
            link(ins)
            v.tensor_copy(totals[:, :], before[:, :, ET]).then_inc(totals_set, 1)
            dve.wait_ge(totals_done, 1)
            link(v.tensor_scalar(groups_i[0:L, :], ps_hist[0][:, 1, :], float(GE - 1), None, ALU.add))
            link(v.tensor_scalar(groups_i[0:L, :], groups_i[0:L, :], GE.bit_length() - 1, None, ALU.logical_shift_right))
            link(v.tensor_copy(groups_f[0:L, :], groups_i[0:L, :]))
            link(v.tensor_tensor_scan(group_end[0:L, :], groups_f[0:L, :], zeros[:, 0:NB], 0.0, ALU.add, ALU.add))
            link(v.tensor_sub(group_start[0:L, :], group_end[0:L, :], groups_f[0:L, :]))
            link(v.tensor_scalar(base[:, :], group_start[0:L, :], float(GE), 1.0 - MIDDLE, ALU.mult, ALU.add))
            v.tensor_add(base[:, :], base[:, :], ps_hist[0][:, 0, :]).then_inc(base_set, 1)
            for b in range(NB):
                dve.wait_ge(quotient_set, b + 1)
                v.tensor_scalar(firstp[:, :, b], quotient[b % 2][:, :], ROUND, -ROUND, ALU.add, ALU.add).then_inc(digit_set, 1)
                dve.wait_ge(digit_set, b + 1)
                ins = v.scalar_tensor_tensor(firstp[:, :, NB + b], firstp[:, :, b], -256.0, before[:, b, 0:ET], ALU.mult, ALU.add)
            ins.then_inc(digits_set, 1)

            def one_hots(n, q):
                at_least(dve, t_done, n - BUFS + 1)
                onehots(n, q, onehot_set)

            def earlier(n, q):
                dve.wait_ge(same_done, n + 1)
                at_least(dve, slot_done, n - 1)
                v.tensor_tensor(ahead[q % 2][:, :, :], ps_same[q % 2][:, 0:CH * L].rearrange("p (c e) -> p c e", c=CH),
                                tri[0:L, 0:L].unsqueeze(1).broadcast_to([L, CH, L]), ALU.mult).then_inc(ahead_set, 1)

            def pick(n, q):
                dve.wait_ge(slot_done, n + 1)
                at_least(dve, slotf_set, n - 1)
                v.tensor_tensor(weighted[q % 2][:, :, :], ps_slot[q % 2][:, :, :], onehot_block[:, DS(n * CH, CH), :], ALU.mult).then_inc(weighted_set, 1)

            def keep_slots(n, q):
                dve.wait_ge(weighted_set, n + 1)
                at_least(dve, slot_set, n - 1)
                v.tensor_reduce(slotf[q % 2][:, :], weighted[q % 2][:, :, :], AX.X, ALU.add).then_inc(slotf_set, 1)

            def write_slots(n, q):
                dve.wait_ge(slotf_set, n + 1)
                v.tensor_scalar(keep["slot"][:, DS(n * CH, CH)], slotf[q % 2][:, :], MIDDLE, None, ALU.add).then_inc(slot_set, 1)

            in_turns(v, TURNS, ((0, one_hots), (4, write_slots), (3, pick), (1, earlier), (3, keep_slots)))
            dve.wait_ge(digits_set, 1)
            link(v.tensor_tensor(gcmp[:, :, :], giota[:, :].unsqueeze(2).broadcast_to([1, GROUPS, NB]),
                                 group_start[0:1, :].unsqueeze(1).broadcast_to([1, GROUPS, NB]), ALU.is_ge))
            link(v.tensor_reduce(gblk[:, :], gcmp[:, :, 1:NB], AX.X, ALU.add))
            v.tensor_copy(keep["group_block"][:, :], gblk[:, :])

        @block.tensor
        def _(pe):
            pe.wait_ge(consts_ready, 2)
            def count(n, q):
                pe.wait_ge(counted_set, n + 1)
                at_least(pe, hist_kept, n - 1)
                for j in range(CH):
                    ins = nc.tensor.matmul(ps_hist[q % 2][:, j, :], onehot[q][:, j, :],
                                           onehot_block[:, DS(n * CH + j, 1), NB:2 * NB].rearrange("p o b -> p (o b)"), start=True, stop=True)
                ins.then_inc(hist_done, 1)

            in_turns(nc.tensor, TURNS, ((0, count),))
            pe.wait_ge(totals_set, 1)
            nc.tensor.matmul(ps_hist[0][:, 0, :], tri[0:L, 0:L], totals[:, :], start=True, stop=True)
            nc.tensor.matmul(ps_hist[0][:, 1, :], ones[0:L, 0:L], totals[:, :], start=True, stop=True).then_inc(totals_done, 1)
            pe.wait_ge(digits_set, 1)

            def turn_over(n, q):
                pe.wait_ge(onehot_set, n + 1)
                at_least(pe, t_kept, n - 1)
                for j in range(CH):
                    ins = nc.tensor.transpose(ps_t[q % 2][:, j, 0:L], onehot[q][:, j, :], identb[0:L, 0:L])
                ins.then_inc(t_done, 1)

            def compare(n, q):
                pe.wait_ge(t_kept, n + 1)
                at_least(pe, ahead_set, n - 1)
                for j in range(CH):
                    ins = nc.tensor.matmul(ps_same[q % 2][:, j * L:(j + 1) * L], onehot_t[q][:, j, :], onehot_t[q][:, j, :], start=True, stop=True)
                ins.then_inc(same_done, 1)

            def slots(n, q):
                pe.wait_ge(ahead_set, n + 1)
                at_least(pe, weighted_set, n - 1)
                for j in range(CH):
                    tile = DS(n * CH + j, 1)
                    nc.tensor.matmul(ps_slot[q % 2][:, j, :], onehot_t[q][:, j, :],
                                     firstp[:, tile, :].rearrange("p o b -> p (o b)"), start=True, stop=False)
                    ins = nc.tensor.matmul(ps_slot[q % 2][:, j, NB:2 * NB], ahead[q % 2][:, j, :],
                                           onehot_block[:, tile, NB:2 * NB].rearrange("p o b -> p (o b)"), start=False, stop=True)
                ins.then_inc(slot_done, 1)

            in_turns(nc.tensor, TURNS, ((1, compare), (0, turn_over), (2, slots)))

        @block.scalar
        def _(act):
            def keep_counts(n, q):
                act.wait_ge(hist_done, n + 1)
                nc.scalar.copy(before[:, :, DS(n * CH + 1, CH)], ps_hist[q % 2][:, :, :].rearrange("p c b -> p b c")).then_inc(hist_kept, 1)

            in_turns(nc.scalar, TURNS, ((0, keep_counts),))
            act.wait_ge(base_set, 1)
            for b in range(NB):
                nc.scalar.activation(before[:, b, 0:ET], before[:, b, 0:ET], ACT.Identity, bias=base[:, b:b + 1]).then_inc(based, 1)
                act.wait_ge(based, b + 1)
                if b >= 2:
                    act.wait_ge(digit_set, b - 1)
                nc.scalar.activation(quotient[b % 2][:, :], before[:, b, 0:ET], ACT.Copy, scale=1.0 / 256, bias=0.5 / 256 - 0.5).then_inc(quotient_set, 1)

            def keep_columns(n, q):
                act.wait_ge(t_done, n + 1)
                at_least(act, slot_done, n - BUFS + 1)
                nc.scalar.copy(onehot_t[q][:, :, :], ps_t[q % 2][:, :, 0:L]).then_inc(t_kept, 1)

            in_turns(nc.scalar, TURNS, ((0, keep_columns),))

        block_ctx.close()
        clear_semaphores(nc, sems)


def scatter_records(nc, pool, keep, recs, written, staged, first, last, ready=None):
    slot_set, key_set = keep["scatter_slot"], keep["scatter_key"]

    def turn(t, s, begins=False):
        at = DS((t * 2 + s) * RECS, RECS)
        if ready is not None:
            pool.wait_ge(ready, t * 2 + s + 1)
            pool.nop(nofuse=True)
        nc.gpsimd.tensor_copy(slot_set[s][:, :], keep["slot"][:, at])
        nc.gpsimd.tensor_copy(key_set[s][:, :], keep["key"][:, at]).then_inc(staged[s], 1)
        pool.wait_ge(staged[s], t - first + 1)
        pool.nop(nofuse=True)
        for j in range(RECS):
            if not begins:
                pool.wait_ge(written[j], t * 32 + s * 16)
                pool.nop(nofuse=True)
            nc.gpsimd.indirect_dma_start(recs[j], bass.IndirectOffsetOnAxis(ap=slot_set[s][:, j:j + 1], axis=0),
                                         key_set[s][:, j:j + 1], None).then_inc(written[j], 16)

    turn(first, 0, begins=first == 0)
    turn(first, 1)
    with nc.gpsimd.Fori(first + 1, last) as t:
        turn(t, 0)
        turn(t, 1)
    for j in range(RECS):
        pool.wait_ge(written[j], last * 32)


def project_and_mix(nc, a, const, keep, x_sb, recs, written, tab_v, tab_u, tab_e):
    ident, ones, eps = const["ident"], const["ones"], const["eps"]
    with ExitStack() as ctx:
        def sb(name, shape, dt=F32):
            return ctx.enter_context(nc.sbuf_tensor(name, shape, dt))

        def ps(name, shape, dt=F32):
            return ctx.enter_context(nc.psum_tensor(name, shape, dt))

        sems = []

        def sem(name):
            sems.append(ctx.enter_context(nc.semaphore(name)))
            return sems[-1]

        w_e, w_r = sb("w_e", [P, KF, HEADS, D]), sb("w_r", [P, KF, HEADS, D])
        w_in, w_out = sb("w_in", [P, KF, F]), sb("w_out", [P, KF, F])
        a_row = sb("a_row", [P, HEADS, 5, D])
        b_in_col, b_out_row = sb("b_in_col", [P, KF]), sb("b_out_row", [1, F])
        wq2, wk2 = sb("wq2", [P, 2 * SLICE]), sb("wk2", [P, 2 * SLICE])
        wv2 = sb("wv2", [P, 2 * D])
        w_node = sb("w_node", [P, KF, 2 * HEADS])
        half_prd = sb("half_prd", [P, HEADS, D])
        prod_e = sb("prod_e", [P, KF, HEADS, D])
        term = sb("term", [P, 4, KF, HEADS])
        stats, moments = sb("stats", [L, NB, 6]), sb("moments", [L, NB, 2])
        deviation, rstd = sb("deviation", [L, NB]), sb("rstd", [L, NB])
        xn = sb("xn", [L, F])
        xn_t = sb("xn_t", [P, KF, L])
        xm_t = sb("xm_t", [P, KF, L])
        row_v, row_e, row_u = sb("row_v", [L, EW]), sb("row_e", [L, F]), sb("row_u", [L, HEADS])
        squares, squares_w, square_sum = sb("squares", [L, HEADS, D]), sb("squares_w", [L, HEADS, D]), sb("square_sum", [L, HEADS])
        q_max, q_sum, q_inv = sb("q_max", [L, HEADS]), sb("q_sum", [L, HEADS]), sb("q_inv", [L, HEADS])
        q_exp, q_soft = sb("q_exp", [L, HEADS, SLICE]), sb("q_soft", [L, HEADS * SLICE])
        qt_all, kt_all = sb("qt_all", [P, 2, N]), sb("kt_all", [P, 2, N])
        v_all = sb("v_all", [L, NB, F])
        k_max, k_sum, k_inv = sb("k_max", [P, 2]), sb("k_sum", [P, 2]), sb("k_inv", [P, 2])
        staged_t = sb("staged_t", [P, 2, L])
        k_rows = sb("k_rows", [L, 2 * P])
        head_of_row, head_of_row_i = sb("head_of_row", [P, 1]), sb("head_of_row_i", [P, 1], I32)
        head_of_col, same_head = sb("head_of_col", [P, 2 * P]), sb("same_head", [P, 2 * P])
        late = prod_e[:, :, :, :].rearrange("p k h d -> p (k h d)")
        kv = late[:, 0:F].rearrange("p (g c) -> p g c", g=2)
        kv_t = late[:, F:2 * F].rearrange("p (g c n) -> p g c n", g=2, c=2)
        kvw = late[:, 2 * F:4 * F].rearrange("p (g f) -> p g f", g=2)
        zero_rows = sb("zero_rows", [L, 2 * P])
        ps_xt, ps_hr, ps_he = ps("ps_xt", [P, F]), ps("ps_hr", [P, F]), ps("ps_he", [P, F])
        ps_s, ps_xm, ps_q = ps("ps_s", [L, 2 * HEADS]), ps("ps_xm", [P, F]), ps("ps_q", [L, F])
        ps_v, ps_k = ps("ps_v", [P, F]), ps("ps_k", [P, F])

        scatter_staged = [sem(f"scatter_staged{h}") for h in range(2)]
        loaded = [sem(f"loaded{i}") for i in range(2)]
        zeroed, masks_set = sem("zeroed"), sem("masks_set")
        dve_link = sem("mix_dve_link")
        var_set, dev_set = sem("var_set"), sem("dev_set")
        weights_set = sem("weights_set")
        names = ("xn_set xt_done xt_kept proj_done rows_kept rows_set rows_free xm_done xm_kept qvk_done kv_kept "
                 "q_shifted q_exped q_set qt_done qt_kept loop_link kmax_set kexp_set k_staged k_done k_kept kv_done "
                 "kv_set kvt_done kvt_kept kvw_done kvw_kept q_staged mix_done mix_added").split()
        s = {n: sem(n) for n in names}
        rows_out, weights_in = sem("rows_out"), sem("weights_in")
        WEIGHT_LOADS = 2 * KF + 5
        block_ctx = ExitStack()
        block = block_ctx.enter_context(nc.Block())

        @block.sync
        def _(sp):
            sp.dma_start(x_sb[:, :, :], a["x"].rearrange("(t p) f -> p t f", p=L)).then_inc(loaded[0], 16)
            sp.wait_ge(zeroed, 1)
            for h in range(2):
                sp.dma_start(wq2[h * D:(h + 1) * D, h * SLICE:(h + 1) * SLICE], a["L0_mix_Wq"]).then_inc(loaded[1], 16)
                sp.dma_start(wk2[h * D:(h + 1) * D, h * SLICE:(h + 1) * SLICE], a["L0_mix_Wk"]).then_inc(loaded[1], 16)
                sp.dma_start(wv2[h * D:(h + 1) * D, h * D:(h + 1) * D], a["L0_mix_Wv"]).then_inc(loaded[1], 16)
            with nc.sync.Fori(0, NB) as t:
                sp.wait_ge(s["rows_set"], t + 2)
                at = DS(t * L, L)
                sp.dma_start(tab_v[at, :], row_v[:, :]).then_inc(rows_out, 16)
                sp.dma_start(tab_u[at, 0:F], row_v[:, 0:F]).then_inc(rows_out, 16)
                sp.dma_start(tab_u[at, F:EW], row_u[:, :]).then_inc(rows_out, 16)
                sp.dma_start(tab_e[at, :], row_e[:, :]).then_inc(rows_out, 16)
                sp.wait_ge(rows_out, t * 64 + 64)
                sp.sem_inc(s["rows_free"], 1)

        @block.gpsimd
        def _(pool):
            nc.gpsimd.memset(wq2[:, :], 0.0)
            nc.gpsimd.memset(wk2[:, :], 0.0)
            nc.gpsimd.memset(zero_rows[:, :], 0.0)
            nc.gpsimd.memset(wv2[:, :], 0.0).then_inc(zeroed, 1)
            nc.gpsimd.iota(head_of_row_i[:, :], pattern=[[1, 1]], base=0, channel_multiplier=1)
            nc.gpsimd.iota(head_of_col[:, :], pattern=[[1, 2 * P // D], [0, D]], base=0, channel_multiplier=0,
                           allow_small_or_imprecise_dtypes=True).then_inc(masks_set, 1)
            scatter_records(nc, pool, keep, recs, written, scatter_staged, SORT_SCATTERS, SCATTERS)

        @block.vector
        def _(dve):
            v = nc.vector
            link = linker(dve, dve_link)
            for n in ("xt_done", "qt_done", "mix_done", "k_done"):
                dve.sem_inc(s[n], 1)
            dve.wait_ge(loaded[0], 16)
            with v.Fori(0, NB) as t:
                ins = v.bn_stats(stats[:, DS(t, 1), :].rearrange("p o s -> p (o s)"),
                                 x_sb[:, DS(t, 1), :].rearrange("p o f -> p (o f)"))
            link(v.memset(q_max[:, :], 0.0))
            for t in range(NB):
                ins = v.bn_aggr(moments[:, t, :], stats[:, t, :])
            ins.then_inc(var_set, 1)
            dve.wait_ge(weights_in, 16 * WEIGHT_LOADS)

            def a_part(i):
                return a_row[:, :, i, :].unsqueeze(1).broadcast_to([P, KF, HEADS, D])

            for i, (w, part) in enumerate(((w_e, 0), (w_e, 1), (w_r, 2))):
                link(v.tensor_tensor(prod_e[:, :, :, :], w[:, :, :, :], a_part(part), ALU.mult))
                link(v.tensor_reduce(term[:, i, :, :], prod_e[:, :, :, :], AX.X, ALU.add))
            v.tensor_sub(w_node[:, :, 0:HEADS], term[:, 0, :, :], term[:, 2, :, :])
            v.tensor_add(w_node[:, :, HEADS:2 * HEADS], term[:, 1, :, :], term[:, 2, :, :])
            v.tensor_scalar(half_prd[:, :, :], a_row[:, :, 4, :], 0.5, None, ALU.mult).then_inc(weights_set, 1)
            dve.wait_ge(weights_set, 1)
            dve.wait_ge(masks_set, 1)
            link(v.tensor_scalar(head_of_row_i[:, :], head_of_row_i[:, :], SLICE.bit_length() - 1, None, ALU.logical_shift_right))
            link(v.tensor_copy(head_of_row[:, :], head_of_row_i[:, :]))
            link(v.tensor_scalar(same_head[:, :], head_of_col[:, :], head_of_row[:, 0:1], None, ALU.is_equal))
            dve.wait_ge(dev_set, 1)
            link(v.reciprocal(rstd[:, :], deviation[:, :]))
            STEPS = 7
            with v.Fori(0, NB) as t:
                step = linker(dve, s["loop_link"], t * STEPS)
                dve.wait_ge(s["xt_done"], t + 1)
                v.tensor_scalar(xn[:, :], x_sb[:, DS(t, 1), :].rearrange("p o f -> p (o f)"), moments[:, DS(t, 1), 0:1].rearrange("p a b -> p (a b)"),
                                rstd[:, DS(t, 1)], ALU.subtract, ALU.mult).then_inc(s["xn_set"], 1)
                dve.wait_ge(s["rows_kept"], t + 2)
                h_r = row_v[:, 0:F].rearrange("p (c h r) -> p h c r", c=KF, h=HEADS)
                step(v.tensor_tensor(squares[:, :, :].rearrange("p h (c r) -> p h c r", c=KF), h_r, h_r, ALU.mult))
                step(v.tensor_tensor(squares_w[:, :, :], squares[:, :, :], half_prd[0:L, :, :], ALU.mult))
                step(v.tensor_reduce(square_sum[:, :], squares_w[:, :, :], AX.X, ALU.add))
                v.tensor_tensor(row_v[:, F:EW], ps_s[:, HEADS:2 * HEADS], square_sum[:, :], ALU.add)
                v.scalar_tensor_tensor(row_u[:, :], ps_s[:, 0:HEADS], -1.0, square_sum[:, :], ALU.mult, ALU.subtract).then_inc(s["rows_set"], 1)
                dve.wait_ge(s["qvk_done"], t + 2)
                q = ps_q[:, 0:HEADS * SLICE].rearrange("p (h s) -> p h s", h=HEADS)
                step(v.tensor_reduce(q_max[:, :], q, AX.X, ALU.max))
                v.tensor_tensor(q_exp[:, :, :], q, q_max[:, :].unsqueeze(2).broadcast_to([L, HEADS, SLICE]), ALU.subtract).then_inc(s["q_shifted"], 1)
                dve.wait_ge(s["q_exped"], t + 1)
                step(v.tensor_reduce(q_sum[:, :], q_exp[:, :, :], AX.X, ALU.add))
                step(v.reciprocal(q_inv[:, :], q_sum[:, :]))
                dve.wait_ge(s["qt_done"], t + 1)
                step(v.tensor_tensor(q_soft[:, :].rearrange("p (h s) -> p h s", h=HEADS), q_exp[:, :, :],
                                     q_inv[:, :].unsqueeze(2).broadcast_to([L, HEADS, SLICE]), ALU.mult))
                dve.sem_inc(s["q_set"], 1)
            assert step.count[0] == STEPS
            dve.wait_ge(s["kv_kept"], NB + 1)
            link(v.tensor_reduce(k_max[:, :], kt_all[:, :, :], AX.X, ALU.max))
            v.tensor_scalar(k_max[:, :], k_max[:, :], -1.0, None, ALU.mult).then_inc(s["kmax_set"], 1)
            dve.wait_ge(s["kexp_set"], 1)
            link(v.tensor_reduce(k_sum[:, :], kt_all[:, :, :], AX.X, ALU.add))
            link(v.reciprocal(k_inv[:, :], k_sum[:, :]))
            with v.Fori(0, NB) as t:
                dve.wait_ge(s["k_done"], t + 1)
                v.tensor_copy(staged_t[:, :, :], kt_all[:, :, DS(t * L, L)]).then_inc(s["k_staged"], 1)
            dve.wait_ge(s["kv_done"], 1)
            for g, acc in enumerate((ps_hr, ps_he)):
                ins = v.scalar_tensor_tensor(kv[:, g, :], acc[:, 0:2 * P], k_inv[:, g:g + 1], same_head[:, :], ALU.mult, ALU.mult)
            ins.then_inc(s["kv_set"], 1)
            dve.wait_ge(s["qt_kept"], NB + 1)
            with v.Fori(0, NB) as t:
                dve.wait_ge(s["mix_done"], t + 1)
                v.tensor_copy(staged_t[:, :, :], qt_all[:, :, DS(t * L, L)]).then_inc(s["q_staged"], 1)
                dve.wait_ge(s["mix_done"], t + 2)
                tile = x_sb[:, DS(t, 1), :].rearrange("p o f -> p (o f)")
                v.tensor_tensor(tile, ps_xm[0:L, :], tile, ALU.add).then_inc(s["mix_added"], 1)

        @block.tensor
        def _(pe):
            t_ = nc.tensor
            pe.wait_ge(weights_set, 1)
            pe.wait_ge(loaded[1], 16 * 6)
            pe.wait_ge(weights_in, 16 * WEIGHT_LOADS)
            with t_.Fori(0, NB) as t:
                pe.wait_ge(s["xn_set"], t + 1)
                pe.wait_ge(s["xt_kept"], t + 1)
                for k in range(KF):
                    ins = t_.transpose(ps_xt[:, k * L:(k + 1) * L], xn[:, k * P:(k + 1) * P], ident[0:L, 0:L])
                ins.then_inc(s["xt_done"], 1)
                pe.wait_ge(s["xt_kept"], t + 2)
                pe.wait_ge(s["rows_kept"], t + 1)
                pe.wait_ge(s["rows_set"], t + 1)
                for k in range(KF):
                    t_.matmul(ps_hr[0:L, :], xn_t[:, k, :], w_r[:, k, :, :].rearrange("p h d -> p (h d)"), start=k == 0, stop=k == KF - 1)
                for k in range(KF):
                    t_.matmul(ps_he[0:L, :], xn_t[:, k, :], w_e[:, k, :, :].rearrange("p h d -> p (h d)"), start=k == 0, stop=k == KF - 1)
                for k in range(KF):
                    ins = t_.matmul(ps_s[:, :], xn_t[:, k, :], w_node[:, k, :], start=k == 0, stop=k == KF - 1)
                ins.then_inc(s["proj_done"], 1)
                pe.wait_ge(s["xm_kept"], t + 1)
                for c in range(KF):
                    for k in range(KF):
                        ins = t_.matmul(ps_xm[:, c * L:(c + 1) * L], w_in[:, k, c * P:(c + 1) * P], xn_t[:, k, :], start=k == 0, stop=k == KF - 1)
                ins.then_inc(s["xm_done"], 1)
                pe.wait_ge(s["xm_kept"], t + 2)
                pe.wait_ge(s["kv_kept"], t + 1)
                pe.wait_ge(s["qt_kept"], t + 1)
                for c in range(KF):
                    t_.matmul(ps_q[:, c * 2 * SLICE:(c + 1) * 2 * SLICE], xm_t[:, c, :], wq2[:, :], start=True, stop=True)
                    t_.matmul(ps_v[0:L, c * P:(c + 1) * P], xm_t[:, c, :], wv2[:, :], start=True, stop=True)
                    half = c % 2 * D
                    ins = t_.matmul(ps_k[half:half + D, c // 2 * L:(c // 2 + 1) * L], wk2[:, :], xm_t[:, c, :], start=True, stop=True)
                ins.then_inc(s["qvk_done"], 1)
                pe.wait_ge(s["q_set"], t + 1)
                pe.wait_ge(s["kv_kept"], t + 2)
                for g in range(2):
                    ins = t_.transpose(ps_k[:, g * L:(g + 1) * L], q_soft[:, g * P:(g + 1) * P], ident[0:L, 0:L])
                ins.then_inc(s["qt_done"], 1)
            pe.wait_ge(s["rows_kept"], NB + 1)
            pe.wait_ge(zeroed, 1)
            for acc in (ps_hr, ps_he):
                t_.matmul(acc[:, 0:2 * P], zero_rows[:, 0:P], zero_rows[:, :], start=True, stop=False)
            with t_.Fori(0, NB) as t:
                pe.wait_ge(s["k_staged"], t + 1)
                pe.wait_ge(s["k_kept"], t + 1)
                for g in range(2):
                    ins = t_.transpose(ps_q[:, g * P:(g + 1) * P], staged_t[:, g, :], ident[:, :])
                ins.then_inc(s["k_done"], 1)
                pe.wait_ge(s["k_kept"], t + 2)
                for g, acc in enumerate((ps_hr, ps_he)):
                    ins = t_.matmul(acc[:, 0:2 * P], k_rows[:, g * P:(g + 1) * P],
                                    v_all[:, DS(t, 1), g * 2 * P:(g + 1) * 2 * P].rearrange("p o c -> p (o c)"), start=False, stop=False)
            for acc in (ps_hr, ps_he):
                ins = t_.matmul(acc[:, 0:2 * P], zero_rows[:, 0:P], zero_rows[:, :], start=False, stop=True)
            ins.then_inc(s["kv_done"], 1)
            pe.wait_ge(s["kv_set"], 1)
            for g in range(2):
                for c in range(2):
                    ins = t_.transpose(ps_xt[:, (2 * g + c) * P:(2 * g + c + 1) * P], kv[:, g, c * P:(c + 1) * P], ident[:, :])
            ins.then_inc(s["kvt_done"], 1)
            pe.wait_ge(s["kvt_kept"], 1)
            pe.wait_ge(s["qt_kept"], NB + 1)
            for g, acc in enumerate((ps_v, ps_k)):
                for c in range(2):
                    ins = t_.matmul(acc[:, :], kv_t[:, g, c, :], w_out[:, 2 * g + c, :], start=c == 0, stop=c == 1)
            ins.then_inc(s["kvw_done"], 1)
            pe.wait_ge(s["kvw_kept"], 1)
            with t_.Fori(0, NB) as t:
                pe.wait_ge(s["q_staged"], t + 1)
                pe.wait_ge(s["mix_added"], t + 1)
                for g in range(2):
                    t_.matmul(ps_xm[0:L, :], staged_t[:, g, :], kvw[:, g, :], start=g == 0, stop=False)
                t_.matmul(ps_xm[0:L, :], ones[0:1, 0:L], b_out_row[:, :], start=False, stop=True).then_inc(s["mix_done"], 1)

        @block.scalar
        def _(act):
            sc = nc.scalar
            for w, name in ((w_r, "L0_gnn_W_r"), (w_e, "L0_gnn_W_e")):
                for k in range(KF):
                    act.dma_start(w[:, k, :, :], a[name][:, k * P:(k + 1) * P, :].rearrange("h p d -> p h d")).then_inc(weights_in, 16)
            act.dma_start(w_in[:, :, :], a["L0_mix_W_in"].rearrange("(k p) f -> p k f", p=P)).then_inc(weights_in, 16)
            act.dma_start(w_out[:, :, :], a["L0_mix_W_out"].rearrange("(k p) f -> p k f", p=P)).then_inc(weights_in, 16)
            act.dma_start(a_row[:, :, :, :], a["L0_gnn_a"].rearrange("h (c d) -> h c d", d=D).partition_broadcast(P)).then_inc(weights_in, 16)
            act.dma_start(b_in_col[:, :], a["L0_mix_b_in"].rearrange("(k p) -> p k", p=P), allow_slow_non_contiguous=True).then_inc(weights_in, 16)
            act.dma_start(b_out_row[:, :], a["L0_mix_b_out"].rearrange("(o f) -> o f", o=1)).then_inc(weights_in, 16)
            for n in ("xt_kept", "rows_kept", "rows_free", "xm_kept", "kv_kept", "qt_kept", "k_kept", "mix_added", "xm_done", "qvk_done", "rows_set"):
                act.sem_inc(s[n], 1)
            act.wait_ge(weights_in, 16 * WEIGHT_LOADS)
            act.wait_ge(var_set, 1)
            sc.activation(deviation[:, :], moments[:, :, 1], ACT.Sqrt, bias=eps[0:L, 0:1]).then_inc(dev_set, 1)
            with sc.Fori(0, NB) as t:
                act.wait_ge(s["xt_done"], t + 2)
                act.wait_ge(s["xm_done"], t + 1)
                sc.copy(xn_t[:, :, :], ps_xt[:, 0:KF * L].rearrange("p (k n) -> p k n", k=KF)).then_inc(s["xt_kept"], 1)
                act.wait_ge(s["proj_done"], t + 1)
                act.wait_ge(s["rows_free"], t + 1)
                sc.copy(row_e[:, :], ps_he[0:L, :])
                sc.copy(row_v[:, 0:F].rearrange("p (c h r) -> p h c r", c=KF, h=HEADS),
                        ps_hr[0:L, :].rearrange("p (h c r) -> p h c r", h=HEADS, c=KF)).then_inc(s["rows_kept"], 1)
                act.wait_ge(s["xm_done"], t + 2)
                act.wait_ge(s["qvk_done"], t + 1)
                for c in range(KF):
                    ins = sc.activation(xm_t[:, c, :], ps_xm[:, c * L:(c + 1) * L], ACT.Identity, bias=b_in_col[:, c:c + 1])
                ins.then_inc(s["xm_kept"], 1)
                act.wait_ge(s["qvk_done"], t + 2)
                sc.copy(v_all[:, DS(t, 1), :].rearrange("p o f -> p (o f)"), ps_v[0:L, :])
                sc.copy(kt_all[:, :, DS(t * L, L)], ps_k[:, 0:2 * L].rearrange("p (g n) -> p g n", g=2)).then_inc(s["kv_kept"], 1)
                act.wait_ge(s["q_shifted"], t + 1)
                sc.activation(q_exp[:, :, :], q_exp[:, :, :], ACT.Exp).then_inc(s["q_exped"], 1)
                act.wait_ge(s["qt_done"], t + 2)
                sc.copy(qt_all[:, :, DS(t * L, L)], ps_k[:, 0:2 * L].rearrange("p (g n) -> p g n", g=2)).then_inc(s["qt_kept"], 1)
            act.wait_ge(s["kmax_set"], 1)
            for g in range(2):
                ins = sc.activation(kt_all[:, g, :], kt_all[:, g, :], ACT.Exp, bias=k_max[:, g:g + 1])
            ins.then_inc(s["kexp_set"], 1)
            with sc.Fori(0, NB) as t:
                act.wait_ge(s["k_done"], t + 2)
                sc.copy(k_rows[:, :], ps_q[:, 0:2 * P]).then_inc(s["k_kept"], 1)
            act.wait_ge(s["kvt_done"], 1)
            sc.copy(kv_t[:, :, :, :].rearrange("p g c n -> p (g c n)"), ps_xt[:, :]).then_inc(s["kvt_kept"], 1)
            act.wait_ge(s["kvw_done"], 1)
            sc.copy(kvw[:, 0, :], ps_v[:, :])
            sc.copy(kvw[:, 1, :], ps_k[:, :]).then_inc(s["kvw_kept"], 1)

        block_ctx.close()
        clear_semaphores(nc, sems)


def read_sorted_edges(nc, const, recs, merged, edge):
    ROWS, PER = ST // 6, 6
    with ExitStack() as ctx:
        def sb(name, shape, dt=F32):
            return ctx.enter_context(nc.sbuf_tensor(name, shape, dt))

        def sem(name):
            return ctx.enter_context(nc.semaphore(name))

        lists = sb("lists", [ROWS, RECS, PER * P], I32)
        best = sb("best", [ROWS, PER * P])
        best_i = sb("best_i", [ROWS, PER * P], I32)
        key_t = sb("key_t", [P, ST], I32)
        source_i = sb("source_i", [P, ST], I32)
        source, scaled, blk, pad = sb("source", [P, ST]), sb("scaled_t", [P, ST]), sb("blk_t", [P, ST]), sb("pad_t", [P, ST])
        ps_key = ctx.enter_context(nc.psum_tensor("ps_key", [P, 2, 512], F32))
        lists_in, merged_set, merged_out = sem("lists_in"), sem("merged_set"), sem("merged_out")
        turned, link_s = sem("turned"), sem("read_link")
        block = ctx.enter_context(nc.Block())

        @block.sync
        def _(sp):
            for j in range(RECS):
                sp.dma_start(lists[:, j, :], recs[j][1:1 + EP, :].rearrange("(r x) o -> r (x o)", r=ROWS)).then_inc(lists_in, 16)
            sp.dma_start(merged[0:1, :], recs[0][0:1, :]).then_inc(merged_out, 16)
            sp.dma_start(merged[EP + 1:EP + 2, :], recs[0][EP + 1:EP + 2, :]).then_inc(merged_out, 16)
            sp.wait_ge(merged_set, 1)
            sp.dma_start(merged[1:1 + EP, :].rearrange("(r x) o -> r (x o)", r=ROWS), best_i[:, :]).then_inc(merged_out, 16)
            sp.wait_ge(merged_out, 48)

        @block.vector
        def _(dve):
            v = nc.vector
            link = linker(dve, link_s)
            dve.wait_ge(lists_in, 16 * RECS)
            link(v.tensor_tensor(best[:, :], lists[:, 0, :], lists[:, 1, :], ALU.min))
            for j in range(2, RECS):
                link(v.tensor_tensor(best[:, :], best[:, :], lists[:, j, :], ALU.min))
            v.tensor_copy(best_i[:, :], best[:, :]).then_inc(merged_set, 1)
            dve.wait_ge(turned, 1)
            link(v.tensor_copy(key_t[:, :].rearrange("p (r i j) -> p i j r", i=2, j=PER // 2),
                               ps_key[:, :, 0:PER // 2 * ROWS].rearrange("p i (j r) -> p i j r", j=PER // 2)))
            link(v.tensor_scalar(source_i[:, :], key_t[:, :], KEY.bit_length() - 1, None, ALU.logical_shift_right))
            v.tensor_scalar(edge["dst"][:, :], key_t[:, :], KEY - 1, None, ALU.bitwise_and)
            link(v.tensor_copy(source[:, :], source_i[:, :]))
            v.tensor_scalar(edge["src"][:, :], source[:, :], float(N - 1), None, ALU.min)
            link(v.tensor_scalar(scaled[:, :], source[:, :], 1.0 / L, 0.5 / L - 0.5, ALU.mult, ALU.add))
            v.tensor_scalar(pad[:, :], source[:, :], float(N), 1000.0, ALU.is_ge, ALU.mult)
            link(v.tensor_scalar(blk[:, :], scaled[:, :], ROUND, -ROUND, ALU.add, ALU.add))
            link(v.scalar_tensor_tensor(source[:, :], blk[:, :], -float(L), source[:, :], ALU.mult, ALU.add))
            link(v.tensor_add(edge["local"][:, :], source[:, :], pad[:, :]))

        @block.tensor
        def _(pe):
            pe.wait_ge(merged_set, 1)
            for j in range(PER):
                half, at = j // (PER // 2), j % (PER // 2) * ROWS
                ins = nc.tensor.transpose(ps_key[:, half, at:at + ROWS], best[:, j * P:(j + 1) * P], const["ident"][0:ROWS, 0:ROWS])
            ins.then_inc(turned, 1)


def score_edges(nc, a, const, edge, tab_v, tab_u, scores):
    ident, row = const["ident"], const["row"]
    BUFS = 3
    TURNS = GROUPS // BUFS
    assert TURNS * BUFS == GROUPS
    with ExitStack() as ctx:
        def sb(name, shape, dt=F32):
            return ctx.enter_context(nc.sbuf_tensor(name, shape, dt))

        def ps(name, shape, dt=F32):
            return ctx.enter_context(nc.psum_tensor(name, shape, dt))

        def sem(name):
            return ctx.enter_context(nc.semaphore(name))

        def sems(name):
            return [sem(f"{name}{h}") for h in range(BUFS)]

        def sbs(name, shape, dt=F32):
            return [sb(f"{name}{h}", shape, dt) for h in range(BUFS)]

        index_v, index_u = sbs("index_v", [P, GROUP], I32), sbs("index_u", [P, GROUP], I32)
        rows_v, rows_u = sbs("rows_v", [P, GROUP, EW]), sbs("rows_u", [P, GROUP, EW])
        w, w_abs = sbs("w", [P, GROUP, EW]), sbs("w_abs", [P, KF, GE])
        slope, z_sum = sbs("slope", [P, KF, GE]), sbs("z_sum", [P, GE])
        score = sbs("score", [HEADS, GE])
        a_abs, minus_prd = sb("a_abs", [P, KF]), sb("minus_prd", [P, KF])
        head_i, head_f = sb("head_i", [P, 1], I32), sb("head_f", [P, 1])
        head_sum = sb("head_sum", [P, HEADS])
        ps_w = [ps(f"ps_w{h}", [P, KF, GE]) for h in range(BUFS)]
        ps_pair, ps_third = ps("ps_score_pair", [P, GE]), ps("ps_score_third", [P, GE])
        ps_score = [ps_pair[0:HEADS, :], ps_pair[P // 2:P // 2 + HEADS, :], ps_third[0:HEADS, :]]

        index_set, gathered, w_set, turned = sems("index_set"), sems("gathered"), sems("w_set"), sems("w_turned")
        abs_set, slope_set, z_link, z_set, summed = sems("abs_set"), sems("slope_set"), sems("z_link"), sems("z_set"), sems("summed")
        score_kept, score_free, score_out = sems("score_kept"), sems("score_free"), sems("score_out")
        vectors_in, iota_set, vectors_set, link_s = sem("vectors_in"), sem("head_iota_set"), sem("vectors_set"), sem("score_link")
        block = ctx.enter_context(nc.Block())

        @block.sync
        def _(sp):
            for tile, part in ((a_abs, 3), (minus_prd, 4)):
                for h in range(HEADS):
                    sp.dma_start(tile[h * R:(h + 1) * R, :], a["L0_gnn_a"][h, part * D:(part + 1) * D].rearrange("(c r) -> r c", r=R),
                                 allow_slow_non_contiguous=True).then_inc(vectors_in, 16)
            with nc.sync.Fori(0, TURNS) as t:
                for h in range(BUFS):
                    sp.wait_ge(score_kept[h], t + 2)
                    sp.dma_start(scores[:, DS((BUFS * t + h) * GE, GE)], score[h][:, :]).then_inc(score_out[h], 16)
                for h in range(BUFS):
                    sp.wait_ge(score_out[h], t * 16 + 16)
                    sp.sem_inc(score_free[h], 1)

        @block.gpsimd
        def _(pool):
            nc.gpsimd.iota(head_i[:, :], pattern=[[1, 1]], base=0, channel_multiplier=1).then_inc(iota_set, 1)
            with nc.gpsimd.Fori(0, TURNS) as t:
                for h in range(BUFS):
                    pool.wait_ge(w_set[h], t + 1)
                    pool.nop(nofuse=True)
                    at = DS((BUFS * t + h) * GROUP, GROUP)
                    nc.gpsimd.tensor_copy(index_v[h][:, :], edge["dst"][:, at])
                    nc.gpsimd.tensor_copy(index_u[h][:, :], edge["src"][:, at]).then_inc(index_set[h], 1)
                    pool.wait_ge(index_set[h], t + 1)
                    pool.nop(nofuse=True)
                    for j in range(GROUP):
                        for rows, index, table in ((rows_v, index_v, tab_v), (rows_u, index_u, tab_u)):
                            nc.gpsimd.indirect_dma_start(rows[h][:, j, :], None, table,
                                                         bass.IndirectOffsetOnAxis(ap=index[h][:, j:j + 1], axis=0)).then_inc(gathered[h], 16)

        @block.vector
        def _(dve):
            v = nc.vector
            link = linker(dve, link_s)
            for h in range(BUFS):
                for free in (w_set, turned, z_set, summed):
                    dve.sem_inc(free[h], 1)
            dve.wait_ge(iota_set, 1)
            link(v.tensor_scalar(head_i[:, :], head_i[:, :], R.bit_length() - 1, None, ALU.logical_shift_right))
            link(v.tensor_copy(head_f[:, :], head_i[:, :]))
            v.tensor_scalar(head_sum[:, :], row[:, 0:HEADS], head_f[:, 0:1], None, ALU.is_equal)
            dve.wait_ge(vectors_in, 16 * 2 * HEADS)
            link(v.tensor_scalar(minus_prd[:, :], minus_prd[:, :], -0.5, None, ALU.mult))
            dve.sem_inc(vectors_set, 2)

            def differ(t, h):
                dve.wait_ge(gathered[h], t * (32 * GROUP) + 32 * GROUP)
                dve.wait_ge(summed[h], t + 1)
                v.tensor_tensor(w[h][:, :, :], rows_v[h][:, :, :], rows_u[h][:, :, :], ALU.subtract).then_inc(w_set[h], 1)

            def multiply(t, h):
                dve.wait_ge(slope_set[h], t + 1)
                v.tensor_tensor(slope[h][:, :, :], w_abs[h][:, :, :], slope[h][:, :, :], ALU.mult).then_inc(z_link[h], 1)
                dve.wait_ge(z_link[h], t * 2 + 1)
                v.tensor_tensor(slope[h][:, 0:2, :], slope[h][:, 0:2, :], slope[h][:, 2:4, :], ALU.add).then_inc(z_link[h], 1)
                dve.wait_ge(z_link[h], t * 2 + 2)
                v.tensor_tensor(z_sum[h][:, :], slope[h][:, 0, :], slope[h][:, 1, :], ALU.add).then_inc(z_set[h], 1)

            for h in range(BUFS):
                differ(0, h)
                if h:
                    multiply(0, h - 1)
            with v.Fori(1, TURNS) as t:
                for h in range(BUFS):
                    differ(t, h)
                    multiply(t if h else t - 1, h - 1 if h else BUFS - 1)
            multiply(TURNS - 1, BUFS - 1)

        @block.tensor
        def _(pe):
            pe.wait_ge(vectors_set, 1)

            def transpose(t, h):
                pe.wait_ge(w_set[h], t + 2)
                pe.wait_ge(abs_set[h], t + 1)
                for c in range(KF):
                    for j in range(GROUP):
                        ins = nc.tensor.transpose(ps_w[h][:, c, j * P:(j + 1) * P], w[h][:, j, c * P:(c + 1) * P], ident[:, :])
                ins.then_inc(turned[h], 1)

            def add_heads(t, h):
                pe.wait_ge(z_set[h], t + 2)
                pe.wait_ge(score_kept[h], t + 1)
                nc.tensor.matmul(ps_score[h][:, :], head_sum[:, :], z_sum[h][:, :], start=True, stop=False)
                for j in range(GROUP):
                    ins = nc.tensor.matmul(ps_score[h][:, j * P:(j + 1) * P], w[h][:, j, F:EW], ident[:, :], start=False, stop=j == GROUP - 1)
                ins.then_inc(summed[h], 1)

            for h in range(BUFS):
                transpose(0, h)
                if h:
                    add_heads(0, h - 1)
            with nc.tensor.Fori(1, TURNS) as t:
                for h in range(BUFS):
                    transpose(t, h)
                    add_heads(t if h else t - 1, h - 1 if h else BUFS - 1)
            add_heads(TURNS - 1, BUFS - 1)

        @block.scalar
        def _(act):
            sc = nc.scalar
            for h in range(BUFS):
                for free in (abs_set, score_free, score_kept):
                    act.sem_inc(free[h], 1)
            act.wait_ge(vectors_set, 2)

            def magnitudes(t, h):
                act.wait_ge(turned[h], t + 2)
                act.wait_ge(z_set[h], t + 1)
                sc.activation(w_abs[h][:, :, :], ps_w[h][:, :, :], ACT.Abs).then_inc(abs_set[h], 1)
                act.wait_ge(abs_set[h], t + 2)
                for c in range(KF):
                    ins = sc.activation(slope[h][:, c, :], w_abs[h][:, c, :], ACT.Identity, bias=a_abs[:, c:c + 1], scale=minus_prd[:, c:c + 1])
                ins.then_inc(slope_set[h], 1)

            def keep_scores(t, h):
                act.wait_ge(summed[h], t + 2)
                act.wait_ge(score_free[h], t + 1)
                sc.copy(score[h][:, :], ps_score[h][:, :]).then_inc(score_kept[h], 1)

            for h in range(BUFS):
                magnitudes(0, h)
                if h:
                    keep_scores(0, h - 1)
            with sc.Fori(1, TURNS) as t:
                for h in range(BUFS):
                    magnitudes(t, h)
                    keep_scores(t if h else t - 1, h - 1 if h else BUFS - 1)
            keep_scores(TURNS - 1, BUFS - 1)


def softmax_weights(nc, const, scores, merged, carry, weights, from_left):
    with ExitStack() as ctx:
        def sb(name, shape, dt=F32):
            return ctx.enter_context(nc.sbuf_tensor(name, shape, dt))

        def sem(name):
            return ctx.enter_context(nc.semaphore(name))

        keys = sb("keys", [P, PIECE + 2], I32)
        reset = sb("reset", [P, PIECE + 1])
        alpha, from_right = sb("alpha", [P, PIECE]), sb("from_right", [P, PIECE])
        ends = sb("ends", [P, 4])
        pieces = sb("pieces", [HEADS, CHUNKS, 4])
        state = sb("state", [HEADS, CHUNKS, 2])
        carries, carry_p = sb("carries", [HEADS, CHUNKS, 2]), sb("carry_p", [P, 2])
        ps_t = [ctx.enter_context(nc.psum_tensor(f"ps_weight_t{h}", [P, 512], F32)) for h in range(2)]
        keys_in, scores_in = sem("keys_in"), sem("scores_in")
        link_s, ends_set, ends_out, pieces_in = sem("softmax_link"), sem("ends_set"), sem("ends_out"), sem("pieces_in")
        carries_set, carries_out, carry_in = sem("carries_set"), sem("carries_out"), sem("carry_in")
        shifted, exped = sem("shifted"), sem("exped")
        turned, kept = [sem(f"weights_turned{h}") for h in range(2)], [sem(f"weights_kept{h}") for h in range(2)]
        block = ctx.enter_context(nc.Block())

        @block.sync
        def _(sp):
            sp.dma_start(alpha[:, :], scores.rearrange("h (c x) -> (h c) x", c=CHUNKS)).then_inc(scores_in, 16)
            for h in range(HEADS):
                rows = slice(h * CHUNKS, (h + 1) * CHUNKS)
                sp.dma_start(keys[rows, 1:PIECE + 1], merged[1:1 + EP, :].rearrange("(c x) o -> c (x o)", c=CHUNKS)).then_inc(keys_in, 16)
                sp.dma_start(keys[rows, 0:1], merged[0:EP, :].rearrange("(c x) o -> c (x o)", c=CHUNKS)[:, 0:1], allow_slow_non_contiguous=True).then_inc(keys_in, 16)
                sp.dma_start(keys[rows, PIECE + 1:PIECE + 2],
                             merged[2:2 + EP, :].rearrange("(c x) o -> c (x o)", c=CHUNKS)[:, PIECE - 1:PIECE], allow_slow_non_contiguous=True).then_inc(keys_in, 16)
            sp.wait_ge(ends_set, 1)
            sp.dma_start(carry[0:P, :], ends[:, :]).then_inc(ends_out, 16)
            sp.wait_ge(ends_out, 16)
            sp.dma_start(pieces[:, :, :], carry[0:P, :].rearrange("(h c) k -> h c k", c=CHUNKS)).then_inc(pieces_in, 16)
            sp.wait_ge(carries_set, 1)
            sp.dma_start(carry[P:2 * P, 0:2].rearrange("(h c) k -> h c k", c=CHUNKS), carries[:, :, :]).then_inc(carries_out, 16)
            sp.wait_ge(carries_out, 16)
            sp.dma_start(carry_p[:, :], carry[P:2 * P, 0:2]).then_inc(carry_in, 16)

        @block.vector
        def _(dve):
            v = nc.vector
            link = linker(dve, link_s)
            dve.wait_ge(keys_in, 16 * 3 * HEADS)
            link(v.tensor_scalar(keys[:, :], keys[:, :], KEY.bit_length() - 1, None, ALU.logical_shift_right))
            link(v.tensor_tensor(reset[:, :], keys[:, 1:PIECE + 2], keys[:, 0:PIECE + 1], ALU.not_equal))
            link(v.tensor_scalar(reset[:, :], reset[:, :], -BIG, None, ALU.mult))
            dve.wait_ge(scores_in, 16)
            link(v.scalar_tensor_tensor(alpha[:, :], alpha[:, :], 0.2, alpha[:, :], ALU.mult, ALU.max))

            def scans(left, right):
                v.tensor_tensor_scan(from_left[:, :], reset[:, 0:PIECE], alpha[:, :], left, ALU.add, ALU.max)
                link(v.tensor_tensor_scan(from_right[:, ::-1], reset[:, 1:PIECE + 1][:, ::-1], alpha[:, ::-1], right, ALU.add, ALU.max))

            scans(-BIG, -BIG)
            v.tensor_copy(ends[:, 0:1], from_left[:, PIECE - 1:PIECE])
            v.tensor_copy(ends[:, 1:2], from_right[:, 0:1])
            v.tensor_reduce(ends[:, 2:3], reset[:, 0:PIECE], AX.X, ALU.min)
            v.tensor_reduce(ends[:, 3:4], reset[:, 1:PIECE + 1], AX.X, ALU.min).then_inc(ends_set, 1)
            dve.wait_ge(pieces_in, 16)
            v.tensor_tensor_scan(state[:, :, 0], pieces[:, :, 2], pieces[:, :, 0], -BIG, ALU.add, ALU.max)
            v.tensor_tensor_scan(state[:, ::-1, 1], pieces[:, ::-1, 3], pieces[:, ::-1, 1], -BIG, ALU.add, ALU.max)
            link(v.memset(carries[:, :, :], -BIG))
            v.tensor_copy(carries[:, 1:CHUNKS, 0], state[:, 0:CHUNKS - 1, 0])
            v.tensor_copy(carries[:, 0:CHUNKS - 1, 1], state[:, 1:CHUNKS, 1]).then_inc(carries_set, 1)
            dve.wait_ge(carry_in, 16)
            scans(carry_p[:, 0:1], carry_p[:, 1:2])
            link(v.tensor_tensor(from_left[:, :], from_left[:, :], from_right[:, :], ALU.max))
            v.tensor_tensor(alpha[:, :], alpha[:, :], from_left[:, :], ALU.subtract).then_inc(shifted, 1)

        @block.scalar
        def _(act):
            act.wait_ge(shifted, 1)
            nc.scalar.activation(alpha[:, :], alpha[:, :], ACT.Exp).then_inc(exped, 1)
            for i in range(PT):
                act.wait_ge(turned[i % 2], i // 2 + 1)
                nc.scalar.copy(weights[:, :, i, :], ps_t[i % 2][:, 0:P].rearrange("p (h c) -> p c h", h=HEADS)).then_inc(kept[i % 2], 1)

        @block.tensor
        def _(pe):
            pe.wait_ge(exped, 1)
            for i in range(PT):
                if i >= 2:
                    pe.wait_ge(kept[i % 2], i // 2)
                nc.tensor.transpose(ps_t[i % 2][:, 0:P], alpha[:, i * P:(i + 1) * P], const["ident"][:, :]).then_inc(turned[i % 2], 1)


def gather_messages(nc, const, edge, group_block, weights, tab_e, sums, denominators):
    row = const["row"]
    ITER = GROUPS // 2
    with ExitStack() as ctx:
        def sb(name, shape, dt=F32):
            return ctx.enter_context(nc.sbuf_tensor(name, shape, dt))

        def sem(name):
            return ctx.enter_context(nc.semaphore(name))

        def sems(name):
            return [sem(f"{name}{h}") for h in range(2)]

        def sbs(name, shape, dt=F32):
            return [sb(f"{name}{h}", shape, dt) for h in range(2)]

        index = sbs("index_e", [P, GROUP], I32)
        rows, messages = sbs("rows_e", [P, GROUP, F]), sbs("messages", [P, GROUP, F])
        onehot = sbs("node_onehot", [P, GROUP, L])
        ps_sum = [ctx.enter_context(nc.psum_tensor(f"ps_sum{h}", [L, F], F32)) for h in range(2)]
        ps_den = [ctx.enter_context(nc.psum_tensor(f"ps_den{h}", [L, 512], F32)) for h in range(2)]
        index_set, gathered, messages_set, summed, added = (sems(n) for n in ("e_index_set", "e_gathered", "messages_set", "e_summed", "e_added"))
        link_s = sem("gather_link")
        tile_weights = weights[:, :, :, :].rearrange("p c i h -> p (c i) h")
        block = ctx.enter_context(nc.Block())

        @block.gpsimd
        def _(pool):
            with nc.gpsimd.Fori(0, ITER) as t:
                for h in range(2):
                    pool.wait_ge(messages_set[h], t + 1)
                    pool.nop(nofuse=True)
                    nc.gpsimd.tensor_copy(index[h][:, :], edge["dst"][:, DS((2 * t + h) * GROUP, GROUP)]).then_inc(index_set[h], 1)
                    pool.wait_ge(index_set[h], t + 1)
                    pool.nop(nofuse=True)
                    for j in range(GROUP):
                        nc.gpsimd.indirect_dma_start(rows[h][:, j, :], None, tab_e,
                                                     bass.IndirectOffsetOnAxis(ap=index[h][:, j:j + 1], axis=0)).then_inc(gathered[h], 16)

        @block.vector
        def _(dve):
            v = nc.vector
            link = linker(dve, link_s)
            v.memset(denominators[:, :, :], 0.0)
            link(v.memset(sums[:, :, :], 0.0))
            for h in range(2):
                for free in (messages_set, summed, added):
                    dve.sem_inc(free[h], 1)

            def weigh(t, h):
                dve.wait_ge(summed[h], t + 1)
                for j in range(GROUP):
                    v.tensor_scalar(onehot[h][:, j, :], row[:, 0:L], edge["local"][:, DS((2 * t + h) * GROUP + j, 1)], None, ALU.is_equal)
                dve.wait_ge(gathered[h], t * (16 * GROUP) + 16 * GROUP)
                w = tile_weights[:, DS((2 * t + h) * GROUP, GROUP), :].rearrange("p j h -> p (j h)")
                v.tensor_tensor(messages[h][:, :, :].rearrange("p j (h d) -> p (j h) d", d=D),
                                rows[h][:, :, :].rearrange("p j (h d) -> p (j h) d", d=D),
                                w.unsqueeze(2).broadcast_to([P, GROUP * HEADS, D]), ALU.mult).then_inc(messages_set[h], 1)

            def add_up(t, h):
                b = dve.value_load(group_block[0:1, DS(2 * t + h, 1)], min_val=0, max_val=NB - 1)
                dve.wait_ge(summed[h], t + 2)
                dve.wait_ge(added[1 - h], t + 1 + h)
                total = sums[:, DS(b, 1), :].rearrange("p o f -> p (o f)")
                v.tensor_tensor(total, ps_sum[h][:, :], total, ALU.add)
                den = denominators[:, DS(b, 1), :].rearrange("p o h -> p (o h)")
                v.tensor_tensor(den, ps_den[h][:, 0:HEADS], den, ALU.add).then_inc(added[h], 1)

            weigh(0, 0)
            weigh(0, 1)
            add_up(0, 0)
            with v.Fori(1, ITER) as t:
                weigh(t, 0)
                add_up(t - 1, 1)
                weigh(t, 1)
                add_up(t, 0)
            add_up(ITER - 1, 1)

        @block.tensor
        def _(pe):
            with nc.tensor.Fori(0, ITER) as t:
                for h in range(2):
                    pe.wait_ge(messages_set[h], t + 2)
                    pe.wait_ge(added[h], t + 1)
                    for j in range(GROUP):
                        nc.tensor.matmul(ps_sum[h][:, :], onehot[h][:, j, :], messages[h][:, j, :], start=j == 0, stop=j == GROUP - 1)
                        ins = nc.tensor.matmul(ps_den[h][:, 0:HEADS], onehot[h][:, j, :],
                                               tile_weights[:, DS((2 * t + h) * GROUP + j, 1), :].rearrange("p o h -> p (o h)"),
                                               start=j == 0, stop=j == GROUP - 1)
                    ins.then_inc(summed[h], 1)


def transpose_ffn_weights(nc, a, const, ffn):
    ident = const["ident"]
    IH = INNER // P
    with ExitStack() as ctx:
        def sem(name):
            return ctx.enter_context(nc.semaphore(name))

        up = [ctx.enter_context(nc.sbuf_tensor(f"up_rows{i}", [P, IH, F], F32)) for i in range(2)]
        down = ctx.enter_context(nc.sbuf_tensor("down_rows", [P, KF, INNER], F32))
        ps_w = [ctx.enter_context(nc.psum_tensor(f"ps_weight{i}", [P, 512], F32)) for i in range(6)]
        loaded, turned, kept, freed = sem("ffn_loaded"), sem("ffn_turned"), sem("ffn_kept"), sem("ffn_freed")
        ROUNDS = EXPERTS + 1
        block = ctx.enter_context(nc.Block())

        @block.sync
        def _(sp):
            with nc.sync.Fori(0, EXPERTS) as e:
                sp.wait_ge(freed, e + 1)
                for rows, name in ((up[0], "L0_ffn_w1"), (up[1], "L0_ffn_w3")):
                    sp.dma_start(rows[:, :, :], a[name][DS(e, 1), :, :].rearrange("o (i p) f -> p (o i) f", p=P)).then_inc(loaded, 16)
                sp.dma_start(down[:, :, :], a["L0_ffn_w2"][DS(e, 1), :, :].rearrange("o (k p) i -> p (o k) i", p=P)).then_inc(loaded, 16)
            sp.wait_ge(freed, EXPERTS + 1)
            sp.dma_start(up[0][:, :, :], a["L0_ffn_sw1"].rearrange("(i p) f -> p i f", p=P)).then_inc(loaded, 16)
            sp.dma_start(up[1][0:EXPERTS, 0, :], a["L0_ffn_gate_w"]).then_inc(loaded, 16)
            sp.dma_start(down[:, :, :], a["L0_ffn_sw2"].rearrange("(k p) i -> p k i", p=P)).then_inc(loaded, 16)

        def turn(pe, both):
            banks = iter(ps_w)
            for i in range(2 if both else 1):
                for half in range(IH):
                    bank = next(banks)
                    for k in range(KF):
                        nc.tensor.transpose(bank[:, k * P:(k + 1) * P], up[i][:, half, k * P:(k + 1) * P], ident[:, :])
            for half in range(IH):
                bank = next(banks)
                for k in range(KF):
                    ins = nc.tensor.transpose(bank[:, k * P:(k + 1) * P], down[:, k, half * P:(half + 1) * P], ident[:, :])
            return ins

        @block.tensor
        def _(pe):
            pe.sem_inc(freed, 1)
            pe.sem_inc(turned, 1)
            with nc.tensor.Fori(0, EXPERTS) as e:
                pe.wait_ge(loaded, e * 48 + 48)
                pe.wait_ge(kept, e + 1)
                turn(pe, True).then_inc(turned, 1)
                pe.wait_ge(turned, e + 2)
                pe.sem_inc(freed, 1)
            pe.wait_ge(loaded, ROUNDS * 48)
            pe.wait_ge(kept, EXPERTS + 1)
            for k in range(KF):
                nc.tensor.transpose(ps_w[5][:, k * EXPERTS:(k + 1) * EXPERTS], up[1][0:EXPERTS, 0, k * P:(k + 1) * P], ident[0:EXPERTS, 0:EXPERTS])
            turn(pe, False).then_inc(turned, 1)

        @block.scalar
        def _(act):
            act.sem_inc(kept, 1)
            sc = nc.scalar
            with sc.Fori(0, EXPERTS) as e:
                act.wait_ge(turned, e + 2)
                for i in range(2):
                    for half in range(IH):
                        at = i * INNER + half * P
                        sc.copy(ffn["up"][:, :, DS(e, 1), at:at + P].rearrange("p k o n -> p k (o n)"),
                                ps_w[i * IH + half][:, :].rearrange("p (k n) -> p k n", k=KF))
                for half in range(IH):
                    ins = sc.activation(ffn["down"][:, DS(e, 1), half, :].rearrange("p o f -> p (o f)"), ps_w[2 * IH + half][:, :], ACT.Copy, scale=0.5)
                ins.then_inc(kept, 1)
            act.wait_ge(turned, ROUNDS + 1)
            for half in range(IH):
                sc.copy(ffn["shared_up"][:, :, half * P:(half + 1) * P], ps_w[half][:, :].rearrange("p (k n) -> p k n", k=KF))
                sc.copy(ffn["shared_down"][:, half, :], ps_w[IH + half][:, :])
            sc.copy(ffn["gate"][:, :, :], ps_w[5][:, 0:KF * EXPERTS].rearrange("p (k e) -> p k e", k=KF))


def route_tokens(nc, const, ffn, x_sb, sums, denominators, tokens, tab_x, lists):
    ident, tri, ones, row, eps = (const[k] for k in ("ident", "tri", "ones", "row", "eps"))
    xn2 = sums
    with ExitStack() as ctx:
        def sb(name, shape, dt=F32):
            return ctx.enter_context(nc.sbuf_tensor(name, shape, dt))

        def ps(name, shape):
            return ctx.enter_context(nc.psum_tensor(name, shape, F32))

        def sem(name):
            return ctx.enter_context(nc.semaphore(name))

        inverse = sb("inverse", [L, NB * HEADS])
        stats, moments = sb("stats2", [L, NB, 6]), sb("moments2", [L, NB, 2])
        deviation, rstd = sb("deviation2", [L, NB]), sb("rstd2", [L, NB])
        staged = sb("xn2_tile", [L, F])
        xn2_t = sb("xn2_t", [P, KF, L])
        logits = sb("logits", [L, NB, EXPERTS])
        best, chosen = sb("best_logit", [L, NB]), sb("chosen", [L, NB])
        is_best, candidate = sb("is_best", [L, NB, EXPERTS]), sb("candidate", [L, NB, EXPERTS])
        far = sb("far_iota", [L, EXPERTS])
        routed, running, ahead = sb("routed", [L, NB, EXPERTS]), sb("running", [L, NB, EXPERTS]), sb("ahead_tiles", [L, NB, EXPERTS])
        zeros = sb("zeros_nb", [L, NB])
        tiles_i, tiles_f = sb("tiles_i", [L, EXPERTS], I32), sb("tiles_f", [L, EXPERTS])
        tile_end, tile_start = sb("tile_end", [L, EXPERTS]), sb("tile_start", [L, EXPERTS])
        slot_f = sb("token_slot_f", [L, NB])
        tile_cmp, tile_sum = sb("tile_cmp", [1, TOKEN_TILES, EXPERTS]), sb("tile_sum", [1, TOKEN_TILES])
        tile_iota = sb("tile_iota", [1, TOKEN_TILES])
        fill = sb("token_fill", [P, TOKEN_TILES], I32)
        ids = sb("token_ids", [L, NB], I32)
        listed = sb("listed", [TOKEN_TILES, RECS, P], I32)
        listed_f = sb("listed_f", [TOKEN_TILES, P])
        ps_t, ps_logit, ps_slot, ps_total, ps_ids = ps("ps_t2", [P, 512]), ps("ps_logit", [L, 512]), ps("ps_tslot", [L, 512]), ps("ps_ttotal", [L, 512]), ps("ps_ids", [P, 512])
        names = ("link var dev xn2_set xn2_out staged_set turned kept logit_done logit_kept prefix_set counted slots_set "
                 "filled fill_out listed_in listed_set ids_turned iotas").split()
        s = {n: sem(f"route_{n}") for n in names}
        written = [sem(f"ids_written{j}") for j in range(RECS)]
        scattered = sem("ids_scattered")
        block = ctx.enter_context(nc.Block())

        @block.sync
        def _(sp):
            sp.wait_ge(s["filled"], 1)
            for one in lists:
                sp.dma_start(one.rearrange("(p c) o -> p (c o)", c=TOKEN_TILES), fill[:, :]).then_inc(s["fill_out"], 16)
            sp.wait_ge(s["xn2_set"], 1)
            sp.dma_start(tab_x.rearrange("(t p) f -> p t f", p=L), xn2[:, :, :]).then_inc(s["xn2_out"], 16)
            sp.wait_ge(scattered, 1)
            for j, one in enumerate(lists):
                sp.dma_start(listed[:, j, :], one.rearrange("(c p) o -> c (p o)", p=P)).then_inc(s["listed_in"], 16)
            sp.wait_ge(s["xn2_out"], 16)

        @block.gpsimd
        def _(pool):
            nc.gpsimd.memset(fill[:, :], PAD_RECORD).then_inc(s["filled"], 1)
            nc.gpsimd.iota(ids[:, :], pattern=[[L, NB]], base=0, channel_multiplier=1)
            nc.gpsimd.iota(tile_iota[:, :], pattern=[[1, TOKEN_TILES]], base=0, channel_multiplier=0, allow_small_or_imprecise_dtypes=True).then_inc(s["iotas"], 1)
            pool.wait_ge(s["iotas"], 1)
            pool.wait_ge(s["fill_out"], 16 * RECS)
            pool.wait_ge(s["slots_set"], 1)
            for t in range(NB):
                j = t % RECS
                if t >= RECS:
                    pool.wait_ge(written[j], 16 * (t // RECS))
                nc.gpsimd.indirect_dma_start(lists[j], bass.IndirectOffsetOnAxis(ap=tokens["slot"][:, t:t + 1], axis=0),
                                             ids[:, t:t + 1], None).then_inc(written[j], 16)
            for j in range(RECS):
                pool.wait_ge(written[j], 16 * (NB // RECS))
            pool.sem_inc(scattered, 1)

        @block.vector
        def _(dve):
            v = nc.vector
            link = linker(dve, s["link"])
            for n in ("turned", "logit_kept"):
                dve.sem_inc(s[n], 1)
            den = denominators[:, :, :].rearrange("p b h -> p (b h)")
            link(v.tensor_scalar(inverse[:, :], den, 1e-16, None, ALU.add))
            link(v.reciprocal(inverse[:, :], inverse[:, :]))
            by_head = sums[:, :, :].rearrange("p b (h d) -> p (b h) d", d=D)
            link(v.tensor_tensor(by_head, by_head, inverse[:, :].unsqueeze(2).broadcast_to([L, NB * HEADS, D]), ALU.mult))
            link(v.tensor_tensor(x_sb[:, :, :], x_sb[:, :, :], sums[:, :, :], ALU.add))
            for t in range(NB):
                ins = v.bn_stats(stats[:, t, :], x_sb[:, t, :])
            link(ins)
            for t in range(NB):
                ins = v.bn_aggr(moments[:, t, :], stats[:, t, :])
            ins.then_inc(s["var"], 1)
            dve.wait_ge(s["dev"], 1)
            link(v.reciprocal(rstd[:, :], deviation[:, :]))
            for t in range(NB):
                ins = v.tensor_scalar(xn2[:, t, :], x_sb[:, t, :], moments[:, t, 0:1], rstd[:, t:t + 1], ALU.subtract, ALU.mult)
            link(ins)
            dve.sem_inc(s["xn2_set"], 1)
            with v.Fori(0, NB) as t:
                dve.wait_ge(s["turned"], t + 1)
                v.tensor_copy(staged[:, :], xn2[:, DS(t, 1), :].rearrange("p o f -> p (o f)")).then_inc(s["staged_set"], 1)
                dve.wait_ge(s["logit_done"], t + 1)
                v.tensor_copy(logits[:, DS(t, 1), :].rearrange("p o e -> p (o e)"), ps_logit[:, 0:EXPERTS]).then_inc(s["logit_kept"], 1)
            dve.wait_ge(s["logit_kept"], NB + 1)
            shape = [L, NB, EXPERTS]
            iota = row[0:L, 0:EXPERTS].unsqueeze(1).broadcast_to(shape)
            link(v.tensor_reduce(best[:, :], logits[:, :, :], AX.X, ALU.max))
            link(v.tensor_tensor(is_best[:, :, :], logits[:, :, :], best[:, :].unsqueeze(2).broadcast_to(shape), ALU.is_equal))
            link(v.tensor_scalar(far[:, :], row[0:L, 0:EXPERTS], float(EXPERTS), None, ALU.add))
            link(v.tensor_scalar(is_best[:, :, :], is_best[:, :, :], -float(EXPERTS), None, ALU.mult))
            link(v.tensor_tensor(candidate[:, :, :], is_best[:, :, :], far[:, :].unsqueeze(1).broadcast_to(shape), ALU.add))
            link(v.tensor_reduce(chosen[:, :], candidate[:, :, :], AX.X, ALU.min))
            link(v.tensor_tensor(routed[:, :, :], iota, chosen[:, :].unsqueeze(2).broadcast_to(shape), ALU.is_equal))
            link(v.memset(zeros[:, :], 0.0))
            for e in range(EXPERTS):
                ins = v.tensor_tensor_scan(running[:, :, e], routed[:, :, e], zeros[:, :], 0.0, ALU.add, ALU.add)
            link(ins)
            v.tensor_tensor(ahead[:, :, :], running[:, :, :], routed[:, :, :], ALU.subtract).then_inc(s["prefix_set"], 1)
            dve.wait_ge(s["counted"], 1)
            link(v.tensor_scalar(tiles_i[:, :], ps_total[:, 0:EXPERTS], float(P - 1), None, ALU.add))
            link(v.tensor_scalar(tiles_i[:, :], tiles_i[:, :], P.bit_length() - 1, None, ALU.logical_shift_right))
            link(v.tensor_copy(tiles_f[:, :], tiles_i[:, :]))
            link(v.tensor_tensor_scan(tile_end[:, :], tiles_f[:, :], zeros[:, 0:EXPERTS], 0.0, ALU.add, ALU.add))
            link(v.tensor_tensor(tile_start[:, :], tile_end[:, :], tiles_f[:, :], ALU.subtract))
            dve.wait_ge(s["iotas"], 1)
            link(v.tensor_tensor(tile_cmp[:, :, :], tile_iota[:, :].unsqueeze(2).broadcast_to([1, TOKEN_TILES, EXPERTS]),
                                 tile_start[0:1, :].unsqueeze(1).broadcast_to([1, TOKEN_TILES, EXPERTS]), ALU.is_ge))
            link(v.tensor_reduce(tile_sum[:, :], tile_cmp[:, :, 1:EXPERTS], AX.X, ALU.add))
            v.tensor_copy(tokens["expert"][:, :], tile_sum[:, :])
            link(v.tensor_scalar(tile_start[:, :], tile_start[:, :], float(P), None, ALU.mult))
            link(v.tensor_tensor(candidate[:, :, :], ps_slot[:, 0:NB * EXPERTS].rearrange("p (t e) -> p t e", e=EXPERTS),
                                 tile_start[:, :].unsqueeze(1).broadcast_to(shape), ALU.add))
            link(v.tensor_tensor(candidate[:, :, :], candidate[:, :, :], routed[:, :, :], ALU.mult))
            link(v.tensor_reduce(slot_f[:, :], candidate[:, :, :], AX.X, ALU.add))
            v.tensor_copy(tokens["slot"][:, :], slot_f[:, :]).then_inc(s["slots_set"], 1)
            dve.wait_ge(s["listed_in"], 16 * RECS)
            link(v.tensor_tensor(listed_f[:, :], listed[:, 0, :], listed[:, 1, :], ALU.min))
            for j in range(2, RECS):
                link(v.tensor_tensor(listed_f[:, :], listed_f[:, :], listed[:, j, :], ALU.min))
            v.tensor_scalar(listed_f[:, :], listed_f[:, :], float(N - 1), None, ALU.min).then_inc(s["listed_set"], 1)
            dve.wait_ge(s["ids_turned"], 1)
            v.tensor_copy(tokens["id"][:, :], ps_ids[:, 0:TOKEN_TILES])

        @block.tensor
        def _(pe):
            with nc.tensor.Fori(0, NB) as t:
                pe.wait_ge(s["staged_set"], t + 1)
                pe.wait_ge(s["kept"], t + 1)
                for k in range(KF):
                    ins = nc.tensor.transpose(ps_t[:, k * L:(k + 1) * L], staged[:, k * P:(k + 1) * P], ident[0:L, 0:L])
                ins.then_inc(s["turned"], 1)
                pe.wait_ge(s["kept"], t + 2)
                pe.wait_ge(s["logit_kept"], t + 1)
                for k in range(KF):
                    ins = nc.tensor.matmul(ps_logit[:, 0:EXPERTS], xn2_t[:, k, :], ffn["gate"][:, k, :], start=k == 0, stop=k == KF - 1)
                ins.then_inc(s["logit_done"], 1)
            pe.wait_ge(s["prefix_set"], 1)
            cols = NB * EXPERTS
            nc.tensor.matmul(ps_slot[:, 0:cols], tri[0:L, 0:L], routed[:, :, :].rearrange("p t e -> p (t e)"), start=True, stop=False)
            nc.tensor.matmul(ps_slot[:, 0:cols], ones[0:L, 0:L], ahead[:, :, :].rearrange("p t e -> p (t e)"), start=False, stop=True)
            nc.tensor.matmul(ps_total[:, 0:EXPERTS], ones[0:L, 0:L], running[:, NB - 1, :], start=True, stop=True).then_inc(s["counted"], 1)
            pe.wait_ge(s["listed_set"], 1)
            nc.tensor.transpose(ps_ids[:, 0:TOKEN_TILES], listed_f[:, :], ident[0:TOKEN_TILES, 0:TOKEN_TILES]).then_inc(s["ids_turned"], 1)

        @block.scalar
        def _(act):
            act.sem_inc(s["kept"], 1)
            act.wait_ge(s["var"], 1)
            nc.scalar.activation(deviation[:, :], moments[:, :, 1], ACT.Sqrt, bias=eps[0:L, 0:1]).then_inc(s["dev"], 1)
            with nc.scalar.Fori(0, NB) as t:
                act.wait_ge(s["turned"], t + 2)
                nc.scalar.copy(xn2_t[:, :, :], ps_t[:, 0:KF * L].rearrange("p (k n) -> p k n", k=KF)).then_inc(s["kept"], 1)


def run_experts(nc, const, ffn, tokens, tab_x, tab_y):
    ident = const["ident"]
    with ExitStack() as ctx:
        def sb(name, shape, dt=F32):
            return ctx.enter_context(nc.sbuf_tensor(name, shape, dt))

        def ps(name):
            return ctx.enter_context(nc.psum_tensor(name, [P, F], F32))

        def sem(name):
            return ctx.enter_context(nc.semaphore(name))

        index, rows = sb("token_index", [P, 1], I32), sb("token_rows", [P, F])
        x_t, hidden_t = sb("token_x_t", [P, KF, P]), sb("hidden_t", [P, KF, P])
        gate = sb("swiglu_gate", [P, INNER])
        hidden, y = sb("hidden", [P, F]), sb("token_y", [P, F])
        ps_t, ps_up, ps_shared, ps_h, ps_y = ps("ps_tx"), ps("ps_up"), ps("ps_shared"), ps("ps_hidden"), ps("ps_y")
        names = "index_set gathered turned kept up_done act_set gated gelu_set hidden_set h_turned h_kept y_done y_kept y_free y_out".split()
        s = {n: sem(f"expert_{n}") for n in names}
        block = ctx.enter_context(nc.Block())

        @block.sync
        def _(sp):
            with nc.sync.Fori(0, TOKEN_TILES) as t:
                sp.wait_ge(s["y_kept"], t + 2)
                sp.dma_start(tab_y[DS(t * P, P), :], y[:, :]).then_inc(s["y_out"], 16)
                sp.wait_ge(s["y_out"], t * 16 + 16)
                sp.sem_inc(s["y_free"], 1)

        @block.gpsimd
        def _(pool):
            with nc.gpsimd.Fori(0, TOKEN_TILES) as t:
                pool.wait_ge(s["turned"], t + 1)
                pool.nop(nofuse=True)
                nc.gpsimd.tensor_copy(index[:, :], tokens["id"][:, DS(t, 1)]).then_inc(s["index_set"], 1)
                pool.wait_ge(s["index_set"], t + 1)
                pool.nop(nofuse=True)
                nc.gpsimd.indirect_dma_start(rows[:, :], None, tab_x, bass.IndirectOffsetOnAxis(ap=index[:, 0:1], axis=0)).then_inc(s["gathered"], 16)

        @block.vector
        def _(dve):
            v = nc.vector
            for n in ("turned", "h_turned", "hidden_set"):
                dve.sem_inc(s[n], 1)
            with v.Fori(0, TOKEN_TILES) as t:
                dve.wait_ge(s["act_set"], t + 1)
                v.scalar_tensor_tensor(gate[:, :], gate[:, :], 1.0, ps_up[:, 0:INNER], ALU.add, ALU.mult).then_inc(s["gated"], 1)
                dve.wait_ge(s["gated"], t + 1)
                dve.wait_ge(s["h_turned"], t + 1)
                v.tensor_tensor(hidden[:, 0:INNER], ps_up[:, INNER:2 * INNER], gate[:, :], ALU.mult).then_inc(s["hidden_set"], 1)

        @block.tensor
        def _(pe):
            with nc.tensor.Fori(0, TOKEN_TILES) as t:
                e = pe.value_load(tokens["expert"][0:1, DS(t, 1)], min_val=0, max_val=EXPERTS - 1)
                pe.wait_ge(s["gathered"], t * 16 + 16)
                pe.wait_ge(s["kept"], t + 1)
                for k in range(KF):
                    ins = nc.tensor.transpose(ps_t[:, k * P:(k + 1) * P], rows[:, k * P:(k + 1) * P], ident[:, :])
                ins.then_inc(s["turned"], 1)
                pe.wait_ge(s["kept"], t + 2)
                pe.wait_ge(s["hidden_set"], t + 1)
                for k in range(KF):
                    nc.tensor.matmul(ps_up[:, :], x_t[:, k, :], ffn["up"][:, k, DS(e, 1), :].rearrange("p o n -> p (o n)"), start=k == 0, stop=k == KF - 1)
                for k in range(KF):
                    ins = nc.tensor.matmul(ps_shared[:, 0:INNER], x_t[:, k, :], ffn["shared_up"][:, k, :], start=k == 0, stop=k == KF - 1)
                ins.then_inc(s["up_done"], 1)
                pe.wait_ge(s["hidden_set"], t + 2)
                pe.wait_ge(s["gelu_set"], t + 1)
                pe.wait_ge(s["h_kept"], t + 1)
                for k in range(KF):
                    ins = nc.tensor.transpose(ps_h[:, k * P:(k + 1) * P], hidden[:, k * P:(k + 1) * P], ident[:, :])
                ins.then_inc(s["h_turned"], 1)
                pe.wait_ge(s["h_kept"], t + 2)
                pe.wait_ge(s["y_kept"], t + 1)
                for half in range(INNER // P):
                    nc.tensor.matmul(ps_y[:, :], hidden_t[:, half, :], ffn["down"][:, DS(e, 1), half, :].rearrange("p o f -> p (o f)"), start=half == 0, stop=False)
                for half in range(INNER // P):
                    ins = nc.tensor.matmul(ps_y[:, :], hidden_t[:, INNER // P + half, :], ffn["shared_down"][:, half, :], start=False, stop=half == INNER // P - 1)
                ins.then_inc(s["y_done"], 1)

        @block.scalar
        def _(act):
            sc = nc.scalar
            for n in ("kept", "h_kept", "y_kept", "y_free"):
                act.sem_inc(s[n], 1)
            with sc.Fori(0, TOKEN_TILES) as t:
                act.wait_ge(s["turned"], t + 2)
                sc.copy(x_t[:, :, :].rearrange("p k n -> p (k n)"), ps_t[:, :]).then_inc(s["kept"], 1)
                act.wait_ge(s["up_done"], t + 1)
                act.wait_ge(s["hidden_set"], t + 1)
                sc.activation(gate[:, :], ps_up[:, 0:INNER], ACT.Tanh, scale=0.5).then_inc(s["act_set"], 1)
                act.wait_ge(s["h_turned"], t + 1)
                sc.activation(hidden[:, INNER:2 * INNER], ps_shared[:, 0:INNER], ACT.Gelu).then_inc(s["gelu_set"], 1)
                act.wait_ge(s["h_turned"], t + 2)
                sc.copy(hidden_t[:, :, :].rearrange("p k n -> p (k n)"), ps_h[:, :]).then_inc(s["h_kept"], 1)
                act.wait_ge(s["y_done"], t + 1)
                act.wait_ge(s["y_free"], t + 1)
                sc.copy(y[:, :], ps_y[:, :]).then_inc(s["y_kept"], 1)


def write_result(nc, tokens, x_sb, tab_y, out):
    BUFFERS = 4
    with ExitStack() as ctx:
        back = [ctx.enter_context(nc.sbuf_tensor(f"back{i}", [L, F], F32)) for i in range(BUFFERS)]
        gathered = [ctx.enter_context(nc.semaphore(f"y_gathered{i}")) for i in range(BUFFERS)]
        added, stored = ctx.enter_context(nc.semaphore("y_added")), ctx.enter_context(nc.semaphore("stored"))
        block = ctx.enter_context(nc.Block())

        @block.gpsimd
        def _(pool):
            for t in range(NB):
                if t >= BUFFERS:
                    pool.wait_ge(added, t - BUFFERS + 1)
                nc.gpsimd.indirect_dma_start(back[t % BUFFERS][:, :], None, tab_y,
                                             bass.IndirectOffsetOnAxis(ap=tokens["slot"][:, t:t + 1], axis=0)).then_inc(gathered[t % BUFFERS], 16)

        @block.vector
        def _(dve):
            for t in range(NB):
                dve.wait_ge(gathered[t % BUFFERS], 16 * (t // BUFFERS + 1))
                nc.vector.tensor_add(x_sb[:, t, :], x_sb[:, t, :], back[t % BUFFERS][:, :]).then_inc(added, 1)

        @block.sync
        def _(sp):
            PER = 4
            for t in range(0, NB, PER):
                sp.wait_ge(added, t + PER)
                sp.dma_start(out[t * L:(t + PER) * L, :].rearrange("(t p) f -> p t f", p=L), x_sb[:, t:t + PER, :]).then_inc(stored, 16)
            sp.wait_ge(stored, 16 * (NB // PER))

def program(nc, a, out):
    def dram(name, shape, dt=F32):
        return nc.dram_tensor(name, shape, dt, kind="Internal").ap()

    recs = [dram(f"records{j}", [REC_ROWS, 1], I32) for j in range(RECS)]
    merged = dram("sorted_records", [EP + 2, 1], I32)
    tab_v, tab_u, tab_e = dram("target_rows", [N, EW]), dram("source_rows", [N, EW]), dram("message_rows", [N, F])
    tab_x, tab_y = dram("token_rows_in", [N, F]), dram("token_rows_out", [TOK_ROWS, F])
    token_lists = [dram(f"token_list{j}", [TOK_ROWS, 1], I32) for j in range(RECS)]
    scores, carry = dram("scores", [HEADS, EP]), dram("carry", [2 * P, 4])
    with ExitStack() as ctx:
        def sb(name, shape, dt=F32):
            return ctx.enter_context(nc.sbuf_tensor(name, shape, dt))

        def sem(name):
            return ctx.enter_context(nc.semaphore(name))

        const = make_constants(nc, sb)
        keep = {"key": sb("key", [L, ET], I32), "slot": sb("slot", [L, ET], I32), "group_block": sb("group_block", [1, GROUPS], I32),
                "scatter_slot": [sb(f"scatter_slot{h}", [L, RECS], I32) for h in range(2)],
                "scatter_key": [sb(f"scatter_key{h}", [L, RECS], I32) for h in range(2)]}
        written = [sem(f"records_written{j}") for j in range(RECS)]
        sort_edges(nc, a["src"], a["dst"], recs, written, const, keep)
        x_sb = sb("x_sb", [L, NB, F])
        project_and_mix(nc, a, const, keep, x_sb, recs, written, tab_v, tab_u, tab_e)
        sums_space, denominators = sb("sums", [P, NB * F]), sb("denominators", [L, NB, HEADS])
        sums = sums_space[0:L, :].rearrange("p (b f) -> p b f", b=NB)
        edge_ctx = ExitStack()

        def sb_edge(name, shape, dt=F32):
            return edge_ctx.enter_context(nc.sbuf_tensor(name, shape, dt))

        edge = {"dst": sb_edge("edge_dst", [P, ST], I32), "src": sb_edge("edge_src", [P, ST], I32), "local": sb_edge("edge_local", [P, ST])}
        read_sorted_edges(nc, const, recs, merged, edge)
        score_edges(nc, a, const, edge, tab_v, tab_u, scores)
        weights = sb_edge("weights", [P, CHUNKS, PT, HEADS])
        softmax_weights(nc, const, scores, merged, carry, weights, sums_space[:, 0:PIECE])
        gather_messages(nc, const, edge, keep["group_block"], weights, tab_e, sums, denominators)
        edge_ctx.close()
        ffn = {"up": sb("up_t", [P, KF, EXPERTS, 2 * INNER]), "down": sb("down_t", [P, EXPERTS, INNER // P, F]),
               "shared_up": sb("shared_up_t", [P, KF, INNER]), "shared_down": sb("shared_down_t", [P, INNER // P, F]),
               "gate": sb("gate_t", [P, KF, EXPERTS])}
        tokens = {"slot": sb("token_slot", [L, NB], I32), "expert": sb("token_expert", [1, TOKEN_TILES], I32), "id": sb("token_id", [P, TOKEN_TILES], I32)}
        transpose_ffn_weights(nc, a, const, ffn)
        route_tokens(nc, const, ffn, x_sb, sums, denominators, tokens, tab_x, token_lists)
        run_experts(nc, const, ffn, tokens, tab_x, tab_y)
        write_result(nc, tokens, x_sb, tab_y, out)

_INS = ['x', 'src', 'dst', 'L0_gnn_W_e', 'L0_gnn_W_r', 'L0_gnn_a', 'L0_mix_W_in', 'L0_mix_b_in', 'L0_mix_Wq',
        'L0_mix_Wk', 'L0_mix_Wv', 'L0_mix_W_out', 'L0_mix_b_out', 'L0_ffn_gate_w', 'L0_ffn_w1', 'L0_ffn_w2',
        'L0_ffn_w3', 'L0_ffn_sw1', 'L0_ffn_sw2']


def kernel(**inputs):
    import numpy as _np
    import concourse.bacc as _bacc
    from concourse import mybir as _mybir
    from concourse.bass_utils import run_bass_kernel_spmd as _run

    nc = _bacc.Bacc("TRN2", target_bir_lowering=False, num_devices=1)
    arrays, args = {}, {}
    for name in _INS:
        a = _np.ascontiguousarray(inputs[name])
        arrays[f"in_{name}_dram"] = a
        args[name] = nc.dram_tensor(f"in_{name}_dram", a.shape, _mybir.dt.from_np(a.dtype), kind="ExternalInput").ap()
    out = nc.dram_tensor("out_0_dram", (2500, 512), _mybir.dt.float32, kind="ExternalOutput").ap()
    program(nc, args, out)
    r = _run(nc, [arrays], core_ids=[0])
    return r.results[0]["out_0_dram"]
```

```python
import concourse.bass as bass
from concourse import mybir
from contextlib import ExitStack

F32 = mybir.dt.float32
BF16 = mybir.dt.bfloat16
I32 = mybir.dt.int32
ALU = mybir.AluOpType
ACT = mybir.ActivationFunctionType
AX = mybir.AxisListType


N, E, F, HEADS, D = 2500, 80000, 512, 8, 64
SLICE, EXPERTS, INNER = 32, 8, 256
P = 128
L = 125
NB = N // L
KF = F // P
ET = E // L
BUFS = 4
CH = 4
GROUP = 2
GE = GROUP * P
CHUNKS = P // HEADS
MAX_GROUPS = (E + NB * (GE - 1)) // GE
PIECE_GROUPS = -(-MAX_GROUPS // CHUNKS)
GROUPS = PIECE_GROUPS * CHUNKS
ST = GROUPS * GROUP
EP = ST * P
PIECE = EP // CHUNKS
PT = PIECE // P
REC_COLS = -(-(EP + 2) // P)
REC_ROWS = REC_COLS * P
KEY = 4096
PAD_RECORD = (KEY - 1) * KEY
ROUND = 12582912.0
TOKEN_TILES = (N + EXPERTS * (P - 1)) // P
TOK_ROWS = TOKEN_TILES * P
R = D // KF
PARTS = 3
PART_LOADS = 4
EW = F + HEADS
MIDDLE = float(EP // 2 // 256 * 256)
RECS = 4
STAGED_TILES = 16
PER_LIST = STAGED_TILES // RECS
SCATTERS = ET // STAGED_TILES // 2
SORT_SCATTERS = 8
BIG = 1e38


def linker(eng, sem, base=0):
    count = [0]

    def link(ins):
        count[0] += 1
        ins.then_inc(sem, 1)
        eng.wait_ge(sem, base + count[0])
    link.count = count
    return link


class Count:

    def __init__(self, reg, scale, offset):
        self.reg, self.scale, self.offset = reg, scale, offset

    def __add__(self, k):
        return Count(self.reg, self.scale, self.offset + k)

    def __sub__(self, k):
        return Count(self.reg, self.scale, self.offset - k)

    def __mul__(self, k):
        return Count(self.reg, self.scale * k, self.offset * k)

    def value(self):
        scaled = self.reg if self.scale == 1 else self.reg * self.scale
        return scaled + self.offset if self.offset else scaled


def DS(start, size):
    return bass.ds(start.value() if isinstance(start, Count) else start, size)


def at_least(eng, sem, value):
    if isinstance(value, Count):
        eng.wait_ge(sem, value.value())
    elif not isinstance(value, int) or value > 0:
        eng.wait_ge(sem, value)


def in_turns(eng, turns, steps, bufs):
    last = max(behind for behind, _ in steps)
    assert last <= bufs
    for n in range(2 * bufs):
        for behind, step in steps:
            if n >= behind:
                step(n - behind, (n - behind) % bufs, (n - behind) // bufs)
    with eng.Fori(2, turns) as t:
        for q in range(bufs):
            for behind, step in steps:
                step(Count(t, bufs, q - behind), (q - behind) % bufs, Count(t, 1, (q - behind) // bufs))
    for n in range(turns * bufs, turns * bufs + last):
        for behind, step in steps:
            if n - behind < turns * bufs:
                step(n - behind, (n - behind) % bufs, (n - behind) // bufs)


def make_constants(nc, sb):
    c = {
        "row": sb("iota_row", [P, P], F32), "col": sb("iota_col", [P, 1], F32),
        "rowb": sb("iota_row_bf", [P, P], BF16),
        "ident": sb("ident", [P, P], F32), "identb": sb("ident_bf", [P, P], BF16),
        "tri": sb("tri", [P, P], F32), "ones": sb("ones", [P, P], F32),
        "eps": sb("eps", [P, 1], F32),
    }
    return c


def clear_semaphores(nc, sems):
    with nc.Block() as block:
        @block.gpsimd
        def _(pool):
            first, last = sems[0].num, sems[-1].num
            assert [one.num for one in sems] == list(range(first, last + 1))
            pool.sem_clear(range(first, last + 1))


def sort_edges(nc, src, dst, recs, written, const, keep):
    ident, identb, tri, ones, row, rowb, col = (const[k] for k in ("ident", "identb", "tri", "ones", "row", "rowb", "col"))
    with ExitStack() as ctx:
        def sb(name, shape, dt):
            return ctx.enter_context(nc.sbuf_tensor(name, shape, dt))

        def ps(name, shape, dt=F32):
            return ctx.enter_context(nc.psum_tensor(name, shape, dt))

        sems = []

        def sem(name):
            sems.append(ctx.enter_context(nc.semaphore(name)))
            return sems[-1]

        src_i, dst_i = sb("src_i", [L, ET], I32), sb("dst_i", [L, ET], I32)
        fill = sb("fill", [P, REC_COLS], I32)
        blockf, localf = sb("blockf", [L, ET], F32), sb("localf", [L, ET], F32)
        scaled = sb("scaled", [L, ET], F32)
        onehot_block = sb("onehot_block", [L, ET, 2 * NB], BF16)
        before = sb("before", [L, NB, ET + 1], F32)
        firstp = sb("firstp", [L, ET, 2 * NB], BF16)
        zeros = sb("zeros", [L, ET], F32)
        quotient = [sb(f"quotient{h}", [L, ET], F32) for h in range(2)]
        onehot = [sb(f"onehot{h}", [L, CH, L], BF16) for h in range(BUFS)]
        onehot_t = [sb(f"onehot_t{h}", [L, CH, L], BF16) for h in range(BUFS)]
        ahead = [sb(f"ahead{h}", [L, CH, L], BF16) for h in range(2)]
        weighted = [sb(f"weighted{h}", [L, CH, 2 * NB], F32) for h in range(2)]
        slotf = [sb(f"slotf{h}", [L, CH], F32) for h in range(2)]
        totals = sb("totals", [L, NB], F32)
        groups_f, groups_i = sb("groups_f", [P, NB], F32), sb("groups_i", [P, NB], I32)
        group_end, group_start = sb("group_end", [P, NB], F32), sb("group_start", [P, NB], F32)
        base = sb("base", [L, NB], F32)
        giota = sb("giota", [1, GROUPS], F32)
        gcmp = before[0:1, :, :].rearrange("p b t -> p (b t)")[:, 0:GROUPS * NB].rearrange("p (g b) -> p g b", b=NB)
        gblk = sb("gblk", [1, GROUPS], F32)
        ps_hist = [ps(f"ps_hist{h}", [L, CH, NB]) for h in range(2)]
        ps_t = [ps(f"ps_t{h}", [L, CH, L + 1], BF16) for h in range(2)]
        ps_same = [ps(f"ps_same{h}", [L, 512]) for h in range(2)]
        ps_slot = [ps(f"ps_slot{h}", [L, CH, 2 * NB]) for h in range(2)]

        iotas_ready, consts_ready = sem("iotas_ready"), sem("consts_ready")
        edges_in, fill_set, fill_done = sem("edges_in"), sem("fill_set"), sem("fill_done")
        v_link = sem("sort_v_link")
        counted_set, hist_done, hist_kept = sem("counted_set"), sem("hist_done"), sem("hist_kept")
        onehot_set, t_done, t_kept, same_done = sem("onehot_set"), sem("t_done"), sem("t_kept"), sem("same_done")
        ahead_set, slot_done, weighted_set, slotf_set, slot_set = sem("ahead_set"), sem("slot_done"), sem("weighted_set"), sem("slotf_set"), sem("slot_set")
        totals_set, totals_done = sem("totals_set"), sem("totals_done")
        base_set, based, quotient_set, digit_set, digits_set = sem("base_set"), sem("based"), sem("quotient_set"), sem("digit_set"), sem("digits_set")
        scatter_staged = [sem(f"sort_scatter_staged{h}") for h in range(2)]
        UNITS = ET // CH
        TURNS = UNITS // BUFS
        block_ctx = ExitStack()
        block = block_ctx.enter_context(nc.Block())

        @block.sync
        def _(sp):
            sp.dma_start(src_i[:, :], src.rearrange("(p t) -> p t", t=ET)).then_inc(edges_in, 16)
            sp.dma_start(dst_i[:, :], dst.rearrange("(p t) -> p t", t=ET)).then_inc(edges_in, 16)
            sp.wait_ge(fill_set, 1)
            for rec in recs:
                sp.dma_start(rec.rearrange("(p c) o -> p (c o)", c=REC_COLS), fill[:, :]).then_inc(fill_done, 16)
            sp.wait_ge(fill_done, 16 * RECS)

        @block.gpsimd
        def _(pool):
            nc.gpsimd.iota(row[:, :], pattern=[[1, P]], base=0, channel_multiplier=0, allow_small_or_imprecise_dtypes=True).then_inc(iotas_ready, 1)
            nc.gpsimd.iota(col[:, :], pattern=[[1, 1]], base=0, channel_multiplier=1, allow_small_or_imprecise_dtypes=True).then_inc(iotas_ready, 1)
            nc.gpsimd.iota(giota[:, :], pattern=[[1, GROUPS]], base=0, channel_multiplier=0, allow_small_or_imprecise_dtypes=True).then_inc(iotas_ready, 1)
            nc.gpsimd.memset(fill[:, :], PAD_RECORD).then_inc(fill_set, 1)
            nc.gpsimd.memset(const["eps"][:, :], 1e-5)
            nc.gpsimd.memset(ones[:, :], 1.0).then_inc(consts_ready, 1)
            pool.wait_ge(fill_done, 16 * RECS)
            scatter_records(nc, pool, keep, recs, written, scatter_staged, 0, SORT_SCATTERS, slot_set)

        @block.vector
        def _(dve):
            link = linker(dve, v_link)
            v = nc.vector
            dve.wait_ge(iotas_ready, 3)
            v.tensor_copy(rowb[:, :], row[:, :])
            v.tensor_scalar(ident[:, :], row[:, :], col[:, 0:1], None, ALU.is_equal)
            v.tensor_scalar(identb[:, :], row[:, :], col[:, 0:1], None, ALU.is_equal)
            link(v.tensor_scalar(tri[:, :], row[:, :], col[:, 0:1], None, ALU.is_gt))
            dve.sem_inc(consts_ready, 1)
            dve.wait_ge(edges_in, 32)
            v.scalar_tensor_tensor(keep["key"][:, :], src_i[:, :], float(KEY), dst_i[:, :], ALU.mult, ALU.add)
            link(v.tensor_scalar(scaled[:, :], src_i[:, :], 1.0 / L, 0.5 / L - 0.5, ALU.mult, ALU.add))
            link(v.tensor_scalar(blockf[:, :], scaled[:, :], ROUND, -ROUND, ALU.add, ALU.add))
            link(v.scalar_tensor_tensor(localf[:, :], blockf[:, :], -float(L), src_i[:, :], ALU.mult, ALU.add))
            link(v.tensor_tensor(onehot_block[:, :, NB:2 * NB], blockf[:, :].unsqueeze(2).broadcast_to([L, ET, NB]),
                                 row[0:L, 0:NB].unsqueeze(1).broadcast_to([L, ET, NB]), ALU.is_equal))
            v.memset(before[:, :, 0:1], 0.0)
            v.memset(zeros[:, :], 0.0)
            link(v.tensor_scalar(onehot_block[:, :, 0:NB], onehot_block[:, :, NB:2 * NB], 256.0, None, ALU.mult))
            def onehots(n, q, one):
                v.tensor_tensor(onehot[q][:, :, :], row[0:L, 0:L].unsqueeze(1).broadcast_to([L, CH, L]),
                                localf[:, DS(n * CH, CH)].unsqueeze(2).broadcast_to([L, CH, L]), ALU.is_equal).then_inc(one, 1)

            for q in range(BUFS):
                onehots(q, q, counted_set)
            with v.Fori(1, TURNS) as t:
                for q in range(BUFS):
                    n = Count(t, BUFS, q)
                    at_least(dve, hist_done, n - (BUFS - 1))
                    onehots(n, q, counted_set)
            dve.wait_ge(hist_kept, UNITS)
            for b in range(NB):
                ins = v.tensor_tensor_scan(before[:, b, 1:ET + 1], before[:, b, 1:ET + 1], zeros[:, :], 0.0, ALU.add, ALU.add)
            link(ins)
            v.tensor_copy(totals[:, :], before[:, :, ET]).then_inc(totals_set, 1)
            dve.wait_ge(totals_done, 1)
            link(v.tensor_scalar(groups_i[0:L, :], ps_hist[0][:, 1, :], float(GE - 1), None, ALU.add))
            link(v.tensor_scalar(groups_i[0:L, :], groups_i[0:L, :], GE.bit_length() - 1, None, ALU.logical_shift_right))
            link(v.tensor_copy(groups_f[0:L, :], groups_i[0:L, :]))
            link(v.tensor_tensor_scan(group_end[0:L, :], groups_f[0:L, :], zeros[:, 0:NB], 0.0, ALU.add, ALU.add))
            link(v.tensor_sub(group_start[0:L, :], group_end[0:L, :], groups_f[0:L, :]))
            link(v.tensor_scalar(base[:, :], group_start[0:L, :], float(GE), 1.0 - MIDDLE, ALU.mult, ALU.add))
            v.tensor_add(base[:, :], base[:, :], ps_hist[0][:, 0, :]).then_inc(base_set, 1)
            for b in range(NB):
                dve.wait_ge(quotient_set, b + 1)
                v.tensor_scalar(firstp[:, :, b], quotient[b % 2][:, :], ROUND, -ROUND, ALU.add, ALU.add).then_inc(digit_set, 1)
                dve.wait_ge(digit_set, b + 1)
                ins = v.scalar_tensor_tensor(firstp[:, :, NB + b], firstp[:, :, b], -256.0, before[:, b, 0:ET], ALU.mult, ALU.add)
            ins.then_inc(digits_set, 1)

            def one_hots(n, q, turn):
                at_least(dve, t_done, n - BUFS + 1)
                onehots(n, q, onehot_set)

            def earlier(n, q, turn):
                at_least(dve, same_done, n + 1)
                at_least(dve, slot_done, n - 1)
                v.tensor_tensor(ahead[q % 2][:, :, :], ps_same[q % 2][:, 0:CH * L].rearrange("p (c e) -> p c e", c=CH),
                                tri[0:L, 0:L].unsqueeze(1).broadcast_to([L, CH, L]), ALU.mult).then_inc(ahead_set, 1)

            def pick(n, q, turn):
                at_least(dve, slot_done, n + 1)
                at_least(dve, slotf_set, n - 1)
                v.tensor_tensor(weighted[q % 2][:, :, :], ps_slot[q % 2][:, :, :], onehot_block[:, DS(n * CH, CH), :], ALU.mult).then_inc(weighted_set, 1)

            def keep_slots(n, q, turn):
                at_least(dve, weighted_set, n + 1)
                at_least(dve, slot_set, n - 1)
                v.tensor_reduce(slotf[q % 2][:, :], weighted[q % 2][:, :, :], AX.X, ALU.add).then_inc(slotf_set, 1)

            def write_slots(n, q, turn):
                at_least(dve, slotf_set, n + 1)
                v.tensor_scalar(keep["slot"][:, DS(n * CH, CH)], slotf[q % 2][:, :], MIDDLE, None, ALU.add).then_inc(slot_set, 1)

            in_turns(v, TURNS, ((0, one_hots), (4, write_slots), (3, pick), (1, earlier), (3, keep_slots)), BUFS)
            dve.wait_ge(digits_set, 1)
            link(v.tensor_tensor(gcmp[:, :, :], giota[:, :].unsqueeze(2).broadcast_to([1, GROUPS, NB]),
                                 group_start[0:1, :].unsqueeze(1).broadcast_to([1, GROUPS, NB]), ALU.is_ge))
            link(v.tensor_reduce(gblk[:, :], gcmp[:, :, 1:NB], AX.X, ALU.add))
            v.tensor_copy(keep["group_block"][:, :], gblk[:, :])

        @block.tensor
        def _(pe):
            pe.wait_ge(consts_ready, 2)
            def count(n, q, turn):
                at_least(pe, counted_set, n + 1)
                at_least(pe, hist_kept, n - 1)
                blocks = onehot_block[:, DS(n * CH, CH), NB:2 * NB]
                for j in range(CH):
                    ins = nc.tensor.matmul(ps_hist[q % 2][:, j, :], onehot[q][:, j, :], blocks[:, j, :], start=True, stop=True)
                ins.then_inc(hist_done, 1)

            in_turns(nc.tensor, TURNS, ((0, count),), BUFS)
            pe.wait_ge(totals_set, 1)
            nc.tensor.matmul(ps_hist[0][:, 0, :], tri[0:L, 0:L], totals[:, :], start=True, stop=True)
            nc.tensor.matmul(ps_hist[0][:, 1, :], ones[0:L, 0:L], totals[:, :], start=True, stop=True).then_inc(totals_done, 1)
            pe.wait_ge(digits_set, 1)

            def turn_over(n, q, turn):
                at_least(pe, onehot_set, n + 1)
                at_least(pe, t_kept, n - 1)
                for j in range(CH):
                    ins = nc.tensor.transpose(ps_t[q % 2][:, j, 0:L], onehot[q][:, j, :], identb[0:L, 0:L])
                ins.then_inc(t_done, 1)

            def compare(n, q, turn):
                at_least(pe, t_kept, n + 1)
                at_least(pe, ahead_set, n - 1)
                for j in range(CH):
                    ins = nc.tensor.matmul(ps_same[q % 2][:, j * L:(j + 1) * L], onehot_t[q][:, j, :], onehot_t[q][:, j, :], start=True, stop=True)
                ins.then_inc(same_done, 1)

            def slots(n, q, turn):
                at_least(pe, ahead_set, n + 1)
                at_least(pe, weighted_set, n - 1)
                for j in range(CH):
                    tile = DS(n * CH + j, 1)
                    nc.tensor.matmul(ps_slot[q % 2][:, j, :], onehot_t[q][:, j, :],
                                     firstp[:, tile, :].rearrange("p o b -> p (o b)"), start=True, stop=False)
                    ins = nc.tensor.matmul(ps_slot[q % 2][:, j, NB:2 * NB], ahead[q % 2][:, j, :],
                                           onehot_block[:, tile, NB:2 * NB].rearrange("p o b -> p (o b)"), start=False, stop=True)
                ins.then_inc(slot_done, 1)

            in_turns(nc.tensor, TURNS, ((1, compare), (0, turn_over), (2, slots)), BUFS)

        @block.scalar
        def _(act):
            def keep_counts(n, q, turn):
                at_least(act, hist_done, n + 1)
                nc.scalar.copy(before[:, :, DS(n * CH + 1, CH)], ps_hist[q % 2][:, :, :].rearrange("p c b -> p b c")).then_inc(hist_kept, 1)

            in_turns(nc.scalar, TURNS, ((0, keep_counts),), BUFS)
            act.wait_ge(base_set, 1)
            for b in range(NB):
                nc.scalar.activation(before[:, b, 0:ET], before[:, b, 0:ET], ACT.Identity, bias=base[:, b:b + 1]).then_inc(based, 1)
                act.wait_ge(based, b + 1)
                if b >= 2:
                    act.wait_ge(digit_set, b - 1)
                nc.scalar.activation(quotient[b % 2][:, :], before[:, b, 0:ET], ACT.Copy, scale=1.0 / 256, bias=0.5 / 256 - 0.5).then_inc(quotient_set, 1)

            def keep_columns(n, q, turn):
                at_least(act, t_done, n + 1)
                at_least(act, slot_done, n - BUFS + 1)
                nc.scalar.copy(onehot_t[q][:, :, :], ps_t[q % 2][:, :, 0:L]).then_inc(t_kept, 1)

            in_turns(nc.scalar, TURNS, ((0, keep_columns),), BUFS)

        block_ctx.close()
        clear_semaphores(nc, sems)


def scatter_records(nc, pool, keep, recs, written, staged, first, last, ready=None):
    slot_set, key_set = keep["scatter_slot"], keep["scatter_key"]

    def turn(t, s, begins=False):
        at = DS((t * 2 + s) * STAGED_TILES, STAGED_TILES)
        if ready is not None:
            pool.wait_ge(ready, (t * 2 + s + 1) * (STAGED_TILES // CH))
            pool.nop(nofuse=True)
        nc.gpsimd.tensor_copy(slot_set[s][:, :], keep["slot"][:, at])
        nc.gpsimd.tensor_copy(key_set[s][:, :], keep["key"][:, at]).then_inc(staged[s], 1)
        pool.wait_ge(staged[s], t - first + 1)
        pool.nop(nofuse=True)
        for c in range(STAGED_TILES):
            j, past = c % RECS, s * PER_LIST + c // RECS
            if not begins or past:
                pool.wait_ge(written[j], t * (2 * PER_LIST * 16) + past * 16)
                pool.nop(nofuse=True)
            nc.gpsimd.indirect_dma_start(recs[j], bass.IndirectOffsetOnAxis(ap=slot_set[s][:, c:c + 1], axis=0),
                                         key_set[s][:, c:c + 1], None).then_inc(written[j], 16)

    turn(first, 0, begins=first == 0)
    turn(first, 1)
    with nc.gpsimd.Fori(first + 1, last) as t:
        turn(t, 0)
        turn(t, 1)
    for j in range(RECS):
        pool.wait_ge(written[j], last * (2 * PER_LIST * 16))


def project_and_mix(nc, a, const, keep, x_sb, recs, written, tab_v, tab_e, tab_parts):
    ident, ones, eps = const["ident"], const["ones"], const["eps"]
    with ExitStack() as ctx:
        def sb(name, shape, dt=F32):
            return ctx.enter_context(nc.sbuf_tensor(name, shape, dt))

        def ps(name, shape, dt=F32):
            return ctx.enter_context(nc.psum_tensor(name, shape, dt))

        sems = []

        def sem(name):
            sems.append(ctx.enter_context(nc.semaphore(name)))
            return sems[-1]

        w_e, w_r = sb("w_e", [P, KF, HEADS, D]), sb("w_r", [P, KF, HEADS, D])
        w_in, w_out = sb("w_in", [P, KF, F]), sb("w_out", [P, KF, F])
        a_row = sb("a_row", [P, HEADS, 5, D])
        b_in_col, b_out_row = sb("b_in_col", [P, KF]), sb("b_out_row", [1, F])
        wq2, wk2 = sb("wq2", [P, 2 * SLICE]), sb("wk2", [P, 2 * SLICE])
        wv2 = sb("wv2", [P, 2 * D])
        w_node = sb("w_node", [P, KF, 2 * HEADS])
        half_prd = sb("half_prd", [P, HEADS, D])
        prod_e = sb("prod_e", [P, KF, HEADS, D])
        term = sb("term", [P, 4, KF, HEADS])
        stats, moments = sb("stats", [L, NB, 6]), sb("moments", [L, NB, 2])
        deviation, rstd = sb("deviation", [L, NB]), sb("rstd", [L, NB])
        xn = sb("xn", [L, F])
        xn_t = sb("xn_t", [P, KF, L])
        xm_t = sb("xm_t", [P, KF, L])
        row_v, row_e, row_u = sb("row_v", [L, EW]), sb("row_e", [L, F]), sb("row_u", [L, HEADS])
        squares, square_sum = sb("squares", [L, HEADS, D]), sb("square_sum", [L, HEADS])
        q_max, q_sum, q_inv = sb("q_max", [L, HEADS]), sb("q_sum", [L, HEADS]), sb("q_inv", [L, HEADS])
        q_exp, q_soft = sb("q_exp", [L, HEADS, SLICE]), sb("q_soft", [L, HEADS * SLICE])
        qt_all, kt_all = sb("qt_all", [P, 2, N]), sb("kt_all", [P, 2, N])
        v_all = sb("v_all", [L, NB, F])
        k_max, k_sum, k_inv = sb("k_max", [P, 2]), sb("k_sum", [P, 2]), sb("k_inv", [P, 2])
        staged_t = [sb(f"staged_t{h}", [P, 2, L]) for h in range(2)]
        row_parts, rest_u = sb("row_parts", [L, PARTS, EW], BF16), sb("rest_u", [L, HEADS])
        head_of_row, head_of_row_i = sb("head_of_row", [P, 1]), sb("head_of_row_i", [P, 1], I32)
        head_of_col, same_head = sb("head_of_col", [P, 2 * P]), sb("same_head", [P, 2 * P])
        late = prod_e[:, :, :, :].rearrange("p k h d -> p (k h d)")
        kv = late[:, 0:F].rearrange("p (g c) -> p g c", g=2)
        kv_t = late[:, F:2 * F].rearrange("p (g c n) -> p g c n", g=2, c=2)
        kvw = late[:, 2 * F:4 * F].rearrange("p (g f) -> p g f", g=2)
        k_rows = [late[0:L, 2 * F + h * 2 * P:2 * F + (h + 1) * 2 * P] for h in range(2)]
        zero_rows = late[0:L, 3 * F:3 * F + 2 * P]
        ps_xt, ps_hr, ps_he = ps("ps_xt", [P, F]), ps("ps_hr", [P, F]), ps("ps_he", [P, F])
        ps_s, ps_xm, ps_q = ps("ps_s", [L, 2 * HEADS]), ps("ps_xm", [P, F]), ps("ps_q", [P, F])
        ps_v, ps_k = ps("ps_v", [P, F]), ps("ps_k", [P, F])

        scatter_staged = [sem(f"scatter_staged{h}") for h in range(2)]
        X_PARTS = 4
        x_in = [sem(f"x_in{i}") for i in range(X_PARTS)]
        head_weights_in, mix_weights_in = sem("head_weights_in"), sem("mix_weights_in")
        zeroed, masks_set = sem("zeroed"), sem("masks_set")
        dve_link = sem("mix_dve_link")
        var_set, dev_set = sem("var_set"), sem("dev_set")
        weights_set = sem("weights_set")
        names = ("xn_set xt_done xt_kept proj_done rows_kept rows_set rows_free xm_done xm_kept qvk_done kv_kept "
                 "q_shifted q_exped q_set qt_done qt_kept loop_link kmax_set kexp_set k_staged k_done k_kept kv_done "
                 "kv_set kv_added kvt_done kvt_kept kvw_done kvw_kept q_staged mix_done mix_added").split()
        s = {n: sem(n) for n in names}
        rows_out, weights_in = sem("rows_out"), sem("weights_in")
        WEIGHT_LOADS, MIX_LOADS = 2 * KF + 1, 4
        block_ctx = ExitStack()
        block = block_ctx.enter_context(nc.Block())

        @block.sync
        def _(sp):
            x_rows, part = a["x"].rearrange("(t p) f -> p t f", p=L), NB // X_PARTS
            for i in range(X_PARTS):
                at = slice(i * part, (i + 1) * part)
                sp.dma_start(x_sb[:, at, :], x_rows[:, at, :]).then_inc(x_in[i], 16)
            sp.wait_ge(zeroed, 1)
            for h in range(2):
                sp.dma_start(wq2[h * D:(h + 1) * D, h * SLICE:(h + 1) * SLICE], a["L0_mix_Wq"]).then_inc(head_weights_in, 16)
                sp.dma_start(wk2[h * D:(h + 1) * D, h * SLICE:(h + 1) * SLICE], a["L0_mix_Wk"]).then_inc(head_weights_in, 16)
                sp.dma_start(wv2[h * D:(h + 1) * D, h * D:(h + 1) * D], a["L0_mix_Wv"]).then_inc(head_weights_in, 16)
            with nc.sync.Fori(0, NB) as t:
                sp.wait_ge(s["rows_set"], t + 2)
                at = DS(t * L, L)
                sp.dma_start(tab_v[at, :], row_v[:, :]).then_inc(rows_out, 16)
                sp.dma_start(tab_e[at, :], row_e[:, :]).then_inc(rows_out, 16)
                sp.dma_start(tab_parts[at, :], row_parts[:, :, :].rearrange("p s c -> p (s c)")).then_inc(rows_out, 16)
                sp.wait_ge(rows_out, t * 48 + 48)
                sp.sem_inc(s["rows_free"], 1)

        @block.gpsimd
        def _(pool):
            nc.gpsimd.memset(wq2[:, :], 0.0)
            nc.gpsimd.memset(wk2[:, :], 0.0)
            nc.gpsimd.memset(wv2[:, :], 0.0).then_inc(zeroed, 1)
            nc.gpsimd.iota(head_of_row_i[:, :], pattern=[[1, 1]], base=0, channel_multiplier=1)
            nc.gpsimd.iota(head_of_col[:, :], pattern=[[1, 2 * P // D], [0, D]], base=0, channel_multiplier=0,
                           allow_small_or_imprecise_dtypes=True).then_inc(masks_set, 1)
            scatter_records(nc, pool, keep, recs, written, scatter_staged, SORT_SCATTERS, SCATTERS)

        @block.vector
        def _(dve):
            v = nc.vector
            link = linker(dve, dve_link)
            for n, buffers in (("xt_done", 1), ("qt_done", 1), ("mix_done", 2), ("k_done", 2)):
                dve.sem_inc(s[n], buffers)
            for i in range(X_PARTS):
                dve.wait_ge(x_in[i], 16)
                for t in range(i * NB // X_PARTS, (i + 1) * NB // X_PARTS):
                    v.bn_stats(stats[:, t, :], x_sb[:, t, :])
            link(v.memset(q_max[:, :], 0.0))
            for t in range(NB):
                ins = v.bn_aggr(moments[:, t, :], stats[:, t, :])
            ins.then_inc(var_set, 1)
            dve.wait_ge(weights_in, 16 * WEIGHT_LOADS)

            def a_part(i):
                return a_row[:, :, i, :].unsqueeze(1).broadcast_to([P, KF, HEADS, D])

            for i, (w, part) in enumerate(((w_e, 0), (w_e, 1), (w_r, 2))):
                link(v.tensor_tensor(prod_e[:, :, :, :], w[:, :, :, :], a_part(part), ALU.mult))
                link(v.tensor_reduce(term[:, i, :, :], prod_e[:, :, :, :], AX.X, ALU.add))
            v.memset(zero_rows, 0.0)
            v.tensor_sub(w_node[:, :, 0:HEADS], term[:, 0, :, :], term[:, 2, :, :])
            v.tensor_add(w_node[:, :, HEADS:2 * HEADS], term[:, 1, :, :], term[:, 2, :, :])
            v.tensor_scalar(half_prd[:, :, :], a_row[:, :, 4, :], 0.5, None, ALU.mult).then_inc(weights_set, 1)
            dve.wait_ge(weights_set, 1)
            dve.wait_ge(masks_set, 1)
            link(v.tensor_scalar(head_of_row_i[:, :], head_of_row_i[:, :], SLICE.bit_length() - 1, None, ALU.logical_shift_right))
            link(v.tensor_copy(head_of_row[:, :], head_of_row_i[:, :]))
            link(v.tensor_scalar(same_head[:, :], head_of_col[:, :], head_of_row[:, 0:1], None, ALU.is_equal))
            dve.wait_ge(dev_set, 1)
            link(v.reciprocal(rstd[:, :], deviation[:, :]))
            STEPS = 13

            def normalize(t):
                dve.wait_ge(s["xt_done"], t + 1)
                v.tensor_scalar(xn[:, :], x_sb[:, DS(t, 1), :].rearrange("p o f -> p (o f)"), moments[:, DS(t, 1), 0:1].rearrange("p a b -> p (a b)"),
                                rstd[:, DS(t, 1)], ALU.subtract, ALU.mult).then_inc(s["xn_set"], 1)

            def node_terms(t, step):
                dve.wait_ge(s["rows_kept"], t + 2)
                h_r = row_v[:, 0:F].rearrange("p (c h r) -> p h c r", c=KF, h=HEADS)
                step(v.tensor_tensor(squares[:, :, :].rearrange("p h (c r) -> p h c r", c=KF), h_r, h_r, ALU.mult))
                step(v.tensor_tensor(squares[:, :, :], squares[:, :, :], half_prd[0:L, :, :], ALU.mult))
                step(v.tensor_reduce(square_sum[:, :], squares[:, :, :], AX.X, ALU.add))
                v.tensor_tensor(row_v[:, F:EW], ps_s[:, HEADS:2 * HEADS], square_sum[:, :], ALU.add)
                step(v.scalar_tensor_tensor(row_u[:, :], ps_s[:, 0:HEADS], -1.0, square_sum[:, :], ALU.mult, ALU.subtract))
                rest = squares[:, :, :].rearrange("p h d -> p (h d)")
                for part in range(PARTS):
                    of_row, of_u = (row_v[:, 0:F], row_u[:, :]) if part == 0 else (rest, rest_u[:, :])
                    v.tensor_copy(row_parts[:, part, 0:F], of_row)
                    ins = v.tensor_copy(row_parts[:, part, F:EW], of_u)
                    if part < PARTS - 1:
                        step(ins)
                        v.tensor_tensor(rest, of_row, row_parts[:, part, 0:F], ALU.subtract)
                        step(v.tensor_tensor(rest_u[:, :], of_u, row_parts[:, part, F:EW], ALU.subtract))
                step(ins)
                dve.sem_inc(s["rows_set"], 1)

            def q_softmax(t, step):
                dve.wait_ge(s["qvk_done"], t + 2)
                q = ps_q[0:L, 0:HEADS * SLICE].rearrange("p (h s) -> p h s", h=HEADS)
                step(v.tensor_reduce(q_max[:, :], q, AX.X, ALU.max))
                v.tensor_tensor(q_exp[:, :, :], q, q_max[:, :].unsqueeze(2).broadcast_to([L, HEADS, SLICE]), ALU.subtract).then_inc(s["q_shifted"], 1)
                dve.wait_ge(s["q_exped"], t + 1)
                step(v.tensor_reduce(q_sum[:, :], q_exp[:, :, :], AX.X, ALU.add))
                step(v.reciprocal(q_inv[:, :], q_sum[:, :]))
                dve.wait_ge(s["qt_done"], t + 1)
                step(v.tensor_tensor(q_soft[:, :].rearrange("p (h s) -> p h s", h=HEADS), q_exp[:, :, :],
                                     q_inv[:, :].unsqueeze(2).broadcast_to([L, HEADS, SLICE]), ALU.mult))
                dve.sem_inc(s["q_set"], 1)

            normalize(0)
            with v.Fori(0, NB - 1) as t:
                step = linker(dve, s["loop_link"], t * STEPS)
                normalize(t + 1)
                node_terms(t, step)
                q_softmax(t, step)
            assert step.count[0] == STEPS
            step = linker(dve, s["loop_link"], (NB - 1) * STEPS)
            node_terms(NB - 1, step)
            q_softmax(NB - 1, step)
            dve.wait_ge(s["kv_kept"], NB + 1)
            link(v.tensor_reduce(k_max[:, :], kt_all[:, :, :], AX.X, ALU.max))
            v.tensor_scalar(k_max[:, :], k_max[:, :], -1.0, None, ALU.mult).then_inc(s["kmax_set"], 1)
            dve.wait_ge(s["kexp_set"], 1)
            link(v.tensor_reduce(k_sum[:, :], kt_all[:, :, :], AX.X, ALU.add))
            link(v.reciprocal(k_inv[:, :], k_sum[:, :]))
            with v.Fori(0, NB // 2) as t:
                for h in range(2):
                    dve.wait_ge(s["k_done"], t * 2 + (h + 1))
                    v.tensor_copy(staged_t[h][:, :, :], kt_all[:, :, DS((t * 2 + h) * L, L)]).then_inc(s["k_staged"], 1)
            dve.wait_ge(s["kv_done"], 1)
            for g, acc in enumerate((ps_hr, ps_he)):
                ins = v.scalar_tensor_tensor(kv[:, g, :], acc[:, 0:2 * P], k_inv[:, g:g + 1], same_head[:, :], ALU.mult, ALU.mult)
            ins.then_inc(s["kv_set"], 1)
            dve.wait_ge(s["qt_kept"], NB + 1)

            def stage_q(t, h):
                dve.wait_ge(s["mix_done"], t + 1)
                v.tensor_copy(staged_t[h][:, :, :], qt_all[:, :, DS(t * L, L)]).then_inc(s["q_staged"], 1)

            def add_mix(t, h):
                dve.wait_ge(s["mix_done"], t + 3)
                tile = x_sb[:, DS(t, 1), :].rearrange("p o f -> p (o f)")
                v.tensor_tensor(tile, (ps_xm, ps_q)[h][0:L, :], tile, ALU.add).then_inc(s["mix_added"], 1)

            stage_q(0, 0)
            with v.Fori(0, NB // 2 - 1) as t:
                stage_q(t * 2 + 1, 1)
                add_mix(t * 2, 0)
                stage_q(t * 2 + 2, 0)
                add_mix(t * 2 + 1, 1)
            stage_q(NB - 1, 1)
            add_mix(NB - 2, 0)
            add_mix(NB - 1, 1)

        @block.tensor
        def _(pe):
            t_ = nc.tensor
            pe.wait_ge(weights_set, 1)
            pe.wait_ge(head_weights_in, 16 * 6)
            pe.wait_ge(weights_in, 16 * WEIGHT_LOADS)

            def transpose_x(t):
                pe.wait_ge(s["xn_set"], t + 1)
                pe.wait_ge(s["xt_kept"], t + 1)
                for k in range(KF):
                    ins = t_.transpose(ps_xt[:, k * L:(k + 1) * L], xn[:, k * P:(k + 1) * P], ident[0:L, 0:L])
                ins.then_inc(s["xt_done"], 1)

            def project(t):
                pe.wait_ge(s["xt_kept"], t + 2)
                pe.wait_ge(s["rows_kept"], t + 1)
                pe.wait_ge(s["rows_set"], t + 1)
                for k in range(KF):
                    t_.matmul(ps_hr[0:L, :], xn_t[:, k, :], w_r[:, k, :, :].rearrange("p h d -> p (h d)"), start=k == 0, stop=k == KF - 1)
                for k in range(KF):
                    t_.matmul(ps_he[0:L, :], xn_t[:, k, :], w_e[:, k, :, :].rearrange("p h d -> p (h d)"), start=k == 0, stop=k == KF - 1)
                for k in range(KF):
                    ins = t_.matmul(ps_s[:, :], xn_t[:, k, :], w_node[:, k, :], start=k == 0, stop=k == KF - 1)
                ins.then_inc(s["proj_done"], 1)

            def transpose_q(t):
                pe.wait_ge(s["q_set"], t + 1)
                pe.wait_ge(s["kv_kept"], t + 2)
                for g in range(2):
                    ins = t_.transpose(ps_k[:, g * L:(g + 1) * L], q_soft[:, g * P:(g + 1) * P], ident[0:L, 0:L])
                ins.then_inc(s["qt_done"], 1)

            def middle(t):
                pe.wait_ge(s["xm_kept"], t + 1)
                for c in range(KF):
                    for k in range(KF):
                        ins = t_.matmul(ps_xm[:, c * L:(c + 1) * L], w_in[:, k, c * P:(c + 1) * P], xn_t[:, k, :], start=k == 0, stop=k == KF - 1)
                ins.then_inc(s["xm_done"], 1)

            def heads(t):
                pe.wait_ge(s["xm_kept"], t + 2)
                pe.wait_ge(s["kv_kept"], t + 1)
                pe.wait_ge(s["qt_kept"], t + 1)
                for c in range(KF):
                    t_.matmul(ps_q[0:L, c * 2 * SLICE:(c + 1) * 2 * SLICE], xm_t[:, c, :], wq2[:, :], start=True, stop=True)
                    t_.matmul(ps_v[0:L, c * P:(c + 1) * P], xm_t[:, c, :], wv2[:, :], start=True, stop=True)
                    half = c % 2 * D
                    ins = t_.matmul(ps_k[half:half + D, c // 2 * L:(c // 2 + 1) * L], wk2[:, :], xm_t[:, c, :], start=True, stop=True)
                ins.then_inc(s["qvk_done"], 1)

            transpose_x(0)
            project(0)
            pe.wait_ge(mix_weights_in, 16 * MIX_LOADS)
            middle(0)
            transpose_x(1)
            heads(0)
            with t_.Fori(1, NB - 1) as t:
                project(t)
                transpose_q(t - 1)
                middle(t)
                transpose_x(t + 1)
                heads(t)
            project(NB - 1)
            transpose_q(NB - 2)
            middle(NB - 1)
            heads(NB - 1)
            transpose_q(NB - 1)
            pe.wait_ge(s["rows_kept"], NB + 1)
            pe.wait_ge(zeroed, 1)
            for acc in (ps_hr, ps_he):
                t_.matmul(acc[:, 0:2 * P], zero_rows[:, 0:P], zero_rows, start=True, stop=False)

            def transpose_k(t, h):
                pe.wait_ge(s["k_staged"], t + 1)
                pe.wait_ge(s["k_kept"], t + 1)
                for g in range(2):
                    ins = t_.transpose((ps_q, ps_xm)[h][0:L, g * P:(g + 1) * P], staged_t[h][:, g, :], ident[:, :])
                ins.then_inc(s["k_done"], 1)

            def add_kv(t, h):
                pe.wait_ge(s["k_kept"], t + 3)
                for g, acc in enumerate((ps_hr, ps_he)):
                    ins = t_.matmul(acc[:, 0:2 * P], k_rows[h][:, g * P:(g + 1) * P],
                                    v_all[:, DS(t, 1), g * 2 * P:(g + 1) * 2 * P].rearrange("p o c -> p (o c)"), start=False, stop=False)
                ins.then_inc(s["kv_added"], 1)

            transpose_k(0, 0)
            with t_.Fori(0, NB // 2 - 1) as t:
                transpose_k(t * 2 + 1, 1)
                add_kv(t * 2, 0)
                transpose_k(t * 2 + 2, 0)
                add_kv(t * 2 + 1, 1)
            transpose_k(NB - 1, 1)
            add_kv(NB - 2, 0)
            add_kv(NB - 1, 1)
            for acc in (ps_hr, ps_he):
                ins = t_.matmul(acc[:, 0:2 * P], zero_rows[:, 0:P], zero_rows, start=False, stop=True)
            ins.then_inc(s["kv_done"], 1)
            pe.wait_ge(s["kv_set"], 1)
            for g in range(2):
                for c in range(2):
                    ins = t_.transpose(ps_xt[:, (2 * g + c) * P:(2 * g + c + 1) * P], kv[:, g, c * P:(c + 1) * P], ident[:, :])
            ins.then_inc(s["kvt_done"], 1)
            pe.wait_ge(s["kvt_kept"], 1)
            pe.wait_ge(s["qt_kept"], NB + 1)
            for g, acc in enumerate((ps_v, ps_k)):
                for c in range(2):
                    ins = t_.matmul(acc[:, :], kv_t[:, g, c, :], w_out[:, 2 * g + c, :], start=c == 0, stop=c == 1)
            ins.then_inc(s["kvw_done"], 1)
            pe.wait_ge(s["kvw_kept"], 1)
            with t_.Fori(0, NB // 2) as t:
                for h, acc in enumerate((ps_xm, ps_q)):
                    pe.wait_ge(s["q_staged"], t * 2 + (h + 1))
                    pe.wait_ge(s["mix_added"], t * 2 + (h + 1))
                    for g in range(2):
                        t_.matmul(acc[0:L, :], staged_t[h][:, g, :], kvw[:, g, :], start=g == 0, stop=False)
                    t_.matmul(acc[0:L, :], ones[0:1, 0:L], b_out_row[:, :], start=False, stop=True).then_inc(s["mix_done"], 1)

        @block.scalar
        def _(act):
            sc = nc.scalar
            act.dma_start(a_row[:, :, :, :], a["L0_gnn_a"].rearrange("h (c d) -> h c d", d=D).partition_broadcast(P)).then_inc(weights_in, 16)
            for w, name in ((w_e, "L0_gnn_W_e"), (w_r, "L0_gnn_W_r")):
                for k in range(KF):
                    act.dma_start(w[:, k, :, :], a[name][:, k * P:(k + 1) * P, :].rearrange("h p d -> p h d")).then_inc(weights_in, 16)
            act.dma_start(w_in[:, :, :], a["L0_mix_W_in"].rearrange("(k p) f -> p k f", p=P)).then_inc(mix_weights_in, 16)
            act.dma_start(w_out[:, :, :], a["L0_mix_W_out"].rearrange("(k p) f -> p k f", p=P)).then_inc(mix_weights_in, 16)
            act.dma_start(b_in_col[:, :], a["L0_mix_b_in"].rearrange("(k p) -> p k", p=P), allow_slow_non_contiguous=True).then_inc(mix_weights_in, 16)
            act.dma_start(b_out_row[:, :], a["L0_mix_b_out"].rearrange("(o f) -> o f", o=1)).then_inc(mix_weights_in, 16)
            for n in ("xt_kept", "rows_kept", "rows_free", "xm_kept", "kv_kept", "qt_kept", "xm_done", "qvk_done", "rows_set"):
                act.sem_inc(s[n], 1)
            for n in ("k_kept", "mix_added", "kv_added"):
                act.sem_inc(s[n], 2)
            act.wait_ge(var_set, 1)
            sc.activation(deviation[:, :], moments[:, :, 1], ACT.Sqrt, bias=eps[0:L, 0:1]).then_inc(dev_set, 1)

            def keep_x(t):
                act.wait_ge(s["xt_done"], t + 2)
                act.wait_ge(s["xm_done"], t + 1)
                sc.copy(xn_t[:, :, :], ps_xt[:, 0:KF * L].rearrange("p (k n) -> p k n", k=KF)).then_inc(s["xt_kept"], 1)

            def keep_rows(t):
                act.wait_ge(s["proj_done"], t + 1)
                act.wait_ge(s["rows_free"], t + 1)
                sc.copy(row_e[:, :], ps_he[0:L, :])
                sc.copy(row_v[:, 0:F].rearrange("p (c h r) -> p h c r", c=KF, h=HEADS),
                        ps_hr[0:L, :].rearrange("p (h c r) -> p h c r", h=HEADS, c=KF)).then_inc(s["rows_kept"], 1)

            def keep_q(t):
                act.wait_ge(s["qt_done"], t + 2)
                sc.copy(qt_all[:, :, DS(t * L, L)], ps_k[:, 0:2 * L].rearrange("p (g n) -> p g n", g=2)).then_inc(s["qt_kept"], 1)

            def keep_middle(t):
                act.wait_ge(s["xm_done"], t + 2)
                act.wait_ge(s["qvk_done"], t + 1)
                for c in range(KF):
                    ins = sc.activation(xm_t[:, c, :], ps_xm[:, c * L:(c + 1) * L], ACT.Identity, bias=b_in_col[:, c:c + 1])
                ins.then_inc(s["xm_kept"], 1)

            def keep_heads(t):
                act.wait_ge(s["qvk_done"], t + 2)
                sc.copy(v_all[:, DS(t, 1), :].rearrange("p o f -> p (o f)"), ps_v[0:L, :])
                sc.copy(kt_all[:, :, DS(t * L, L)], ps_k[:, 0:2 * L].rearrange("p (g n) -> p g n", g=2)).then_inc(s["kv_kept"], 1)
                act.wait_ge(s["q_shifted"], t + 1)
                sc.activation(q_exp[:, :, :], q_exp[:, :, :], ACT.Exp).then_inc(s["q_exped"], 1)

            keep_x(0)
            keep_rows(0)
            act.wait_ge(mix_weights_in, 16 * MIX_LOADS)
            keep_middle(0)
            keep_x(1)
            keep_heads(0)
            with sc.Fori(1, NB - 1) as t:
                keep_rows(t)
                keep_q(t - 1)
                keep_middle(t)
                keep_x(t + 1)
                keep_heads(t)
            keep_rows(NB - 1)
            keep_q(NB - 2)
            keep_middle(NB - 1)
            keep_heads(NB - 1)
            keep_q(NB - 1)
            act.wait_ge(s["kmax_set"], 1)
            for g in range(2):
                ins = sc.activation(kt_all[:, g, :], kt_all[:, g, :], ACT.Exp, bias=k_max[:, g:g + 1])
            ins.then_inc(s["kexp_set"], 1)
            with sc.Fori(0, NB // 2) as t:
                for h, turned in enumerate((ps_q, ps_xm)):
                    act.wait_ge(s["k_done"], t * 2 + (h + 3))
                    act.wait_ge(s["kv_added"], t * 2 + (h + 1))
                    sc.copy(k_rows[h], turned[0:L, 0:2 * P]).then_inc(s["k_kept"], 1)
            act.wait_ge(s["kvt_done"], 1)
            sc.copy(kv_t[:, :, :, :].rearrange("p g c n -> p (g c n)"), ps_xt[:, :]).then_inc(s["kvt_kept"], 1)
            act.wait_ge(s["kvw_done"], 1)
            sc.copy(kvw[:, 0, :], ps_v[:, :])
            sc.copy(kvw[:, 1, :], ps_k[:, :]).then_inc(s["kvw_kept"], 1)

        block_ctx.close()
        clear_semaphores(nc, sems)


def read_sorted_edges(nc, const, recs, merged, edge, tab_parts, parts, parts_in):
    ROWS, PER = ST // 6, 6
    with ExitStack() as ctx:
        def sb(name, shape, dt=F32):
            return ctx.enter_context(nc.sbuf_tensor(name, shape, dt))

        def sem(name):
            return ctx.enter_context(nc.semaphore(name))

        lists = sb("lists", [ROWS, RECS, PER * P], I32)
        best = sb("best", [ROWS, PER * P])
        best_i = sb("best_i", [ROWS, PER * P], I32)
        key_t = sb("key_t", [P, ST], I32)
        source_i = sb("source_i", [P, ST], I32)
        source, scaled, blk, pad = sb("source", [P, ST]), sb("scaled_t", [P, ST]), sb("blk_t", [P, ST]), sb("pad_t", [P, ST])
        ps_key = ctx.enter_context(nc.psum_tensor("ps_key", [P, 2, 512], F32))
        lists_in, merged_set, merged_out = sem("lists_in"), sem("merged_set"), sem("merged_out")
        turned, link_s = sem("turned"), sem("read_link")
        block = ctx.enter_context(nc.Block())

        @block.sync
        def _(sp):
            for j in range(RECS):
                sp.dma_start(lists[:, j, :], recs[j][1:1 + EP, :].rearrange("(r x) o -> r (x o)", r=ROWS)).then_inc(lists_in, 16)
            sp.dma_start(merged[0:1, :], recs[0][0:1, :]).then_inc(merged_out, 16)
            sp.dma_start(merged[EP + 1:EP + 2, :], recs[0][EP + 1:EP + 2, :]).then_inc(merged_out, 16)
            per = NB // PART_LOADS
            for i in range(PART_LOADS):
                sp.dma_start(parts[:, i * per:(i + 1) * per, :, :].rearrange("p b s c -> p b (s c)"),
                             tab_parts[i * per * L:(i + 1) * per * L, :].rearrange("(b p) c -> p b c", p=L)).then_inc(parts_in, 16)
            sp.wait_ge(merged_set, 1)
            sp.dma_start(merged[1:1 + EP, :].rearrange("(r x) o -> r (x o)", r=ROWS), best_i[:, :]).then_inc(merged_out, 16)
            sp.wait_ge(merged_out, 48)

        @block.vector
        def _(dve):
            v = nc.vector
            link = linker(dve, link_s)
            dve.wait_ge(lists_in, 16 * RECS)
            link(v.tensor_tensor(best[:, :], lists[:, 0, :], lists[:, 1, :], ALU.min))
            for j in range(2, RECS):
                link(v.tensor_tensor(best[:, :], best[:, :], lists[:, j, :], ALU.min))
            v.tensor_copy(best_i[:, :], best[:, :]).then_inc(merged_set, 1)
            dve.wait_ge(turned, 1)
            link(v.tensor_copy(key_t[:, :].rearrange("p (r i j) -> p i j r", i=2, j=PER // 2),
                               ps_key[:, :, 0:PER // 2 * ROWS].rearrange("p i (j r) -> p i j r", j=PER // 2)))
            link(v.tensor_scalar(source_i[:, :], key_t[:, :], KEY.bit_length() - 1, None, ALU.logical_shift_right))
            v.tensor_scalar(edge["dst"][:, :], key_t[:, :], KEY - 1, None, ALU.bitwise_and)
            link(v.tensor_copy(source[:, :], source_i[:, :]))
            v.tensor_scalar(edge["src"][:, :], source[:, :], float(N - 1), None, ALU.min)
            link(v.tensor_scalar(scaled[:, :], source[:, :], 1.0 / L, 0.5 / L - 0.5, ALU.mult, ALU.add))
            v.tensor_scalar(pad[:, :], source[:, :], float(N), 1000.0, ALU.is_ge, ALU.mult)
            link(v.tensor_scalar(blk[:, :], scaled[:, :], ROUND, -ROUND, ALU.add, ALU.add))
            link(v.scalar_tensor_tensor(source[:, :], blk[:, :], -float(L), source[:, :], ALU.mult, ALU.add))
            link(v.tensor_add(edge["local"][:, :], source[:, :], pad[:, :]))

        @block.tensor
        def _(pe):
            pe.wait_ge(merged_set, 1)
            for j in range(PER):
                half, at = j // (PER // 2), j % (PER // 2) * ROWS
                ins = nc.tensor.transpose(ps_key[:, half, at:at + ROWS], best[:, j * P:(j + 1) * P], const["ident"][0:ROWS, 0:ROWS])
            ins.then_inc(turned, 1)


def score_edges(nc, a, const, edge, group_block, tab_v, parts, parts_in, scores):
    ident, identb, row, rowb = const["ident"], const["identb"], const["row"], const["rowb"]
    BUFS, TURN = 3, 6
    TURNS = GROUPS // TURN
    assert TURNS * TURN == GROUPS and GROUP == 2
    HALF = EW // 2
    with ExitStack() as ctx:
        def sb(name, shape, dt=F32):
            return ctx.enter_context(nc.sbuf_tensor(name, shape, dt))

        def ps(name, shape, dt=F32):
            return ctx.enter_context(nc.psum_tensor(name, shape, dt))

        def sem(name):
            return ctx.enter_context(nc.semaphore(name))

        def sbs(name, shape, dt=F32):
            return [sb(f"{name}{h}", shape, dt) for h in range(BUFS)]

        index = [sb(f"index_v{q}", [P, GROUP], I32) for q in range(TURN)]
        rows = [sb(f"rows_v{q}", [P, GROUP, EW]) for q in range(TURN)]
        onehot, onehot_t = sbs("source_onehot", [P, GROUP, L], BF16), sbs("source_onehot_t", [L, GROUP, P], BF16)
        w, w_abs = [sb(f"w{q}", [P, GROUP, EW]) for q in range(TURN)], sbs("w_abs", [P, KF, GE])
        slope, z_sum = sbs("slope", [P, KF, GE]), sbs("z_sum", [P, 2, GE])
        score = sbs("score", [HEADS, GE])
        a_abs, minus_prd = sb("a_abs", [P, KF]), sb("minus_prd", [P, KF])
        head_i, head_f = sb("head_i", [P, 1], I32), sb("head_f", [P, 1])
        head_sum = sb("head_sum", [P, HEADS])
        ps_w = [ps(f"ps_w{h}", [P, KF, GE]) for h in range(2)]
        ps_u, ps_onehot = ps("ps_u", [P, 2, 512]), ps("ps_onehot", [L, GROUP, P], BF16)
        ps_heads = ps("ps_heads", [P, GE])
        ps_score = [ps_heads[0:HEADS, :], ps_heads[P // 2:P // 2 + HEADS, :]]

        index_set, onehot_set, onehot_turned, onehot_kept = sem("index_set"), sem("onehot_set"), sem("onehot_turned"), sem("onehot_kept")
        expanded, turned, abs_set, slope_set = sem("expanded"), sem("w_turned"), sem("abs_set"), sem("slope_set")
        product_set, z_set, summed = sem("product_set"), sem("z_set"), sem("summed")
        differed = sem("differed")
        score_kept, score_free = sem("score_kept"), sem("score_free")
        gathered = [sem(f"gathered{h}") for h in range(TURN)]
        score_out = [sem(f"score_out{h}") for h in range(BUFS)]
        vectors_in, iota_set, vectors_set, link_s = sem("vectors_in"), sem("head_iota_set"), sem("vectors_set"), sem("score_link")
        block = ctx.enter_context(nc.Block())

        @block.sync
        def _(sp):
            for tile, part in ((a_abs, 3), (minus_prd, 4)):
                for h in range(HEADS):
                    sp.dma_start(tile[h * R:(h + 1) * R, :], a["L0_gnn_a"][h, part * D:(part + 1) * D].rearrange("(c r) -> r c", r=R),
                                 allow_slow_non_contiguous=True).then_inc(vectors_in, 16)
            with nc.sync.Fori(0, GROUPS // BUFS) as t:
                for h in range(BUFS):
                    sp.wait_ge(score_kept, t * BUFS + (h + 1))
                    sp.dma_start(scores[:, DS((BUFS * t + h) * GE, GE)], score[h][:, :]).then_inc(score_out[h], 16)
                for h in range(BUFS):
                    sp.wait_ge(score_out[h], t * 16 + 16)
                    sp.sem_inc(score_free, 1)

        @block.gpsimd
        def _(pool):
            nc.gpsimd.iota(head_i[:, :], pattern=[[1, 1]], base=0, channel_multiplier=1).then_inc(iota_set, 1)

            def gather(n, q, turn):
                if not isinstance(n, int) or n >= TURN:
                    at_least(pool, differed, n * GROUP - (TURN - 1) * GROUP)
                    pool.nop(nofuse=True)
                nc.gpsimd.tensor_copy(index[q][:, :], edge["dst"][:, DS(n * GROUP, GROUP)]).then_inc(index_set, 1)
                at_least(pool, index_set, n + 1)
                pool.nop(nofuse=True)
                for j in range(GROUP):
                    nc.gpsimd.indirect_dma_start(rows[q][:, j, :], None, tab_v,
                                                 bass.IndirectOffsetOnAxis(ap=index[q][:, j:j + 1], axis=0)).then_inc(gathered[q], 16)

            in_turns(nc.gpsimd, TURNS, ((0, gather),), TURN)

        @block.vector
        def _(dve):
            v = nc.vector
            link = linker(dve, link_s)
            dve.wait_ge(iota_set, 1)
            link(v.tensor_scalar(head_i[:, :], head_i[:, :], R.bit_length() - 1, None, ALU.logical_shift_right))
            link(v.tensor_copy(head_f[:, :], head_i[:, :]))
            v.tensor_scalar(head_sum[:, :], row[:, 0:HEADS], head_f[:, 0:1], None, ALU.is_equal)
            dve.wait_ge(vectors_in, 16 * 2 * HEADS)
            link(v.tensor_scalar(minus_prd[:, :], minus_prd[:, :], -0.5, None, ALU.mult))
            dve.sem_inc(vectors_set, 2)

            def locate(n, q, turn):
                at_least(dve, onehot_turned, n - BUFS + 1)
                for j in range(GROUP):
                    ins = v.tensor_scalar(onehot[q % BUFS][:, j, :], rowb[:, 0:L], edge["local"][:, DS(n * GROUP + j, 1)], None, ALU.is_equal)
                ins.then_inc(onehot_set, 1)

            def differ(n, q, turn, j):
                if j == 0:
                    at_least(dve, gathered[q], turn * (16 * GROUP) + 16 * GROUP)
                    at_least(dve, summed, n - TURN + 1)
                at_least(dve, expanded, n * GROUP + (j + 1))
                v.tensor_tensor(w[q][:, j, :].rearrange("p (a b) -> p a b", a=2), rows[q][:, j, :].rearrange("p (a b) -> p a b", a=2),
                                ps_u[:, :, 0:HALF], ALU.subtract).then_inc(differed, 1)

            def differ_first(n, q, turn):
                differ(n, q, turn, 0)

            def differ_second(n, q, turn):
                differ(n, q, turn, 1)

            def multiply(n, q, turn):
                h = q % BUFS
                at_least(dve, slope_set, n + 1)
                v.tensor_tensor(slope[h][:, :, :], w_abs[h][:, :, :], slope[h][:, :, :], ALU.mult).then_inc(product_set, 1)

            def add_chunks(n, q, turn):
                h = q % BUFS
                at_least(dve, product_set, n + 1)
                at_least(dve, summed, n - BUFS + 1)
                v.tensor_tensor(z_sum[h][:, :, :], slope[h][:, 0:2, :], slope[h][:, 2:4, :], ALU.add).then_inc(z_set, 1)

            in_turns(v, TURNS, ((2, differ_first), (5, multiply), (2, differ_second), (0, locate), (5, add_chunks)), TURN)

        @block.tensor
        def _(pe):
            pe.wait_ge(vectors_set, 1)
            pe.wait_ge(parts_in, 16 * PART_LOADS)

            def turn_onehot(n, q, turn):
                at_least(pe, onehot_set, n + 1)
                at_least(pe, onehot_kept, n)
                for j in range(GROUP):
                    ins = nc.tensor.transpose(ps_onehot[:, j, :], onehot[q % BUFS][:, j, :], identb[:, :])
                ins.then_inc(onehot_turned, 1)

            block_of = {}

            def expand(n, q, j, b):
                at_least(pe, onehot_kept, n + 1)
                at_least(pe, differed, n * GROUP + j)
                for half in range(2):
                    for part in range(PARTS):
                        rows_of_part = parts[:, DS(b, 1), part, half * HALF:(half + 1) * HALF].rearrange("p o c -> p (o c)")
                        ins = nc.tensor.matmul(ps_u[:, half, 0:HALF], onehot_t[q % BUFS][:, j, :], rows_of_part, start=part == 0, stop=part == PARTS - 1)
                ins.then_inc(expanded, 1)

            def expand_first(n, q, turn):
                block_of[q] = pe.value_load(group_block[0:1, DS(n, 1)], min_val=0, max_val=NB - 1)
                expand(n, q, 0, block_of[q])

            def expand_second(n, q, turn):
                expand(n, q, 1, block_of[q])

            def transpose(n, q, turn):
                at_least(pe, differed, n * GROUP + GROUP)
                at_least(pe, abs_set, n - 1)
                for c in range(KF):
                    for j in range(GROUP):
                        ins = nc.tensor.transpose(ps_w[q % 2][:, c, j * P:(j + 1) * P], w[q][:, j, c * P:(c + 1) * P], ident[:, :])
                ins.then_inc(turned, 1)

            def add_heads(n, q, turn):
                h = q % BUFS
                at_least(pe, z_set, n + 1)
                at_least(pe, score_kept, n - 1)
                for half in range(2):
                    nc.tensor.matmul(ps_score[q % 2], head_sum[:, :], z_sum[h][:, half, :], start=half == 0, stop=False)
                for j in range(GROUP):
                    ins = nc.tensor.matmul(ps_score[q % 2][:, j * P:(j + 1) * P], w[q][:, j, F:EW], ident[:, :], start=False, stop=j == GROUP - 1)
                ins.then_inc(summed, 1)

            in_turns(nc.tensor, TURNS, ((2, expand_first), (1, turn_onehot), (6, add_heads), (2, expand_second), (3, transpose)), TURN)

        @block.scalar
        def _(act):
            sc = nc.scalar
            act.wait_ge(vectors_set, 2)

            def keep_onehot(n, q, turn):
                at_least(act, onehot_turned, n + 1)
                at_least(act, expanded, (n - BUFS + 1) * GROUP)
                sc.copy(onehot_t[q % BUFS][:, :, :], ps_onehot[:, :, :]).then_inc(onehot_kept, 1)

            def magnitudes(n, q, turn):
                h = q % BUFS
                at_least(act, turned, n + 1)
                at_least(act, z_set, n - BUFS + 1)
                sc.activation(w_abs[h][:, :, :], ps_w[q % 2][:, :, :], ACT.Abs).then_inc(abs_set, 1)

            def slopes(n, q, turn):
                h = q % BUFS
                at_least(act, abs_set, n + 1)
                for c in range(KF):
                    ins = sc.activation(slope[h][:, c, :], w_abs[h][:, c, :], ACT.Identity, bias=a_abs[:, c:c + 1], scale=minus_prd[:, c:c + 1])
                ins.then_inc(slope_set, 1)

            def keep_scores(n, q, turn):
                at_least(act, summed, n + 1)
                at_least(act, score_free, n - BUFS + 1)
                sc.copy(score[q % BUFS][:, :], ps_score[q % 2]).then_inc(score_kept, 1)

            in_turns(sc, TURNS, ((4, magnitudes), (1, keep_onehot), (4, slopes), (6, keep_scores)), TURN)


def softmax_weights(nc, const, scores, merged, carry, weights, from_left):
    with ExitStack() as ctx:
        def sb(name, shape, dt=F32):
            return ctx.enter_context(nc.sbuf_tensor(name, shape, dt))

        def sem(name):
            return ctx.enter_context(nc.semaphore(name))

        keys = sb("keys", [P, PIECE + 2], I32)
        reset = sb("reset", [P, PIECE + 1])
        alpha, from_right = sb("alpha", [P, PIECE]), sb("from_right", [P, PIECE])
        ends = sb("ends", [P, 4])
        pieces = sb("pieces", [HEADS, CHUNKS, 4])
        state = sb("state", [HEADS, CHUNKS, 2])
        carries, carry_p = sb("carries", [HEADS, CHUNKS, 2]), sb("carry_p", [P, 2])
        ps_t = [ctx.enter_context(nc.psum_tensor(f"ps_weight_t{h}", [P, 512], F32)) for h in range(2)]
        keys_in, scores_in = sem("keys_in"), sem("scores_in")
        link_s, ends_set, ends_out, pieces_in = sem("softmax_link"), sem("ends_set"), sem("ends_out"), sem("pieces_in")
        carries_set, carries_out, carry_in = sem("carries_set"), sem("carries_out"), sem("carry_in")
        shifted, exped = sem("shifted"), sem("exped")
        turned, kept = [sem(f"weights_turned{h}") for h in range(2)], [sem(f"weights_kept{h}") for h in range(2)]
        block = ctx.enter_context(nc.Block())

        @block.sync
        def _(sp):
            sp.dma_start(alpha[:, :], scores.rearrange("h (c x) -> (h c) x", c=CHUNKS)).then_inc(scores_in, 16)
            for h in range(HEADS):
                rows = slice(h * CHUNKS, (h + 1) * CHUNKS)
                sp.dma_start(keys[rows, 1:PIECE + 1], merged[1:1 + EP, :].rearrange("(c x) o -> c (x o)", c=CHUNKS)).then_inc(keys_in, 16)
                sp.dma_start(keys[rows, 0:1], merged[0:EP, :].rearrange("(c x) o -> c (x o)", c=CHUNKS)[:, 0:1], allow_slow_non_contiguous=True).then_inc(keys_in, 16)
                sp.dma_start(keys[rows, PIECE + 1:PIECE + 2],
                             merged[2:2 + EP, :].rearrange("(c x) o -> c (x o)", c=CHUNKS)[:, PIECE - 1:PIECE], allow_slow_non_contiguous=True).then_inc(keys_in, 16)
            sp.wait_ge(ends_set, 1)
            sp.dma_start(carry[0:P, :], ends[:, :]).then_inc(ends_out, 16)
            sp.wait_ge(ends_out, 16)
            sp.dma_start(pieces[:, :, :], carry[0:P, :].rearrange("(h c) k -> h c k", c=CHUNKS)).then_inc(pieces_in, 16)
            sp.wait_ge(carries_set, 1)
            sp.dma_start(carry[P:2 * P, 0:2].rearrange("(h c) k -> h c k", c=CHUNKS), carries[:, :, :]).then_inc(carries_out, 16)
            sp.wait_ge(carries_out, 16)
            sp.dma_start(carry_p[:, :], carry[P:2 * P, 0:2]).then_inc(carry_in, 16)

        @block.vector
        def _(dve):
            v = nc.vector
            link = linker(dve, link_s)
            dve.wait_ge(keys_in, 16 * 3 * HEADS)
            link(v.tensor_scalar(keys[:, :], keys[:, :], KEY.bit_length() - 1, None, ALU.logical_shift_right))
            link(v.tensor_tensor(reset[:, :], keys[:, 1:PIECE + 2], keys[:, 0:PIECE + 1], ALU.not_equal))
            link(v.tensor_scalar(reset[:, :], reset[:, :], -BIG, None, ALU.mult))
            dve.wait_ge(scores_in, 16)
            link(v.scalar_tensor_tensor(alpha[:, :], alpha[:, :], 0.2, alpha[:, :], ALU.mult, ALU.max))

            def scans(left, right):
                v.tensor_tensor_scan(from_left[:, :], reset[:, 0:PIECE], alpha[:, :], left, ALU.add, ALU.max)
                link(v.tensor_tensor_scan(from_right[:, ::-1], reset[:, 1:PIECE + 1][:, ::-1], alpha[:, ::-1], right, ALU.add, ALU.max))

            scans(-BIG, -BIG)
            v.tensor_copy(ends[:, 0:1], from_left[:, PIECE - 1:PIECE])
            v.tensor_copy(ends[:, 1:2], from_right[:, 0:1])
            v.tensor_reduce(ends[:, 2:3], reset[:, 0:PIECE], AX.X, ALU.min)
            v.tensor_reduce(ends[:, 3:4], reset[:, 1:PIECE + 1], AX.X, ALU.min).then_inc(ends_set, 1)
            dve.wait_ge(pieces_in, 16)
            v.tensor_tensor_scan(state[:, :, 0], pieces[:, :, 2], pieces[:, :, 0], -BIG, ALU.add, ALU.max)
            v.tensor_tensor_scan(state[:, ::-1, 1], pieces[:, ::-1, 3], pieces[:, ::-1, 1], -BIG, ALU.add, ALU.max)
            link(v.memset(carries[:, :, :], -BIG))
            v.tensor_copy(carries[:, 1:CHUNKS, 0], state[:, 0:CHUNKS - 1, 0])
            v.tensor_copy(carries[:, 0:CHUNKS - 1, 1], state[:, 1:CHUNKS, 1]).then_inc(carries_set, 1)
            dve.wait_ge(carry_in, 16)
            scans(carry_p[:, 0:1], carry_p[:, 1:2])
            link(v.tensor_tensor(from_left[:, :], from_left[:, :], from_right[:, :], ALU.max))
            v.tensor_tensor(alpha[:, :], alpha[:, :], from_left[:, :], ALU.subtract).then_inc(shifted, 1)

        @block.scalar
        def _(act):
            act.wait_ge(shifted, 1)
            nc.scalar.activation(alpha[:, :], alpha[:, :], ACT.Exp).then_inc(exped, 1)
            for i in range(PT):
                act.wait_ge(turned[i % 2], i // 2 + 1)
                nc.scalar.copy(weights[:, :, i, :], ps_t[i % 2][:, 0:P].rearrange("p (h c) -> p c h", h=HEADS)).then_inc(kept[i % 2], 1)

        @block.tensor
        def _(pe):
            pe.wait_ge(exped, 1)
            for i in range(PT):
                if i >= 2:
                    pe.wait_ge(kept[i % 2], i // 2)
                nc.tensor.transpose(ps_t[i % 2][:, 0:P], alpha[:, i * P:(i + 1) * P], const["ident"][:, :]).then_inc(turned[i % 2], 1)


def gather_messages(nc, const, edge, group_block, weights, tab_e, sums, denominators):
    row = const["row"]
    BUFS, TURN = 3, 6
    TURNS = GROUPS // TURN
    assert TURNS * TURN == GROUPS
    with ExitStack() as ctx:
        def sb(name, shape, dt=F32):
            return ctx.enter_context(nc.sbuf_tensor(name, shape, dt))

        def sem(name):
            return ctx.enter_context(nc.semaphore(name))

        index = [sb(f"index_e{i}", [P, BUFS, GROUP], I32) for i in range(TURN // BUFS)]
        rows = [sb(f"rows_e{q}", [P, GROUP, F]) for q in range(TURN)]
        messages = [sb(f"messages{h}", [P, GROUP, F]) for h in range(BUFS)]
        onehot = [sb(f"node_onehot{h}", [P, GROUP, L]) for h in range(BUFS)]
        ps_sum = [ctx.enter_context(nc.psum_tensor(f"ps_sum{h}", [L, F], F32)) for h in range(BUFS)]
        ps_den = [ctx.enter_context(nc.psum_tensor(f"ps_den{h}", [L, 512], F32)) for h in range(BUFS)]
        messages_set, summed, added = (sem(n) for n in ("messages_set", "e_summed", "e_added"))
        index_set = [sem(f"e_index_set{i}") for i in range(TURN // BUFS)]
        gathered = [sem(f"e_gathered{q}") for q in range(TURN)]
        link_s = sem("gather_link")
        tile_weights = weights.rearrange("p c i h -> p (c i) h")
        block = ctx.enter_context(nc.Block())

        @block.gpsimd
        def _(pool):
            def gather(n, q, turn):
                i, at = q // BUFS, q % BUFS
                if at == 0:
                    for before in range(q, q + BUFS):
                        at_least(pool, gathered[before], turn * (16 * GROUP))
                    pool.nop(nofuse=True)
                    nc.gpsimd.tensor_copy(index[i][:, :, :].rearrange("p g j -> p (g j)"), edge["dst"][:, DS(n * GROUP, BUFS * GROUP)]).then_inc(index_set[i], 1)
                    at_least(pool, index_set[i], turn + 1)
                at_least(pool, messages_set, n - TURN + 1)
                pool.nop(nofuse=True)
                for j in range(GROUP):
                    nc.gpsimd.indirect_dma_start(rows[q][:, j, :], None, tab_e,
                                                 bass.IndirectOffsetOnAxis(ap=index[i][:, at, j:j + 1], axis=0)).then_inc(gathered[q], 16)

            in_turns(nc.gpsimd, TURNS, ((0, gather),), TURN)

        @block.vector
        def _(dve):
            v = nc.vector
            link = linker(dve, link_s)
            v.memset(denominators[:, :, :], 0.0)
            link(v.memset(sums[:, :, :], 0.0))

            def weigh(n, q, turn):
                h = q % BUFS
                at_least(dve, summed, n - BUFS + 1)
                for j in range(GROUP):
                    v.tensor_scalar(onehot[h][:, j, :], row[:, 0:L], edge["local"][:, DS(n * GROUP + j, 1)], None, ALU.is_equal)
                at_least(dve, gathered[q], turn * (16 * GROUP) + 16 * GROUP)
                w = tile_weights[:, DS(n * GROUP, GROUP), :].rearrange("p j h -> p (j h)")
                v.tensor_tensor(messages[h][:, :, :].rearrange("p j (h d) -> p (j h) d", d=D),
                                rows[q][:, :, :].rearrange("p j (h d) -> p (j h) d", d=D),
                                w.unsqueeze(2).broadcast_to([P, GROUP * HEADS, D]), ALU.mult).then_inc(messages_set, 1)

            def add_up(n, q, turn):
                b = dve.value_load(group_block[0:1, DS(n, 1)], min_val=0, max_val=NB - 1)
                at_least(dve, summed, n + 1)
                at_least(dve, added, n)
                total = sums[:, DS(b, 1), :].rearrange("p o f -> p (o f)")
                v.tensor_tensor(total, ps_sum[q % BUFS][:, :], total, ALU.add)
                den = denominators[:, DS(b, 1), :].rearrange("p o h -> p (o h)")
                v.tensor_tensor(den, ps_den[q % BUFS][:, 0:HEADS], den, ALU.add).then_inc(added, 1)

            in_turns(v, TURNS, ((0, weigh), (2, add_up)), TURN)

        @block.tensor
        def _(pe):
            def add_edges(n, q, turn):
                h = q % BUFS
                at_least(pe, messages_set, n + 1)
                at_least(pe, added, n - BUFS + 1)
                for j in range(GROUP):
                    nc.tensor.matmul(ps_sum[h][:, :], onehot[h][:, j, :], messages[h][:, j, :], start=j == 0, stop=j == GROUP - 1)
                    ins = nc.tensor.matmul(ps_den[h][:, 0:HEADS], onehot[h][:, j, :],
                                           tile_weights[:, DS(n * GROUP + j, 1), :].rearrange("p o h -> p (o h)"),
                                           start=j == 0, stop=j == GROUP - 1)
                ins.then_inc(summed, 1)

            in_turns(nc.tensor, TURNS, ((0, add_edges),), TURN)


def route_and_share(nc, a, const, ffn, x_sb, sums, denominators, spare, raw_space, tokens, tab_x, lists):
    ident, tri, ones, row, eps = (const[k] for k in ("ident", "tri", "ones", "row", "eps"))
    IH = INNER // P
    COUPLES = EXPERTS // 2
    EARLY = COUPLES // 2
    PAIRS = NB // 2
    STAGED = 4
    MATRICES = 2 + 3 * EXPERTS

    def first(e):
        return e * 3 + 2

    with ExitStack() as ctx:
        def sb(name, shape, dt=F32):
            return ctx.enter_context(nc.sbuf_tensor(name, shape, dt))

        def ps(name, shape):
            return ctx.enter_context(nc.psum_tensor(name, shape, F32))

        def sem(name):
            return ctx.enter_context(nc.semaphore(name))

        raw = [raw_space[:, i * KF * INNER:(i + 1) * KF * INNER] for i in range(3)]
        gate_rows = sb("gate_rows", [EXPERTS, F])
        inverse = sb("inverse", [L, NB * HEADS])
        stats, moments = sb("stats2", [L, NB, 6]), sb("moments2", [L, NB, 2])
        deviation, rstd = sb("deviation2", [L, NB]), sb("rstd2", [L, NB])
        staged = [spare[0:L, h * F:(h + 1) * F] for h in range(2)] + [sb(f"xn2_tile{h}", [L, F])[:, :] for h in range(2, STAGED)]
        xn2_t = [spare[:, 2 * F + h * KF * L:2 * F + (h + 1) * KF * L].rearrange("p (k n) -> p k n", k=KF) for h in range(2)]
        shared_t = [sb(f"shared_t{h}", [P, IH, L]) for h in range(2)]
        logits = sb("logits", [L, NB, EXPERTS])
        best, chosen = sb("best_logit", [L, NB]), sb("chosen", [L, NB])
        is_best, candidate = sb("is_best", [L, NB, EXPERTS]), sb("candidate", [L, NB, EXPERTS])
        far = sb("far_iota", [L, EXPERTS])
        routed, running, ahead = sb("routed", [L, NB, EXPERTS]), sb("running", [L, NB, EXPERTS]), sb("ahead_tiles", [L, NB, EXPERTS])
        zeros = sb("zeros_nb", [L, NB])
        tiles_i, tiles_f = sb("tiles_i", [L, EXPERTS], I32), sb("tiles_f", [L, EXPERTS])
        tile_end, tile_start = sb("tile_end", [L, EXPERTS]), sb("tile_start", [L, EXPERTS])
        slot_f = sb("token_slot_f", [L, NB])
        tile_cmp, tile_sum = sb("tile_cmp", [1, TOKEN_TILES, EXPERTS]), sb("tile_sum", [1, TOKEN_TILES])
        tile_iota = sb("tile_iota", [1, TOKEN_TILES])
        fill = sb("token_fill", [P, TOKEN_TILES], I32)
        ids = sb("token_ids", [L, NB], I32)
        listed = sb("listed", [TOKEN_TILES, RECS, P], I32)
        listed_f = sb("listed_f", [TOKEN_TILES, P])
        ps_w = [ps(f"ps_weight{i}", [P, F]) for i in range(4)]
        ps_xt = [ps(f"ps_xt2{h}", [P, F]) for h in range(2)]
        ps_logit, ps_count = ps("ps_logit", [L, F]), ps("ps_count", [P, F])
        ps_hidden, ps_y = ps_w[0:2], ps_w[2:4]
        ps_slot, ps_total = ps_count[0:L, 0:NB * EXPERTS], ps_count[0:L, NB * EXPERTS:NB * EXPERTS + EXPERTS]
        ps_ids = ps_count[:, 256:256 + TOKEN_TILES]

        names = ("link sums_used var dev staged_set turned kept logits_done prefix_set counted slots_set "
                 "filled fill_out listed_in listed_set ids_turned iotas gate_in gate_turned gate_kept hidden_done shared_set y_done y_added").split()
        s = {n: sem(f"route_{n}") for n in names}
        loaded = [sem(f"weights_loaded{i}") for i in range(3)]
        weights_turned, weights_kept = sem("weights_turned"), sem("weights_kept")
        written = [sem(f"ids_written{j}") for j in range(RECS)]
        scattered = sem("ids_scattered")
        xn2_out = [sem(f"xn2_out{h}") for h in range(STAGED)]
        block = ctx.enter_context(nc.Block())

        @block.sync
        def _(sp):
            sp.dma_start(gate_rows[:, :], a["L0_ffn_gate_w"]).then_inc(s["gate_in"], 16)
            sp.dma_start(raw[0].rearrange("p (i f) -> p i f", f=F), a["L0_ffn_sw1"].rearrange("(i p) f -> p i f", p=P)).then_inc(loaded[0], 16)
            sp.dma_start(raw[2].rearrange("p (k i) -> p k i", k=KF), a["L0_ffn_sw2"].rearrange("(k p) i -> p k i", p=P)).then_inc(loaded[2], 16)

            def load(e, begins=False):
                for i, name in enumerate(("L0_ffn_w1", "L0_ffn_w3", "L0_ffn_w2")):
                    if begins:
                        if i != 1:
                            sp.wait_ge(weights_turned, 1 if i == 0 else 2)
                    else:
                        sp.wait_ge(weights_turned, e * 3 + i)
                    rows = raw[i].rearrange("p (k i) -> p k i", k=KF) if i == 2 else raw[i].rearrange("p (i f) -> p i f", f=F)
                    sp.dma_start(rows, a[name][DS(e, 1), :, :].rearrange("o (k p) f -> p (o k) f", p=P)).then_inc(loaded[i], 16)

            sp.wait_ge(s["filled"], 1)
            for one in lists:
                sp.dma_start(one.rearrange("(p c) o -> p (c o)", c=TOKEN_TILES), fill[:, :]).then_inc(s["fill_out"], 16)
            load(0, begins=True)
            with nc.sync.Fori(1, EXPERTS) as e:
                load(e)
            sp.wait_ge(scattered, 1)
            for j, one in enumerate(lists):
                sp.dma_start(listed[:, j, :], one.rearrange("(c p) o -> c (p o)", p=P)).then_inc(s["listed_in"], 16)

        @block.gpsimd
        def _(pool):
            nc.gpsimd.memset(fill[:, :], PAD_RECORD).then_inc(s["filled"], 1)
            nc.gpsimd.iota(ids[:, :], pattern=[[L, NB]], base=0, channel_multiplier=1)
            nc.gpsimd.iota(tile_iota[:, :], pattern=[[1, TOKEN_TILES]], base=0, channel_multiplier=0, allow_small_or_imprecise_dtypes=True).then_inc(s["iotas"], 1)
            pool.wait_ge(s["iotas"], 1)

            def store(n, q, turn):
                at_least(pool, s["staged_set"], n + 1)
                nc.gpsimd.dma_start(tab_x[DS(n * L, L), :], staged[q]).then_inc(xn2_out[q], 16)

            in_turns(nc.gpsimd, NB // STAGED, ((0, store),), STAGED)
            for q in range(STAGED):
                pool.wait_ge(xn2_out[q], 16 * (NB // STAGED))
            pool.wait_ge(s["fill_out"], 16 * RECS)
            pool.wait_ge(s["slots_set"], 1)
            for t in range(NB):
                j = t % RECS
                if t >= RECS:
                    pool.wait_ge(written[j], 16 * (t // RECS))
                nc.gpsimd.indirect_dma_start(lists[j], bass.IndirectOffsetOnAxis(ap=tokens["slot"][:, t:t + 1], axis=0),
                                             ids[:, t:t + 1], None).then_inc(written[j], 16)
            for j in range(RECS):
                pool.wait_ge(written[j], 16 * (NB // RECS))
            pool.sem_inc(scattered, 1)

        @block.vector
        def _(dve):
            v = nc.vector
            link = linker(dve, s["link"])
            den = denominators[:, :, :].rearrange("p b h -> p (b h)")
            link(v.tensor_scalar(inverse[:, :], den, 1e-16, None, ALU.add))
            link(v.reciprocal(inverse[:, :], inverse[:, :]))
            by_head = sums[:, :, :].rearrange("p b (h d) -> p (b h) d", d=D)
            link(v.tensor_tensor(by_head, by_head, inverse[:, :].unsqueeze(2).broadcast_to([L, NB * HEADS, D]), ALU.mult))
            link(v.tensor_tensor(x_sb[:, :, :], x_sb[:, :, :], sums[:, :, :], ALU.add))
            dve.sem_inc(s["sums_used"], 1)
            for t in range(NB):
                ins = v.bn_stats(stats[:, t, :], x_sb[:, t, :])
            link(ins)
            for t in range(NB):
                ins = v.bn_aggr(moments[:, t, :], stats[:, t, :])
            ins.then_inc(s["var"], 1)
            dve.wait_ge(s["dev"], 1)
            link(v.reciprocal(rstd[:, :], deviation[:, :]))

            def normalize(n, q):
                v.tensor_scalar(staged[q], x_sb[:, DS(n, 1), :].rearrange("p o f -> p (o f)"), moments[:, DS(n, 1), 0:1].rearrange("p a b -> p (a b)"),
                                rstd[:, DS(n, 1)], ALU.subtract, ALU.mult).then_inc(s["staged_set"], 1)

            def stage(n, q, turn):
                at_least(dve, s["turned"], n - STAGED + 1)
                at_least(dve, xn2_out[q], turn * 16)
                normalize(n, q)

            in_turns(v, NB // STAGED, ((0, stage),), STAGED)
            shape = [L, NB, EXPERTS]
            iota = row[0:L, 0:EXPERTS].unsqueeze(1).broadcast_to(shape)
            dve.wait_ge(s["logits_done"], NB)
            link(v.tensor_copy(logits[:, :, :].rearrange("p t e -> p (t e)"), ps_logit[:, 0:NB * EXPERTS]))
            link(v.tensor_reduce(best[:, :], logits[:, :, :], AX.X, ALU.max))
            link(v.tensor_tensor(is_best[:, :, :], logits[:, :, :], best[:, :].unsqueeze(2).broadcast_to(shape), ALU.is_equal))
            link(v.tensor_scalar(far[:, :], row[0:L, 0:EXPERTS], float(EXPERTS), None, ALU.add))
            link(v.tensor_scalar(is_best[:, :, :], is_best[:, :, :], -float(EXPERTS), None, ALU.mult))
            link(v.tensor_tensor(candidate[:, :, :], is_best[:, :, :], far[:, :].unsqueeze(1).broadcast_to(shape), ALU.add))
            link(v.tensor_reduce(chosen[:, :], candidate[:, :, :], AX.X, ALU.min))
            link(v.tensor_tensor(routed[:, :, :], iota, chosen[:, :].unsqueeze(2).broadcast_to(shape), ALU.is_equal))
            link(v.memset(zeros[:, :], 0.0))
            for e in range(EXPERTS):
                ins = v.tensor_tensor_scan(running[:, :, e], routed[:, :, e], zeros[:, :], 0.0, ALU.add, ALU.add)
            link(ins)
            v.tensor_tensor(ahead[:, :, :], running[:, :, :], routed[:, :, :], ALU.subtract).then_inc(s["prefix_set"], 1)
            dve.wait_ge(s["counted"], 1)
            link(v.tensor_scalar(tiles_i[:, :], ps_total, float(P - 1), None, ALU.add))
            link(v.tensor_scalar(tiles_i[:, :], tiles_i[:, :], P.bit_length() - 1, None, ALU.logical_shift_right))
            link(v.tensor_copy(tiles_f[:, :], tiles_i[:, :]))
            link(v.tensor_tensor_scan(tile_end[:, :], tiles_f[:, :], zeros[:, 0:EXPERTS], 0.0, ALU.add, ALU.add))
            link(v.tensor_tensor(tile_start[:, :], tile_end[:, :], tiles_f[:, :], ALU.subtract))
            dve.wait_ge(s["iotas"], 1)
            link(v.tensor_tensor(tile_cmp[:, :, :], tile_iota[:, :].unsqueeze(2).broadcast_to([1, TOKEN_TILES, EXPERTS]),
                                 tile_start[0:1, :].unsqueeze(1).broadcast_to([1, TOKEN_TILES, EXPERTS]), ALU.is_ge))
            link(v.tensor_reduce(tile_sum[:, :], tile_cmp[:, :, 1:EXPERTS], AX.X, ALU.add))
            v.tensor_copy(tokens["expert"][:, :], tile_sum[:, :])
            link(v.tensor_scalar(tile_start[:, :], tile_start[:, :], float(P), None, ALU.mult))
            link(v.tensor_tensor(candidate[:, :, :], ps_slot.rearrange("p (t e) -> p t e", e=EXPERTS),
                                 tile_start[:, :].unsqueeze(1).broadcast_to(shape), ALU.add))
            link(v.tensor_tensor(candidate[:, :, :], candidate[:, :, :], routed[:, :, :], ALU.mult))
            link(v.tensor_reduce(slot_f[:, :], candidate[:, :, :], AX.X, ALU.add))
            v.tensor_copy(tokens["slot"][:, :], slot_f[:, :]).then_inc(s["slots_set"], 1)

            def stage_again(n, q, turn):
                at_least(dve, s["turned"], n + (NB - 1))
                normalize(n, q)

            def add_shared(n, q, turn):
                at_least(dve, s["y_done"], n + 1)
                tile = x_sb[:, DS(n, 1), :].rearrange("p o f -> p (o f)")
                v.tensor_tensor(tile, ps_y[q][0:L, :], tile, ALU.add).then_inc(s["y_added"], 1)

            for q in range(STAGED):
                dve.wait_ge(xn2_out[q], 16 * (NB // STAGED))
            in_turns(v, PAIRS, ((0, stage_again), (2, add_shared)), 2)
            dve.wait_ge(s["listed_in"], 16 * RECS)
            link(v.tensor_tensor(listed_f[:, :], listed[:, 0, :], listed[:, 1, :], ALU.min))
            for j in range(2, RECS):
                link(v.tensor_tensor(listed_f[:, :], listed_f[:, :], listed[:, j, :], ALU.min))
            v.tensor_scalar(listed_f[:, :], listed_f[:, :], float(N - 1), None, ALU.min).then_inc(s["listed_set"], 1)
            dve.wait_ge(s["ids_turned"], 1)
            v.tensor_copy(tokens["id"][:, :], ps_ids)

        @block.tensor
        def _(pe):
            t_ = nc.tensor

            def turn_matrix(m, i, pair, loads):
                pe.wait_ge(loaded[i], loads * 16)
                at_least(pe, weights_kept, m - 1)
                for half in range(IH):
                    for k in range(KF):
                        at = k * INNER + half * P if i == 2 else half * F + k * P
                        ins = t_.transpose(ps_w[2 * pair + half][:, k * P:(k + 1) * P], raw[i][:, at:at + P], ident[:, :])
                ins.then_inc(weights_turned, 1)

            def turn_couple(c):
                for n in range(2 * 3):
                    e, i = c * 2 + n // 3, n % 3
                    turn_matrix(first(e) + i, i, n % 2, e + (1 if i == 1 else 2))

            def turn_tile(n, q, done):
                at_least(pe, s["staged_set"], n + (done + 1))
                at_least(pe, s["kept"], n + (done - 1))
                for k in range(KF):
                    ins = t_.transpose(ps_xt[q % 2][:, k * L:(k + 1) * L], staged[q][:, k * P:(k + 1) * P], ident[0:L, 0:L])
                ins.then_inc(s["turned"], 1)

            def gate(n, q, turn):
                at_least(pe, s["kept"], n + 1)
                for k in range(KF):
                    ins = t_.matmul(ps_logit[:, DS(n * EXPERTS, EXPERTS)], xn2_t[q % 2][:, k, :], ffn["gate"][:, k, :], start=k == 0, stop=k == KF - 1)
                ins.then_inc(s["logits_done"], 1)

            pe.wait_ge(s["gate_in"], 16)
            for k in range(KF):
                ins = t_.transpose(ps_count[:, k * EXPERTS:(k + 1) * EXPERTS], gate_rows[:, k * P:(k + 1) * P], ident[0:EXPERTS, 0:EXPERTS])
            ins.then_inc(s["gate_turned"], 1)
            turn_matrix(0, 0, 0, 1)
            turn_matrix(1, 2, 1, 1)
            with t_.Fori(0, EARLY) as c:
                turn_couple(c)
            pe.wait_ge(s["gate_kept"], 1)
            def turn_first(n, q, turn):
                turn_tile(n, q, 0)

            in_turns(t_, NB // STAGED, ((0, turn_first), (1, gate)), STAGED)
            turn_couple(EARLY)
            pe.wait_ge(s["prefix_set"], 1)
            t_.matmul(ps_slot, tri[0:L, 0:L], routed[:, :, :].rearrange("p t e -> p (t e)"), start=True, stop=False)
            t_.matmul(ps_slot, ones[0:L, 0:L], ahead[:, :, :].rearrange("p t e -> p (t e)"), start=False, stop=True)
            t_.matmul(ps_total, ones[0:L, 0:L], running[:, NB - 1, :], start=True, stop=True).then_inc(s["counted"], 1)
            with t_.Fori(EARLY + 1, COUPLES) as c:
                turn_couple(c)
            pe.wait_ge(weights_kept, MATRICES)

            def turn_again(n, q, turn):
                turn_tile(n, q, NB)

            def hidden(n, q, turn):
                at_least(pe, s["kept"], n + (NB + 1))
                at_least(pe, s["shared_set"], n - 1)
                for c in range(IH):
                    for k in range(KF):
                        ins = t_.matmul(ps_hidden[q][:, c * L:(c + 1) * L], ffn["shared_up"][:, k, c * P:(c + 1) * P], xn2_t[q][:, k, :],
                                        start=k == 0, stop=k == KF - 1)
                ins.then_inc(s["hidden_done"], 1)

            def down(n, q, turn):
                at_least(pe, s["shared_set"], n + 1)
                at_least(pe, s["y_added"], n - 1)
                for c in range(IH):
                    ins = t_.matmul(ps_y[q][0:L, :], shared_t[q][:, c, :], ffn["shared_down"][:, c, :], start=c == 0, stop=c == IH - 1)
                ins.then_inc(s["y_done"], 1)

            in_turns(t_, PAIRS, ((1, hidden), (0, turn_again), (2, down)), 2)
            pe.wait_ge(s["listed_set"], 1)
            t_.transpose(ps_ids, listed_f[:, :], ident[0:TOKEN_TILES, 0:TOKEN_TILES]).then_inc(s["ids_turned"], 1)

        @block.scalar
        def _(act):
            sc = nc.scalar

            def keep_matrix(m, pair, places, halve=False):
                act.wait_ge(weights_turned, m + 1)
                for half, place in enumerate(places):
                    bank = ps_w[2 * pair + half][:, :]
                    bank = bank if len(place.shape) == 2 else bank.rearrange("p (k n) -> p k n", k=KF)
                    ins = sc.activation(place, bank, ACT.Copy, scale=0.5) if halve else sc.copy(place, bank)
                ins.then_inc(weights_kept, 1)

            def keep_couple(c):
                for n in range(2 * 3):
                    e, i = c * 2 + n // 3, n % 3
                    if i == 2:
                        keep_matrix(first(e) + i, n % 2, [ffn["down"][:, DS(e, 1), half, :].rearrange("p o f -> p (o f)") for half in range(IH)], True)
                    else:
                        at = [i * INNER + half * P for half in range(IH)]
                        keep_matrix(first(e) + i, n % 2, [ffn["up"][:, :, DS(e, 1), x:x + P].rearrange("p k o n -> p k (o n)") for x in at])

            act.wait_ge(s["gate_turned"], 1)
            sc.copy(ffn["gate"][:, :, :], ps_count[:, 0:KF * EXPERTS].rearrange("p (k e) -> p k e", k=KF)).then_inc(s["gate_kept"], 1)
            keep_matrix(0, 0, [ffn["shared_up"][:, :, half * P:(half + 1) * P] for half in range(IH)])
            keep_matrix(1, 1, [ffn["shared_down"][:, half, :] for half in range(IH)])
            act.wait_ge(s["sums_used"], 1)
            with sc.Fori(0, EARLY) as c:
                keep_couple(c)
            act.wait_ge(s["var"], 1)
            sc.activation(deviation[:, :], moments[:, :, 1], ACT.Sqrt, bias=eps[0:L, 0:1]).then_inc(s["dev"], 1)

            def keep_tile(n, q, turn):
                at_least(act, s["turned"], n + 1)
                at_least(act, s["logits_done"], n - 1)
                sc.copy(xn2_t[q % 2][:, :, :], ps_xt[q % 2][:, 0:KF * L].rearrange("p (k n) -> p k n", k=KF)).then_inc(s["kept"], 1)

            def keep_again(n, q, turn):
                at_least(act, s["turned"], n + (NB + 1))
                at_least(act, s["hidden_done"], n - 1)
                sc.copy(xn2_t[q][:, :, :], ps_xt[q][:, 0:KF * L].rearrange("p (k n) -> p k n", k=KF)).then_inc(s["kept"], 1)

            def gelu(n, q, turn):
                at_least(act, s["hidden_done"], n + 1)
                at_least(act, s["y_done"], n - 1)
                sc.activation(shared_t[q][:, :, :], ps_hidden[q][:, 0:IH * L].rearrange("p (c n) -> p c n", c=IH), ACT.Gelu).then_inc(s["shared_set"], 1)

            in_turns(sc, NB // STAGED, ((0, keep_tile),), STAGED)
            with sc.Fori(EARLY, COUPLES) as c:
                keep_couple(c)
            act.wait_ge(s["logits_done"], NB)
            in_turns(sc, PAIRS, ((1, gelu), (0, keep_again)), 2)


def run_experts(nc, const, ffn, tokens, tab_x, tab_y):
    ident = const["ident"]
    LAST = TOKEN_TILES - 1
    with ExitStack() as ctx:
        def sb(name, shape, dt=F32):
            return ctx.enter_context(nc.sbuf_tensor(name, shape, dt))

        def ps(name):
            return ctx.enter_context(nc.psum_tensor(name, [P, F], F32))

        def sem(name):
            return ctx.enter_context(nc.semaphore(name))

        index, rows = sb("token_index", [P, 1], I32), sb("token_rows", [P, F])
        x_t, hidden_t = sb("token_x_t", [P, KF, P]), sb("hidden_t", [P, INNER // P, P])
        gate, hidden, y = sb("swiglu_gate", [P, INNER]), sb("hidden", [P, INNER]), sb("token_y", [P, F])
        ps_t, ps_up, ps_h, ps_y = ps("ps_tx"), ps("ps_up"), ps("ps_hidden"), ps("ps_y")
        names = "index_set gathered turned kept up_done tanh_set gated hidden_set h_turned h_kept y_done y_kept y_free y_out".split()
        s = {n: sem(f"expert_{n}") for n in names}
        block = ctx.enter_context(nc.Block())

        @block.sync
        def _(sp):
            with nc.sync.Fori(0, TOKEN_TILES) as t:
                sp.wait_ge(s["y_kept"], t + 2)
                sp.dma_start(tab_y[DS(t * P, P), :], y[:, :]).then_inc(s["y_out"], 16)
                sp.wait_ge(s["y_out"], t * 16 + 16)
                sp.sem_inc(s["y_free"], 1)

        @block.gpsimd
        def _(pool):
            with nc.gpsimd.Fori(0, TOKEN_TILES) as t:
                pool.wait_ge(s["turned"], t + 1)
                pool.nop(nofuse=True)
                nc.gpsimd.tensor_copy(index[:, :], tokens["id"][:, DS(t, 1)]).then_inc(s["index_set"], 1)
                pool.wait_ge(s["index_set"], t + 1)
                pool.nop(nofuse=True)
                nc.gpsimd.indirect_dma_start(rows[:, :], None, tab_x, bass.IndirectOffsetOnAxis(ap=index[:, 0:1], axis=0)).then_inc(s["gathered"], 16)

        @block.vector
        def _(dve):
            v = nc.vector
            for n in ("turned", "h_turned", "hidden_set"):
                dve.sem_inc(s[n], 1)
            with v.Fori(0, TOKEN_TILES) as t:
                dve.wait_ge(s["tanh_set"], t + 1)
                v.scalar_tensor_tensor(gate[:, :], gate[:, :], 1.0, ps_up[:, 0:INNER], ALU.add, ALU.mult).then_inc(s["gated"], 1)
                dve.wait_ge(s["gated"], t + 1)
                dve.wait_ge(s["h_turned"], t + 1)
                v.tensor_tensor(hidden[:, :], ps_up[:, INNER:2 * INNER], gate[:, :], ALU.mult).then_inc(s["hidden_set"], 1)

        @block.tensor
        def _(pe):
            t_ = nc.tensor

            def expert(t):
                return pe.value_load(tokens["expert"][0:1, DS(t, 1)], min_val=0, max_val=EXPERTS - 1)

            def turn(t):
                pe.wait_ge(s["gathered"], t * 16 + 16)
                pe.wait_ge(s["kept"], t + 1)
                for k in range(KF):
                    ins = t_.transpose(ps_t[:, k * P:(k + 1) * P], rows[:, k * P:(k + 1) * P], ident[:, :])
                ins.then_inc(s["turned"], 1)

            def up(t):
                e = expert(t)
                pe.wait_ge(s["kept"], t + 2)
                pe.wait_ge(s["hidden_set"], t + 1)
                for k in range(KF):
                    ins = t_.matmul(ps_up[:, :], x_t[:, k, :], ffn["up"][:, k, DS(e, 1), :].rearrange("p o n -> p (o n)"), start=k == 0, stop=k == KF - 1)
                ins.then_inc(s["up_done"], 1)

            def turn_hidden(t):
                pe.wait_ge(s["hidden_set"], t + 2)
                pe.wait_ge(s["h_kept"], t + 1)
                for half in range(INNER // P):
                    ins = t_.transpose(ps_h[:, half * P:(half + 1) * P], hidden[:, half * P:(half + 1) * P], ident[:, :])
                ins.then_inc(s["h_turned"], 1)

            def down(t):
                e = expert(t)
                pe.wait_ge(s["h_kept"], t + 2)
                pe.wait_ge(s["y_kept"], t + 1)
                for half in range(INNER // P):
                    ins = t_.matmul(ps_y[:, :], hidden_t[:, half, :], ffn["down"][:, DS(e, 1), half, :].rearrange("p o f -> p (o f)"), start=half == 0, stop=half == INNER // P - 1)
                ins.then_inc(s["y_done"], 1)

            turn(0)
            up(0)
            turn(1)
            turn_hidden(0)
            with t_.Fori(1, LAST) as t:
                up(t)
                turn(t + 1)
                down(t - 1)
                turn_hidden(t)
            up(LAST)
            down(LAST - 1)
            turn_hidden(LAST)
            down(LAST)

        @block.scalar
        def _(act):
            sc = nc.scalar
            for n in ("kept", "h_kept", "y_kept", "y_free", "up_done", "y_done"):
                act.sem_inc(s[n], 1)

            def keep_x(t):
                act.wait_ge(s["turned"], t + 2)
                act.wait_ge(s["up_done"], t + 1)
                sc.copy(x_t[:, :, :].rearrange("p k n -> p (k n)"), ps_t[:, :]).then_inc(s["kept"], 1)

            def tanh(t):
                act.wait_ge(s["up_done"], t + 2)
                act.wait_ge(s["hidden_set"], t + 1)
                sc.activation(gate[:, :], ps_up[:, 0:INNER], ACT.Tanh, scale=0.5).then_inc(s["tanh_set"], 1)

            def keep_hidden(t):
                act.wait_ge(s["h_turned"], t + 2)
                act.wait_ge(s["y_done"], t + 1)
                sc.copy(hidden_t[:, :, :].rearrange("p k n -> p (k n)"), ps_h[:, 0:INNER]).then_inc(s["h_kept"], 1)

            def keep_y(t):
                act.wait_ge(s["y_done"], t + 2)
                act.wait_ge(s["y_free"], t + 1)
                sc.copy(y[:, :], ps_y[:, :]).then_inc(s["y_kept"], 1)

            keep_x(0)
            tanh(0)
            keep_x(1)
            keep_hidden(0)
            with sc.Fori(1, LAST) as t:
                tanh(t)
                keep_x(t + 1)
                keep_y(t - 1)
                keep_hidden(t)
            tanh(LAST)
            keep_y(LAST - 1)
            keep_hidden(LAST)
            keep_y(LAST)


def write_result(nc, tokens, x_sb, tab_y, out):
    BUFFERS = 4
    with ExitStack() as ctx:
        back = [ctx.enter_context(nc.sbuf_tensor(f"back{i}", [L, F], F32)) for i in range(BUFFERS)]
        gathered = [ctx.enter_context(nc.semaphore(f"y_gathered{i}")) for i in range(BUFFERS)]
        added, stored = ctx.enter_context(nc.semaphore("y_added")), ctx.enter_context(nc.semaphore("stored"))
        block = ctx.enter_context(nc.Block())

        @block.gpsimd
        def _(pool):
            for t in range(NB):
                if t >= BUFFERS:
                    pool.wait_ge(added, t - BUFFERS + 1)
                nc.gpsimd.indirect_dma_start(back[t % BUFFERS][:, :], None, tab_y,
                                             bass.IndirectOffsetOnAxis(ap=tokens["slot"][:, t:t + 1], axis=0)).then_inc(gathered[t % BUFFERS], 16)

        @block.vector
        def _(dve):
            for t in range(NB):
                dve.wait_ge(gathered[t % BUFFERS], 16 * (t // BUFFERS + 1))
                nc.vector.tensor_add(x_sb[:, t, :], x_sb[:, t, :], back[t % BUFFERS][:, :]).then_inc(added, 1)

        @block.sync
        def _(sp):
            PER = 4
            for t in range(0, NB, PER):
                sp.wait_ge(added, t + PER)
                sp.dma_start(out[t * L:(t + PER) * L, :].rearrange("(t p) f -> p t f", p=L), x_sb[:, t:t + PER, :]).then_inc(stored, 16)
            sp.wait_ge(stored, 16 * (NB // PER))

def program(nc, a, out):
    def dram(name, shape, dt=F32):
        return nc.dram_tensor(name, shape, dt, kind="Internal").ap()

    recs = [dram(f"records{j}", [REC_ROWS, 1], I32) for j in range(RECS)]
    merged = dram("sorted_records", [EP + 2, 1], I32)
    tab_v, tab_e = dram("target_rows", [N, EW]), dram("message_rows", [N, F])
    tab_parts = dram("source_parts", [N, PARTS * EW], BF16)
    tab_x, tab_y = dram("token_rows_in", [N, F]), dram("token_rows_out", [TOK_ROWS, F])
    token_lists = [dram(f"token_list{j}", [TOK_ROWS, 1], I32) for j in range(RECS)]
    scores, carry = dram("scores", [HEADS, EP]), dram("carry", [2 * P, 4])
    with ExitStack() as ctx:
        def sb(name, shape, dt=F32):
            return ctx.enter_context(nc.sbuf_tensor(name, shape, dt))

        def sem(name):
            return ctx.enter_context(nc.semaphore(name))

        const = make_constants(nc, sb)
        keep = {"key": sb("key", [L, ET], I32), "slot": sb("slot", [L, ET], I32), "group_block": sb("group_block", [1, GROUPS], I32),
                "scatter_slot": [sb(f"scatter_slot{h}", [L, STAGED_TILES], I32) for h in range(2)],
                "scatter_key": [sb(f"scatter_key{h}", [L, STAGED_TILES], I32) for h in range(2)]}
        written = [sem(f"records_written{j}") for j in range(RECS)]
        sort_edges(nc, a["src"], a["dst"], recs, written, const, keep)
        x_sb = sb("x_sb", [L, NB, F])
        project_and_mix(nc, a, const, keep, x_sb, recs, written, tab_v, tab_e, tab_parts)
        assert NB * PARTS * EW <= 2 * (NB * F + CHUNKS * PT * HEADS)
        edge_space, denominators = sb("edge_space", [P, NB * F + CHUNKS * PT * HEADS]), sb("denominators", [L, NB, HEADS])
        parts = edge_space[0:L, 0:NB * PARTS * EW // 2].bitcast(BF16).rearrange("p (b s c) -> p b s c", b=NB, s=PARTS)
        sums_space = edge_space[:, 0:NB * F]
        weights_space = edge_space[:, NB * F:NB * F + CHUNKS * PT * HEADS]
        weights = weights_space.rearrange("p (c i h) -> p c i h", c=CHUNKS, h=HEADS)
        sums = sums_space[0:L, :].rearrange("p (b f) -> p b f", b=NB)
        parts_in = sem("parts_in")
        edge_ctx = ExitStack()

        def sb_edge(name, shape, dt=F32):
            return edge_ctx.enter_context(nc.sbuf_tensor(name, shape, dt))

        edge = {"dst": sb_edge("edge_dst", [P, ST], I32), "src": sb_edge("edge_src", [P, ST], I32), "local": sb_edge("edge_local", [P, ST])}
        read_sorted_edges(nc, const, recs, merged, edge, tab_parts, parts, parts_in)
        score_edges(nc, a, const, edge, keep["group_block"], tab_v, parts, parts_in, scores)
        softmax_weights(nc, const, scores, merged, carry, weights, sums_space[:, 0:PIECE])
        gather_messages(nc, const, edge, keep["group_block"], weights, tab_e, sums, denominators)
        edge_ctx.close()
        ffn = {"up": sb("up_t", [P, KF, EXPERTS, 2 * INNER]), "down": sums_space[:, 0:EXPERTS * INNER // P * F].rearrange("p (e i f) -> p e i f", e=EXPERTS, f=F),
               "shared_up": sb("shared_up_t", [P, KF, INNER]), "shared_down": sb("shared_down_t", [P, INNER // P, F]),
               "gate": sb("gate_t", [P, KF, EXPERTS])}
        tokens = {"slot": sb("token_slot", [L, NB], I32), "expert": sb("token_expert", [1, TOKEN_TILES], I32), "id": sb("token_id", [P, TOKEN_TILES], I32)}
        route_and_share(nc, a, const, ffn, x_sb, sums, denominators, sums_space[:, EXPERTS * INNER // P * F:NB * F], weights_space, tokens, tab_x, token_lists)
        run_experts(nc, const, ffn, tokens, tab_x, tab_y)
        write_result(nc, tokens, x_sb, tab_y, out)

_INS = ['x', 'src', 'dst', 'L0_gnn_W_e', 'L0_gnn_W_r', 'L0_gnn_a', 'L0_mix_W_in', 'L0_mix_b_in', 'L0_mix_Wq',
        'L0_mix_Wk', 'L0_mix_Wv', 'L0_mix_W_out', 'L0_mix_b_out', 'L0_ffn_gate_w', 'L0_ffn_w1', 'L0_ffn_w2',
        'L0_ffn_w3', 'L0_ffn_sw1', 'L0_ffn_sw2']


def kernel(**inputs):
    import numpy as _np
    import concourse.bacc as _bacc
    from concourse import mybir as _mybir
    from concourse.bass_utils import run_bass_kernel_spmd as _run

    nc = _bacc.Bacc("TRN2", target_bir_lowering=False, num_devices=1)
    arrays, args = {}, {}
    for name in _INS:
        a = _np.ascontiguousarray(inputs[name])
        arrays[f"in_{name}_dram"] = a
        args[name] = nc.dram_tensor(f"in_{name}_dram", a.shape, _mybir.dt.from_np(a.dtype), kind="ExternalInput").ap()
    out = nc.dram_tensor("out_0_dram", (2500, 512), _mybir.dt.float32, kind="ExternalOutput").ap()
    program(nc, args, out)
    r = _run(nc, [arrays], core_ids=[0])
    return r.results[0]["out_0_dram"]
```
